# Optimizing a Trainium2 kernel written in Bass

```python
import numpy as np
import jax
import jax.numpy as jnp

def _softmax(x, axis=-1):
    return jax.nn.softmax(x, axis=axis)

def _gelu(x):
    return jax.nn.gelu(x, approximate=True)

def _silu(x):
    return jax.nn.silu(x)

def _sigmoid(x):
    return jax.nn.sigmoid(x)

def _layernorm(x, axis=-1, eps=1e-05):
    m = jnp.mean(x, axis=axis, keepdims=True)
    v = jnp.var(x, axis=axis, keepdims=True)
    return (x - m) / jnp.sqrt(v + eps)

def _scatter_add(tgt, idx, src, axis=0):
    return tgt.at[idx].add(src)

def _segment_sum(src, seg, n):
    return jax.ops.segment_sum(src, seg, n)
kernel_name = 'mk_seq_postln_d2_jaxref_r4_7f6b8a'

def setup_inputs(seed: int=0):
    np.random.seed(seed)
    _w = jnp.asarray

    def _L0_attn_setup():
        import jax, jax.numpy as jnp
        import numpy as np
        EMBED_DIM = 512
        NUM_HEADS = 16
        HEAD_DIM = EMBED_DIM // NUM_HEADS // 2
        DEPTH = 12
        LAMBDA_INIT = 0.8 - 0.6 * np.exp(-0.3 * DEPTH)
        EPS = 1e-05

        def _attn(q, k, v):
            scale = HEAD_DIM ** (-0.5)
            scores = jnp.einsum('bthd,bshd->bhts', q, k) * scale
            probs = jax.nn.softmax(scores, axis=-1)
            return jnp.einsum('bhts,bshe->bthe', probs, v)
        key = jax.random.key(seed)
        ks = jax.random.split(key, 9)
        B, T = (1, 512)
        scale = 1.0 / np.sqrt(EMBED_DIM)
        return {'x': jax.random.normal(ks[0], (B, T, EMBED_DIM), jnp.float32), 'wq': jax.random.normal(ks[1], (EMBED_DIM, EMBED_DIM), jnp.float32) * scale, 'wk': jax.random.normal(ks[2], (EMBED_DIM, EMBED_DIM), jnp.float32) * scale, 'wv': jax.random.normal(ks[3], (EMBED_DIM, EMBED_DIM), jnp.float32) * scale, 'wo': jax.random.normal(ks[4], (EMBED_DIM, EMBED_DIM), jnp.float32) * scale, 'lambda_q1': jax.random.normal(ks[5], (HEAD_DIM,), jnp.float32) * 0.1, 'lambda_k1': jax.random.normal(ks[6], (HEAD_DIM,), jnp.float32) * 0.1, 'lambda_q2': jax.random.normal(ks[7], (HEAD_DIM,), jnp.float32) * 0.1, 'lambda_k2': jax.random.normal(ks[8], (HEAD_DIM,), jnp.float32) * 0.1, 'subln_w': jnp.ones((2 * HEAD_DIM,), jnp.float32)}
    _L0_attn_in = _L0_attn_setup()

    def _L0_ffn_setup():
        import jax, jax.numpy as jnp
        import numpy as np
        ZERO_POINT = 128.0

        def _dequant(wq, scale):
            return (wq.astype(jnp.float32) - ZERO_POINT) * scale[:, None]
        key = jax.random.key(seed)
        ks = jax.random.split(key, 7)
        H, I = (512, 2048)
        B, S = (2, 512)
        hidden_state = jax.random.normal(ks[0], (B, S, H), dtype=jnp.float32)
        gate_w = jax.random.randint(ks[1], (I, H), 0, 64, dtype=jnp.int32)
        up_w = jax.random.randint(ks[2], (I, H), 0, 64, dtype=jnp.int32)
        down_w = jax.random.randint(ks[3], (H, I), 0, 64, dtype=jnp.int32)
        gate_scale = jax.random.uniform(ks[4], (I,), dtype=jnp.float32) * 0.02
        up_scale = jax.random.uniform(ks[5], (I,), dtype=jnp.float32) * 0.02
        down_scale = jax.random.uniform(ks[6], (H,), dtype=jnp.float32) * 0.02
        return {'hidden_state': hidden_state, 'gate_w': gate_w, 'gate_scale': gate_scale, 'up_w': up_w, 'up_scale': up_scale, 'down_w': down_w, 'down_scale': down_scale}
    _L0_ffn_in = _L0_ffn_setup()

    def _L1_attn_setup():
        import math
        import jax, jax.numpy as jnp
        import numpy as np
        EMBED = 512
        NUM_HEADS = 32
        NUM_KV_HEADS = 8
        DEPTH = 12
        H = NUM_HEADS // 2
        KVH = NUM_KV_HEADS // 2
        NREP = H // KVH
        HD = EMBED // NUM_HEADS
        LAMBDA_INIT = 0.8 - 0.6 * math.exp(-0.3 * DEPTH)
        EPS = 1e-05
        B, T = (2, 512)
        key = jax.random.key(seed)
        ks = jax.random.split(key, 10)
        s = 0.02
        return {'x': jax.random.normal(ks[0], (B, T, EMBED), dtype=jnp.float32), 'Wq': jax.random.normal(ks[1], (EMBED, EMBED), dtype=jnp.float32) * s, 'Wk': jax.random.normal(ks[2], (EMBED // NREP, EMBED), dtype=jnp.float32) * s, 'Wv': jax.random.normal(ks[3], (EMBED // NREP, EMBED), dtype=jnp.float32) * s, 'Wo': jax.random.normal(ks[4], (EMBED, EMBED), dtype=jnp.float32) * s, 'lambda_q1': jax.random.normal(ks[5], (HD,), dtype=jnp.float32) * 0.1, 'lambda_k1': jax.random.normal(ks[6], (HD,), dtype=jnp.float32) * 0.1, 'lambda_q2': jax.random.normal(ks[7], (HD,), dtype=jnp.float32) * 0.1, 'lambda_k2': jax.random.normal(ks[8], (HD,), dtype=jnp.float32) * 0.1, 'ln_w': jnp.ones((2 * HD,), dtype=jnp.float32)}
    _L1_attn_in = _L1_attn_setup()

    def _L1_ffn_setup():
        import jax, jax.numpy as jnp
        import numpy as np
        key = jax.random.key(seed)
        k1, k2, k3, k4 = jax.random.split(key, 4)
        B, S, D_IN, D_OUT = (4, 1024, 512, 512)
        x = jax.random.normal(k1, (B, S, D_IN), dtype=jnp.float32)
        weight = jax.random.normal(k2, (D_OUT, D_IN), dtype=jnp.float32) * 0.02
        scale_weight = jax.random.uniform(k3, (D_OUT,), dtype=jnp.float32, minval=0.5, maxval=1.5)
        bias = jax.random.normal(k4, (D_OUT,), dtype=jnp.float32) * 0.02
        return {'x': x, 'weight': weight, 'scale_weight': scale_weight, 'bias': bias}
    _L1_ffn_in = _L1_ffn_setup()
    _d = {'L0_attn_x': _L0_attn_in['x'], 'L0_attn_wq': _L0_attn_in['wq'], 'L0_attn_wk': _L0_attn_in['wk'], 'L0_attn_wv': _L0_attn_in['wv'], 'L0_attn_wo': _L0_attn_in['wo'], 'L0_attn_lambda_q1': _L0_attn_in['lambda_q1'], 'L0_attn_lambda_k1': _L0_attn_in['lambda_k1'], 'L0_attn_lambda_q2': _L0_attn_in['lambda_q2'], 'L0_attn_lambda_k2': _L0_attn_in['lambda_k2'], 'L0_attn_subln_w': _L0_attn_in['subln_w'], 'L0_ffn_gate_w': _L0_ffn_in['gate_w'], 'L0_ffn_gate_scale': _L0_ffn_in['gate_scale'], 'L0_ffn_up_w': _L0_ffn_in['up_w'], 'L0_ffn_up_scale': _L0_ffn_in['up_scale'], 'L0_ffn_down_w': _L0_ffn_in['down_w'], 'L0_ffn_down_scale': _L0_ffn_in['down_scale'], 'L1_attn_Wq': _L1_attn_in['Wq'], 'L1_attn_Wk': _L1_attn_in['Wk'], 'L1_attn_Wv': _L1_attn_in['Wv'], 'L1_attn_Wo': _L1_attn_in['Wo'], 'L1_attn_lambda_q1': _L1_attn_in['lambda_q1'], 'L1_attn_lambda_k1': _L1_attn_in['lambda_k1'], 'L1_attn_lambda_q2': _L1_attn_in['lambda_q2'], 'L1_attn_lambda_k2': _L1_attn_in['lambda_k2'], 'L1_attn_ln_w': _L1_attn_in['ln_w'], 'L1_ffn_weight': _L1_ffn_in['weight'], 'L1_ffn_scale_weight': _L1_ffn_in['scale_weight'], 'L1_ffn_bias': _L1_ffn_in['bias']}
    _x0 = _d['L0_attn_x']
    _d['L0_attn_x'] = jax.random.normal(jax.random.fold_in(jax.random.key(seed), 1), (2, 1024, 512), dtype=_x0.dtype)
    del _x0
    return _d

def reference(L0_attn_x, L0_attn_wq, L0_attn_wk, L0_attn_wv, L0_attn_wo, L0_attn_lambda_q1, L0_attn_lambda_k1, L0_attn_lambda_q2, L0_attn_lambda_k2, L0_attn_subln_w, L0_ffn_gate_w, L0_ffn_gate_scale, L0_ffn_up_w, L0_ffn_up_scale, L0_ffn_down_w, L0_ffn_down_scale, L1_attn_Wq, L1_attn_Wk, L1_attn_Wv, L1_attn_Wo, L1_attn_lambda_q1, L1_attn_lambda_k1, L1_attn_lambda_q2, L1_attn_lambda_k2, L1_attn_ln_w, L1_ffn_weight, L1_ffn_scale_weight, L1_ffn_bias):

    def _L0_attn_ref(x, wq, wk, wv, wo, lambda_q1, lambda_k1, lambda_q2, lambda_k2, subln_w):
        import jax, jax.numpy as jnp
        import numpy as np
        EMBED_DIM = 512
        NUM_HEADS = 16
        HEAD_DIM = EMBED_DIM // NUM_HEADS // 2
        DEPTH = 12
        LAMBDA_INIT = 0.8 - 0.6 * np.exp(-0.3 * DEPTH)
        EPS = 1e-05

        def _attn(q, k, v):
            scale = HEAD_DIM ** (-0.5)
            scores = jnp.einsum('bthd,bshd->bhts', q, k) * scale
            probs = jax.nn.softmax(scores, axis=-1)
            return jnp.einsum('bhts,bshe->bthe', probs, v)
        b, t, _ = x.shape
        q = (x @ wq.T).reshape(b, t, NUM_HEADS, 2, HEAD_DIM)
        k = (x @ wk.T).reshape(b, t, NUM_HEADS, 2, HEAD_DIM)
        v = (x @ wv.T).reshape(b, t, NUM_HEADS, 2 * HEAD_DIM)
        q1, q2 = (q[:, :, :, 0], q[:, :, :, 1])
        k1, k2 = (k[:, :, :, 0], k[:, :, :, 1])
        attn1 = _attn(q1, k1, v)
        attn2 = _attn(q2, k2, v)
        lam1 = jnp.exp(jnp.sum(lambda_q1 * lambda_k1))
        lam2 = jnp.exp(jnp.sum(lambda_q2 * lambda_k2))
        lambda_full = lam1 - lam2 + LAMBDA_INIT
        attn = attn1 - lambda_full * attn2
        rms = jax.lax.rsqrt(jnp.mean(attn * attn, axis=-1, keepdims=True) + EPS)
        attn = attn * rms * subln_w
        attn = attn * (1.0 - LAMBDA_INIT)
        attn = attn.reshape(b, t, NUM_HEADS * 2 * HEAD_DIM)
        return attn @ wo.T

    def _L0_ffn_ref(hidden_state, gate_w, gate_scale, up_w, up_scale, down_w, down_scale):
        import jax, jax.numpy as jnp
        import numpy as np
        ZERO_POINT = 128.0

        def _dequant(wq, scale):
            return (wq.astype(jnp.float32) - ZERO_POINT) * scale[:, None]
        Wg = _dequant(gate_w, gate_scale)
        Wu = _dequant(up_w, up_scale)
        Wd = _dequant(down_w, down_scale)
        g = jnp.einsum('bsh,ih->bsi', hidden_state, Wg)
        u = jnp.einsum('bsh,ih->bsi', hidden_state, Wu)
        h = jax.nn.silu(g) * u
        return jnp.einsum('bsi,hi->bsh', h, Wd)

    def _L1_attn_ref(x, Wq, Wk, Wv, Wo, lambda_q1, lambda_k1, lambda_q2, lambda_k2, ln_w):
        import math
        import jax, jax.numpy as jnp
        import numpy as np
        EMBED = 512
        NUM_HEADS = 32
        NUM_KV_HEADS = 8
        DEPTH = 12
        H = NUM_HEADS // 2
        KVH = NUM_KV_HEADS // 2
        NREP = H // KVH
        HD = EMBED // NUM_HEADS
        LAMBDA_INIT = 0.8 - 0.6 * math.exp(-0.3 * DEPTH)
        EPS = 1e-05
        B, T = (2, 512)
        bsz, tgt, _ = x.shape
        q = (x @ Wq.T).reshape(bsz, tgt, 2 * H, HD)
        k = (x @ Wk.T).reshape(bsz, tgt, 2 * KVH, HD)
        v = (x @ Wv.T).reshape(bsz, tgt, KVH, 2 * HD)
        k = jnp.repeat(k, NREP, axis=2)
        v = jnp.repeat(v, 2 * NREP, axis=2)
        q = q.transpose(0, 2, 1, 3)
        k = k.transpose(0, 2, 1, 3)
        v = v.transpose(0, 2, 1, 3)
        scale = HD ** (-0.5)
        scores = jnp.einsum('bhqd,bhkd->bhqk', q, k) * scale
        causal = jnp.tril(jnp.ones((tgt, tgt), dtype=bool))
        scores = jnp.where(causal, scores, jnp.finfo(scores.dtype).min)
        probs = jax.nn.softmax(scores, axis=-1)
        attn_out = jnp.einsum('bhqk,bhkd->bhqd', probs, v)
        attn1 = attn_out[:, 0::2]
        attn2 = attn_out[:, 1::2]
        lam1 = jnp.exp(jnp.sum(lambda_q1 * lambda_k1))
        lam2 = jnp.exp(jnp.sum(lambda_q2 * lambda_k2))
        lambda_full = lam1 - lam2 + LAMBDA_INIT
        attn = attn1 - lambda_full * attn2
        attn = attn * jax.lax.rsqrt(jnp.mean(attn * attn, axis=-1, keepdims=True) + EPS) * ln_w
        attn = attn * (1.0 - LAMBDA_INIT)
        attn = attn.transpose(0, 2, 1, 3).reshape(bsz, tgt, EMBED)
        return attn @ Wo.T

    def _L1_ffn_ref(x, weight, scale_weight, bias):
        import jax, jax.numpy as jnp
        import numpy as np
        w = weight * scale_weight[:, None]
        out = jnp.einsum('bsi,oi->bso', x, w) + bias
        return out
    x = L0_attn_x
    x = _layernorm(x + _L0_attn_ref(x, L0_attn_wq, L0_attn_wk, L0_attn_wv, L0_attn_wo, L0_attn_lambda_q1, L0_attn_lambda_k1, L0_attn_lambda_q2, L0_attn_lambda_k2, L0_attn_subln_w), axis=-1)
    x = _layernorm(x + _L0_ffn_ref(x, L0_ffn_gate_w, L0_ffn_gate_scale, L0_ffn_up_w, L0_ffn_up_scale, L0_ffn_down_w, L0_ffn_down_scale), axis=-1)
    x = _layernorm(x + _L1_attn_ref(x, L1_attn_Wq, L1_attn_Wk, L1_attn_Wv, L1_attn_Wo, L1_attn_lambda_q1, L1_attn_lambda_k1, L1_attn_lambda_q2, L1_attn_lambda_k2, L1_attn_ln_w), axis=-1)
    x = _layernorm(x + _L1_ffn_ref(x, L1_ffn_weight, L1_ffn_scale_weight, L1_ffn_bias), axis=-1)
    return x

_drawn_inputs = setup_inputs


def setup_inputs(seed=0):
    import zlib

    import numpy as np

    out = dict(_drawn_inputs(seed))
    spreads = {'L0_attn_subln_w': (1.0, 0.2), 'L1_attn_ln_w': (1.0, 0.6)}
    factors = {'L0_attn_lambda_q1': 24.637,
     'L0_attn_lambda_q2': 8.0,
     'L0_attn_lambda_k2': 5.534,
     'L1_attn_lambda_q1': 8.0,
     'L1_attn_lambda_k1': 3.088,
     'L1_attn_lambda_q2': 200.0,
     'L1_attn_lambda_k2': 8.0,
     'L1_ffn_bias': 3.261}
    for name, (base, spread) in spreads.items():
        noise = np.random.default_rng([zlib.crc32(name.encode()), seed]).standard_normal(out[name].shape)
        drawn = base * np.exp(spread * noise) if base else spread * noise
        out[name] = jnp.asarray(drawn.astype(out[name].dtype))
    for name, factor in factors.items():
        out[name] = (out[name] * factor).astype(out[name].dtype)
    return out
```

```python
import math
from contextlib import ExitStack

import concourse.bass as bass
from concourse import mybir

F32 = mybir.dt.float32
BF16 = mybir.dt.bfloat16
I32 = mybir.dt.int32
ALU = mybir.AluOpType
ACT = mybir.ActivationFunctionType
AX = mybir.AxisListType
ds = bass.ds

P = 128
B, T, D = 2, 1024, 512
TOK = B * T
KD = D // P
CH = 512
NCH = TOK // CH
NT = TOK // P
HD = 16
VD = 2 * HD
NH = D // VD
KV_HEADS = 4
PARTS = 3
FFN = 2048
FT = FFN // P
Q_PART = [0, 0, 0, 1, 1, 2]
K_PART = [0, 1, 2, 0, 1, 0]
SROWS = len(Q_PART) * HD
FROWS = SROWS + 2
KT = T // P
QC = T // CH
QPC = CH // P
HEADS = B * NH
FFN_W = 2 * KD * FFN + FT * D
FFN_SLICE = FFN_W // (HEADS // 2)
EPS = 1e-5
LAMBDA_INIT = 0.8 - 0.6 * math.exp(-0.3 * 12)
MASKED = -1e30
ZERO_POINT = 128.0
PRING = 4


class Layer:

    def __init__(self, name, k_dims, v_dims, causal):
        self.name, self.k_dims, self.v_dims, self.causal = name, k_dims, v_dims, causal
        self.k_subs = k_dims // HD // NH if k_dims == D else 1
        self.steps = [(qc, kt, max(0, kt - QPC * qc) * P if causal else 0)
                      for qc in range(QC) for kt in range(QPC * (qc + 1) if causal else KT)]
        self.units = []
        for sub in range(2):
            for qt in range(KT):
                keys = (qt + 1) * P if causal else T
                for kc in range(-(-keys // CH)):
                    self.units.append((sub, qt, kc, min(CH, keys - kc * CH)))
        assert len(self.steps) % PRING == 0 and len(self.units) % 2 == 0
        self.first_unit_step = 2
        self.units_at = {s: [] for s in range(len(self.steps))}
        for u in range(len(self.units)):
            self.units_at[self.first_unit_step + u // 3].append(u)
        self.last_unit_step = self.first_unit_step + (len(self.units) - 1) // 3
        self.qc_last = [max(s for s, x in enumerate(self.steps) if x[0] == qc) for qc in range(QC)]

    def v_column(self, n):
        return (n % NH) * VD if self.v_dims == D else ((n % NH) // (NH // KV_HEADS)) * VD

    def k_stack(self, n):
        return n if self.k_subs == 2 else n // 2


L0 = Layer("l0", D, D, False)
L1 = Layer("l1", D // 4, D // 4, True)


def qkv_phase(nc, L, xT_d, w_d, q_stack_d, k_stack_d, v_sb):
    names = ["wq", "wk", "wv"]
    widths = [D, L.k_dims, L.v_dims]
    q_tiles, k_tiles = D // P, L.k_dims // P
    MT = q_tiles + k_tiles
    with ExitStack() as ctx:
        sb = lambda n, s, d: ctx.enter_context(nc.sbuf_tensor(f"{L.name}_{n}", s, d))
        ps = lambda n, s, d: ctx.enter_context(nc.psum_tensor(f"{L.name}_{n}", s, d))
        sem = lambda n: ctx.enter_context(nc.semaphore(f"{L.name}_{n}"))
        w = [sb(f"{n}_sb", [P, KD, x], F32) for n, x in zip(names, widths)]
        xc = sb("xc", [P, 2, KD, CH], F32)
        part = [[sb(f"part{r}{i}", [P, CH], BF16) for i in range(PARTS)] for r in range(2)]
        rest = [sb(f"rest{r}", [P, CH], F32) for r in range(2)]
        p_qk = ps("p_qk", [P, 2, CH], F32)
        p_v = ps("p_v", [P, 2, CH], F32)
        w_in, x_in = sem("w_in"), [sem("x_in0"), sem("x_in1")]
        qk_done, v_done, v_kept = sem("qk_done"), sem("v_done"), sem("v_kept")
        part1, rest1, part2, part3 = sem("part1"), sem("rest1"), sem("part2"), sem("part3")
        stored = [sem("stored0"), sem("stored1")]
        block = ctx.enter_context(nc.Block())

        @block.sync
        def _(sp):
            with sp.Fori(0, NCH // 2, 1) as j:
                for par in range(2):
                    for m in range(MT):
                        r = (par * MT + m) % 2
                        is_q = m < q_tiles
                        dst = q_stack_d if is_q else k_stack_d
                        bat, tin = j, par * CH
                        sp.wait_ge(part3, (j * 2 + par) * MT + m + 1)
                        for g in range(len(Q_PART)):
                            i = (Q_PART if is_q else K_PART)[g]
                            subs = P // HD
                            mm = m if is_q else m - q_tiles
                            per_batch = (D if is_q else L.k_dims) // HD
                            out = dst[ds(bat * per_batch + mm * subs, subs), g * HD:(g + 1) * HD, tin:tin + CH]
                            sp.dma_start(out, part[r][i][:, :]).then_inc(stored[r], 16)
            for r in range(2):
                sp.wait_ge(stored[r], 16 * len(Q_PART) * NCH * MT // 2)

        @block.gpsimd
        def _(pool):
            for t, d in zip(w, w_d):
                pool.dma_start(t[:, :, :], d.rearrange("(k p) n -> p k n", p=P)).then_inc(w_in, 16)
            def load(c, par):
                pool.dma_start(xc[:, par, :, :], xT_d.rearrange("(k p) n -> p k n", p=P)[:, :, ds(c * CH, CH)]
                               ).then_inc(x_in[par], 16)

            for par in range(2):
                load(par, par)
            with pool.Fori(0, NCH // 2 - 1, 1) as j:
                for par in range(2):
                    pool.wait_ge(v_done, (2 * j + par + 1) * QPC)
                    load(2 * j + 2 + par, par)

        @block.tensor
        def _(pe):
            pe.wait_ge(w_in, 16 * len(w))
            with pe.Fori(0, NCH // 2, 1) as j:
                for par in range(2):
                    pe.wait_ge(x_in[par], 16 * j + 16)
                    for m in range(MT):
                        u = par * MT + m
                        pe.wait_ge(rest1, j * (2 * MT) + max(u - 1, 0))
                        wt, mm = (w[0], m) if m < q_tiles else (w[1], m - q_tiles)
                        for k in range(KD):
                            last = pe.matmul(p_qk[:, u % 2, :], wt[:, k, mm * P:(mm + 1) * P], xc[:, par, k, :],
                                             start=k == 0, stop=k == KD - 1)
                        last.then_inc(qk_done, 1)
                    for t in range(QPC):
                        u = par * QPC + t
                        pe.wait_ge(v_kept, j * (2 * QPC) + max(u - 1, 0))
                        for k in range(KD):
                            last = pe.matmul(p_v[:, u % 2, 0:L.v_dims], xc[:, par, k, t * P:(t + 1) * P],
                                             w[2][:, k, :], start=k == 0, stop=k == KD - 1)
                        last.then_inc(v_done, 1)

        @block.scalar
        def _(act):
            with act.Fori(0, NCH // 2, 1) as j:
                for u in range(2 * MT):
                    n = j * (2 * MT) + u
                    r = u % 2
                    act.wait_ge(qk_done, n + 1)
                    act.wait_ge(stored[r], 16 * len(Q_PART) * (j * MT + u // 2))
                    act.activation(part[r][0][:, :], p_qk[:, r, :], ACT.Copy).then_inc(part1, 1)
                    act.wait_ge(rest1, n + 1)
                    act.activation(part[r][1][:, :], rest[r][:, :], ACT.Copy).then_inc(part2, 1)
                    if u % MT == MT - 1:
                        for t in range(QPC):
                            k = (u // MT) * QPC + t
                            act.wait_ge(v_done, j * (2 * QPC) + k + 1)
                            act.activation(v_sb[:, ds((j * (2 * QPC) + k) * L.v_dims, L.v_dims)],
                                           p_v[:, k % 2, 0:L.v_dims], ACT.Copy).then_inc(v_kept, 1)

        @block.vector
        def _(dve):
            with dve.Fori(0, NCH // 2, 1) as j:
                for u in range(2 * MT):
                    n = j * (2 * MT) + u
                    r = u % 2
                    dve.wait_ge(part1, n + 1)
                    dve.wait_ge(part3, j * (2 * MT) + max(u - 1, 0))
                    dve.tensor_tensor(rest[r][:, :], p_qk[:, r, :], part[r][0][:, :], ALU.subtract).then_inc(rest1, 1)
                    dve.wait_ge(part2, n + 1)
                    dve.tensor_tensor(part[r][2][:, :], rest[r][:, :], part[r][1][:, :],
                                      ALU.subtract).then_inc(part3, 1)


def attention_phase(nc, L, q_stack_d, k_stack_d, v_sb, attn, neg_lambda, C, ffn_w=None, ffn_src=()):
    S, U = len(L.steps), len(L.units)
    KS = L.k_subs
    with ExitStack() as ctx:
        sb = lambda n, s, d: ctx.enter_context(nc.sbuf_tensor(f"{L.name}_{n}", s, d))
        ps = lambda n, s, d: ctx.enter_context(nc.psum_tensor(f"{L.name}_{n}", s, d))
        sem = lambda n: ctx.enter_context(nc.semaphore(f"{L.name}_{n}"))
        q = [sb(f"q{i}", [P, 2, T], BF16) for i in range(2)]
        k = [sb(f"k{i}", [P, KS, T], BF16) for i in range(2)]
        v = [sb(f"v{i}", [P, KT, VD], F32) for i in range(2)]
        prob = [sb(f"prob{i}", [P, 2, CH], F32) for i in range(PRING)]
        ones = sb("ones", [P, VD], F32)
        maxima = sb("maxima", [P, 2 * KT, 2], F32)
        shift = sb("shift", [P, 2 * KT], F32)
        shift_parts = sb("shift_parts", [P, 2, 2 * KT], BF16)
        shift_rows = sb("shift_rows", [4 * KT, P], BF16)
        sums = sb("sums", [P, CH], F32)
        recip = sb("recip", [P, QPC, 2], F32)
        half = sb("half", [P, 2, QPC, VD], F32)
        p_score = ps("p_score", [P, 2, 2, CH], F32)
        p_max = ps("p_max", [P, 2, CH], F32)
        p_out = ps("p_out", [P, CH], F32)
        p_turn = ps("p_turn", [P, QPC, P], F32)
        q_in = [sem("q_in0"), sem("q_in1")]
        shift_in = [sem("shift_in0"), sem("shift_in1")]
        ready = sem("ready")
        scored, exped, summed = sem("scored"), sem("exped"), sem("summed")
        max_scored, reduced = sem("max_scored"), sem("reduced")
        shift_a, shift_b, shift_c = sem("shift_a"), sem("shift_b"), sem("shift_c")
        shift_turned, shift_copied = sem("shift_turned"), sem("shift_copied")
        out_copied, out_turned, out_recip, out_scaled, out_kept = (
            sem("out_copied"), sem("out_turned"), sem("out_recip"), sem("out_scaled"), sem("out_kept"))
        v_in = sem("v_in")
        wt_in = sem("wt_in")
        block = ctx.enter_context(nc.Block())

        @block.sync
        def _(sp):
            def load(n, par, first=False):
                if not first:
                    sp.wait_ge(scored, (n - 1) * S)
                sp.dma_start(q[par][0:SROWS, :, :],
                             q_stack_d[ds(2 * n, 2)].rearrange("s r t -> r s t")).then_inc(q_in[par], 16)
                sp.dma_start(k[par][0:SROWS, :, :],
                             k_stack_d[ds(L.k_stack(n) * KS, KS)].rearrange("s r t -> r s t")
                             ).then_inc(q_in[par], 16)

            def shift_row(n, par):
                sp.wait_ge(shift_copied, n + 1)
                for i in range(2):
                    sp.dma_start(q[par][SROWS + i:SROWS + i + 1, :, :],
                                 shift_rows[2 * KT * i:2 * KT * (i + 1), :]).then_inc(shift_in[par], 16)

            load(0, 0, first=True)
            shift_row(0, 0)
            load(1, 1, first=True)
            shift_row(1, 1)
            with sp.Fori(0, HEADS // 2 - 1, 1) as j:
                for par in range(2):
                    load(2 * j + 2 + par, par)
                    shift_row(2 * j + 2 + par, par)
            for par in range(2):
                sp.wait_ge(shift_in[par], 32 * HEADS // 2)

        @block.gpsimd
        def _(pool):
            def take_v(n, par):
                tiles = v_sb[:, 0:NT * L.v_dims].rearrange("p (t c) -> p t c", c=L.v_dims)
                pool.tensor_copy(v[par][:, :, :], tiles[:, ds((n // NH) * KT, KT), ds(L.v_column(n), VD)]
                                 ).then_inc(v_in, 1)

            if ffn_w is not None:
                for at, src in ffn_src:
                    pool.dma_start(ffn_w[:, at:at + src.shape[1] * src.shape[2]].bitcast(I32), src
                                   ).then_inc(wt_in, 16)
            for par in range(2):
                take_v(par, par)
            with pool.Fori(0, HEADS // 2 - 1, 1) as j:
                for par in range(2):
                    pool.wait_ge(summed, (2 * j + par + 1) * S)
                    take_v(2 * j + 2 + par, par)

        def sequence(n, has_next):
            for s in range(S):
                yield "score", s
                if s == 1:
                    yield "turn", QC - 1
                if s > 0:
                    yield "sum", s - 1
                for qc in range(QC - 1):
                    if s == L.qc_last[qc] + 3:
                        yield "turn", qc
                if has_next:
                    for u in L.units_at[s]:
                        yield "max", u
                    if s == L.last_unit_step + 1:
                        yield "turn_shift", 0
            yield "sum", S - 1

        @block.tensor
        def _(pe):
            def max_unit(n, par, u):
                sub, qt, kc, keys = L.units[u]
                if u == 0:
                    pe.wait_ge(q_in[par], 32 * (n // 2) + 32)
                if u < 2:
                    pe.wait_ge(shift_copied, n)
                pe.wait_ge(reduced, n * U + max(u - 1, 0))
                diagonal = L.causal and kc == qt // QPC
                last = pe.matmul(p_max[:, u % 2, 0:keys], q[par][0:SROWS, sub, qt * P:(qt + 1) * P],
                                 k[par][0:SROWS, sub * (KS - 1), kc * CH:kc * CH + keys], start=True, stop=not diagonal)
                if diagonal:
                    last = pe.matmul(p_max[:, u % 2, keys - P:keys], C.ident_b[:, :], C.mask_qk[:, :],
                                     start=False, stop=True)
                last.then_inc(max_scored, 1)

            def turn_shift(n):
                pe.wait_ge(shift_c, n + 1)
                pe.transpose(p_max[0:4 * KT, 0, 0:P // 2].bitcast(BF16), shift_parts[:, :, :].rearrange(
                    "p a b -> p (a b)"), C.ident_b[:, :]).then_inc(shift_turned, 1)

            def score(n, par, s):
                qc, kt, off = L.steps[s]
                if s == 0:
                    pe.wait_ge(shift_in[par], 32 * (n // 2) + 32)
                pe.wait_ge(exped, n * S + max(s - 1, 0))
                for sub in range(2):
                    diagonal = L.causal and kt >= QPC * qc
                    last = pe.matmul(p_score[:, s % 2, sub, off:CH], k[par][0:FROWS, sub * (KS - 1), kt * P:(kt + 1) * P],
                                     q[par][0:FROWS, sub, qc * CH + off:(qc + 1) * CH], start=True, stop=not diagonal)
                    if diagonal:
                        last = pe.matmul(p_score[:, s % 2, sub, off:off + P], C.ident_b[:, :], C.mask_kq[:, :],
                                         start=False, stop=True)
                last.then_inc(scored, 1)

            def sum_up(n, par, s):
                qc, kt, off = L.steps[s]
                if s == 0:
                    pe.wait_ge(v_in, n + 1)
                first, final = kt == 0, s == L.qc_last[qc]
                if first:
                    pe.wait_ge(out_copied, QC * n + qc)
                pe.wait_ge(exped, n * S + s + 1)
                for sub in range(2):
                    for i, lhs in enumerate((v[par][:, kt, :], ones[:, :])):
                        r0 = (2 * sub + i) * VD
                        last = pe.matmul(p_out[r0:r0 + VD, off:CH], lhs, prob[s % PRING][:, sub, off:CH],
                                         start=first, stop=final)
                last.then_inc(summed, 1)

            def turn(count):
                pe.wait_ge(out_copied, count)
                pe.wait_ge(out_kept, count)
                for i in range(QPC):
                    last = pe.transpose(p_turn[:, i, :], sums[:, i * P:(i + 1) * P], C.ident[:, :])
                last.then_inc(out_turned, 1)

            def head(n, par, has_next=True):
                for what, i in sequence(n, has_next):
                    if what == "score":
                        score(n, par, i)
                    elif what == "sum":
                        sum_up(n, par, i)
                    elif what == "turn":
                        turn(QC * n + (0 if i == QC - 1 else i + 1))
                    elif what == "max":
                        max_unit(n + 1, 1 - par, i)
                    else:
                        turn_shift(n + 1)

            pe.wait_ge(ready, 5)
            for u in range(U):
                max_unit(0, 0, u)
            turn_shift(0)
            with pe.Fori(0, HEADS // 2 - 1, 1) as j:
                for par in range(2):
                    head(2 * j + par, par)
            head(HEADS - 2, 0)
            head(HEADS - 1, 1, has_next=False)
            turn(QC * HEADS)

        @block.scalar
        def _(act):
            def copy_shift(n, sent=None):
                act.wait_ge(shift_turned, n + 1)
                if sent:
                    act.wait_ge(*sent)
                act.activation(shift_rows[:, :], p_max[0:4 * KT, 0, 0:P // 2].bitcast(BF16),
                               ACT.Copy).then_inc(shift_copied, 1)

            def copy_out(n, qc):
                act.wait_ge(summed, n * S + L.qc_last[qc] + 1)
                act.wait_ge(out_turned, QC * n + qc + 1)
                act.activation(sums[:, :], p_out[:, :], ACT.Copy).then_inc(out_copied, 1)

            def head(n, par, has_next=True):
                for what, i in sequence(n, has_next):
                    if what == "score":
                        qc, kt, off = L.steps[i]
                        act.wait_ge(scored, n * S + i + 1)
                        act.wait_ge(summed, n * S + max(i - PRING + 1, 0))
                        act.activation(prob[i % PRING][:, :, off:CH], p_score[:, i % 2, :, off:CH], ACT.Exp,
                                       scale=HD ** -0.5).then_inc(exped, 1)
                    elif what == "sum" and i in L.qc_last:
                        copy_out(n, L.qc_last.index(i))
                    elif what == "turn_shift":
                        copy_shift(n + 1, (shift_in[par], 32 * (n // 2) + 32))

            def convert(i):
                if ffn_w is not None:
                    at = ds(i * FFN_SLICE, FFN_SLICE)
                    act.activation(ffn_w[:, at], ffn_w[:, at].bitcast(I32), ACT.Copy, bias=-ZERO_POINT)

            copy_shift(0)
            if ffn_w is not None:
                act.wait_ge(wt_in, 16 * len(ffn_src))
            convert(0)
            with act.Fori(0, HEADS // 2 - 1, 1) as j:
                for par in range(2):
                    head(2 * j + par, par)
                convert(j + 1)
            head(HEADS - 2, 0)
            head(HEADS - 1, 1, has_next=False)

        @block.vector
        def _(dve):
            def reduce(n, u):
                sub, qt, kc, keys = L.units[u]
                dve.wait_ge(max_scored, n * U + u + 1)
                if u == 0:
                    dve.wait_ge(shift_a, n)
                dve.tensor_reduce(maxima[:, sub * KT + qt, kc:kc + 1], p_max[:, u % 2, 0:keys], AX.X, ALU.max,
                                  negate=True).then_inc(reduced, 1)

            def make_shift(n):
                dve.wait_ge(reduced, (n + 1) * U)
                dve.tensor_reduce(shift[:, :], maxima[:, :, :], AX.X, ALU.min).then_inc(shift_a, 1)
                dve.wait_ge(shift_a, n + 1)
                dve.wait_ge(shift_turned, n)
                dve.tensor_copy(shift_parts[:, 0, :], shift[:, :]).then_inc(shift_b, 1)
                dve.wait_ge(shift_b, n + 1)
                dve.tensor_tensor(shift_parts[:, 1, :], shift[:, :], shift_parts[:, 0, :],
                                  ALU.subtract).then_inc(shift_c, 1)

            def keep(count, n, qc):
                dve.wait_ge(out_turned, count + 1)
                cols = p_turn[:, :, :].rearrange("p b (s w) -> p b s w", s=2)
                dve.wait_ge(out_kept, count)
                dve.reciprocal(recip[:, :, :], cols[:, :, :, VD]).then_inc(out_recip, 1)
                dve.wait_ge(out_recip, count + 1)
                for sub in range(2):
                    dve.tensor_tensor(half[:, sub, :, :], cols[:, :, sub, 0:VD],
                                      recip[:, :, sub:sub + 1].to_broadcast([P, QPC, VD]),
                                      ALU.mult).then_inc(out_scaled, 1)
                dve.wait_ge(out_scaled, 2 * count + 2)
                tiles = attn[:, :].rearrange("p (t c) -> p t c", c=D)
                to = tiles[:, ds((n // NH) * KT + qc * QPC, QPC), ds((n % NH) * VD, VD)]
                dve.scalar_tensor_tensor(
                    out=to, in0=half[:, 1, :, :], scalar=neg_lambda, in1=half[:, 0, :, :],
                    op0=ALU.mult, op1=ALU.add).then_inc(out_kept, 1)

            def head(n, par, has_next=True):
                for what, i in sequence(n, has_next):
                    if what == "max":
                        reduce(n + 1, i)
                        if i == U - 1:
                            make_shift(n + 1)
                    elif what == "turn" and i == QC - 1:
                        keep(QC * n, (n + (HEADS - 1)) % HEADS, i)
                    elif what == "turn":
                        keep(QC * n + i + 1, n, i)

            dve.memset(ones[:, :], 1.0).then_inc(ready, 1)
            for i in range(2):
                dve.memset(k[i][SROWS:FROWS, :, :], 1.0).then_inc(ready, 1)
            dve.memset(sums[:, :], 1.0).then_inc(ready, 1)
            dve.memset(maxima[:, :, :], 3e38).then_inc(ready, 1)
            dve.wait_ge(ready, 5)
            for u in range(U):
                reduce(0, u)
            make_shift(0)
            with dve.Fori(0, HEADS // 2 - 1, 1) as j:
                for par in range(2):
                    head(2 * j + par, par)
            head(HEADS - 2, 0)
            head(HEADS - 1, 1, has_next=False)
            keep(QC * HEADS, HEADS - 1, QC - 1)


def mix_phase(nc, name, attn, wo_d, norm_w, x_d, x_out_d, xT_out_d, C):
    with ExitStack() as ctx:
        sb = lambda n, s, d: ctx.enter_context(nc.sbuf_tensor(f"{name}_{n}", s, d))
        ps = lambda n, s, d: ctx.enter_context(nc.psum_tensor(f"{name}_{n}", s, d))
        sem = lambda n: ctx.enter_context(nc.semaphore(f"{name}_{n}"))
        wo = sb("wo", [P, KD, D], F32)
        wo_in, wo_ready = sem("wo_in"), sem("wo_ready")
        square = sb("square", [P, D], F32)
        mean_sq = sb("mean_sq", [P, NH], F32)
        rms = sb("rms", [P, NH], F32)
        inv_rms = sb("inv_rms", [P, NH], F32)
        normed = [sb(f"normed{i}", [P, D], F32) for i in range(2)]
        normed_T = [sb(f"normed_T{i}", [P, KD, P], F32) for i in range(2)]
        x = [sb(f"x{i}", [P, D], F32) for i in range(2)]
        res = sb("res", [P, D], F32)
        stats = sb("stats", [P, 6], F32)
        mv = sb("mv", [P, 2], F32)
        idle = sb("idle", [P, 1], F32)
        std = sb("std", [P, 1], F32)
        rstd = sb("rstd", [P, 1], F32)
        y = [sb(f"y{i}", [P, D], F32) for i in range(2)]
        y_T = [sb(f"y_T{i}", [P, KD, P], F32) for i in range(2)]
        p_nT = ps("p_nT", [P, 2, KD, P], F32)
        p_o = ps("p_o", [P, 2, D], F32)
        p_yT = ps("p_yT", [P, 2, KD, P], F32)
        x_in = [sem("x_in0"), sem("x_in1")]
        squared, summed, rooted, inverted, scaled = (sem("squared"), sem("summed"), sem("rooted"), sem("inverted"),
                                                     sem("scaled"))
        turned, turned_kept, projected = sem("turned"), sem("turned_kept"), sem("projected")
        added, stat1, stat2, std_done, rstd_done, y_done = (sem("added"), sem("stat1"), sem("stat2"),
                                                            sem("std_done"), sem("rstd_done"), sem("y_done"))
        y_turned, y_kept = sem("y_turned"), sem("y_kept")
        out = [sem("out0"), sem("out1")]
        block = ctx.enter_context(nc.Block())
        def order(engine, first, second):
            first(0, 0)
            first(1, 1)
            second(0, 0)
            with engine.Fori(0, NT // 2 - 1, 1) as j:
                for par in range(2):
                    first(2 * j + 2 + par, par)
                    second(2 * j + 1 + par, 1 - par)
            second(NT - 1, 1)

        xT_v = xT_out_d.rearrange("(k p) n -> p k n", p=P)

        @block.sync
        def _(sp):
            def load(t, par):
                sp.wait_ge(added, at_least(t, -1))
                sp.dma_start(x[par][:, :], x_d[ds(t * P, P), :]).then_inc(x_in[par], 16)

            def store(t, par):
                sp.wait_ge(y_done, t + 1)
                sp.wait_ge(y_kept, t + 1)
                sp.dma_start(x_out_d[ds(t * P, P), :], y[par][:, :]).then_inc(out[par], 16)
                sp.dma_start(xT_v[:, :, ds(t * P, P)], y_T[par][:, :, :]).then_inc(out[par], 16)

            sp.dma_start(wo[:, :, :], wo_d.rearrange("(k p) n -> p k n", p=P)).then_inc(wo_in, 16)
            order(sp, load, store)
            for par in range(2):
                sp.wait_ge(out[par], 32 * NT // 2)

        @block.gpsimd
        def _(pool):
            pool.wait_ge(wo_in, 16)
            for k in range(KD):
                pool.tensor_scalar(wo[:, k, :], wo[:, k, :], norm_w, 1.0 - LAMBDA_INIT, ALU.mult,
                                   ALU.mult).then_inc(wo_ready, 1)

        @block.vector
        def _(dve):
            def first(t, par):
                a = attn[:, ds(t * D, D)]
                dve.wait_ge(summed, t)
                dve.tensor_tensor(square[:, :], a, a, ALU.mult).then_inc(squared, 1)
                dve.wait_ge(squared, t + 1)
                dve.wait_ge(rooted, t)
                dve.tensor_reduce(mean_sq[:, :], square[:, :].rearrange("p (h w) -> p h w", w=VD), AX.X,
                                  ALU.add).then_inc(summed, 1)
                dve.wait_ge(rooted, t + 1)
                dve.wait_ge(scaled, t)
                dve.reciprocal(inv_rms[:, :], rms[:, :]).then_inc(inverted, 1)
                dve.wait_ge(inverted, t + 1)
                dve.wait_ge(turned, at_least(t, -1))
                dve.tensor_tensor(normed[par][:, :].rearrange("p (h w) -> p h w", w=VD),
                                  a.rearrange("p (h w) -> p h w", w=VD),
                                  inv_rms[:, :].unsqueeze(2).to_broadcast([P, NH, VD]), ALU.mult).then_inc(scaled, 1)

            def second(t, par):
                dve.wait_ge(projected, t + 1)
                dve.wait_ge(x_in[par], 16 * (t // 2) + 16)
                dve.wait_ge(y_done, t)
                dve.tensor_tensor(res[:, :], p_o[:, par, :], x[par][:, :], ALU.add).then_inc(added, 1)
                dve.wait_ge(added, t + 1)
                dve.bn_stats(stats[:, :], res[:, :]).then_inc(stat1, 1)
                dve.wait_ge(stat1, t + 1)
                dve.memset(idle[:, :], 0.0)
                dve.bn_aggr(mv[:, :], stats[:, :]).then_inc(stat2, 1)
                dve.wait_ge(std_done, t + 1)
                dve.reciprocal(rstd[:, :], std[:, :]).then_inc(rstd_done, 1)
                dve.wait_ge(rstd_done, t + 1)
                dve.wait_ge(out[par], 32 * (t // 2))
                dve.wait_ge(y_turned, at_least(t, -1))
                dve.tensor_scalar(y[par][:, :], res[:, :], mv[:, 0:1], rstd[:, 0:1], ALU.subtract,
                                  ALU.mult).then_inc(y_done, 1)

            order(dve, first, second)

        @block.scalar
        def _(act):
            def first(t, par):
                act.wait_ge(summed, t + 1)
                act.wait_ge(inverted, t)
                act.activation(rms[:, :], mean_sq[:, :], ACT.Sqrt, bias=C.eps[:, 0:1], scale=1.0 / VD
                               ).then_inc(rooted, 1)
                act.wait_ge(turned, t + 1)
                act.wait_ge(projected, at_least(t, -1))
                act.activation(normed_T[par][:, :, :], p_nT[:, par, :, :], ACT.Copy).then_inc(turned_kept, 1)

            def second(t, par):
                act.wait_ge(stat2, t + 1)
                act.wait_ge(rstd_done, t)
                act.activation(std[:, :], mv[:, 1:2], ACT.Sqrt, bias=C.eps[:, 0:1]).then_inc(std_done, 1)
                act.wait_ge(y_turned, t + 1)
                act.wait_ge(out[par], 32 * (t // 2))
                act.activation(y_T[par][:, :, :], p_yT[:, par, :, :], ACT.Copy).then_inc(y_kept, 1)

            order(act, first, second)

        @block.tensor
        def _(pe):
            def first(t, par):
                pe.wait_ge(scaled, t + 1)
                pe.wait_ge(turned_kept, at_least(t, -1))
                for i in range(KD):
                    last = pe.transpose(p_nT[:, par, i, :], normed[par][:, i * P:(i + 1) * P], C.ident[:, :])
                last.then_inc(turned, 1)
                pe.wait_ge(turned_kept, t + 1)
                pe.wait_ge(added, at_least(t, -1))
                for i in range(KD):
                    last = pe.matmul(p_o[:, par, :], normed_T[par][:, i, :], wo[:, i, :], start=i == 0,
                                     stop=i == KD - 1)
                last.then_inc(projected, 1)

            def second(t, par):
                pe.wait_ge(y_done, t + 1)
                pe.wait_ge(y_kept, at_least(t, -1))
                for i in range(KD):
                    last = pe.transpose(p_yT[:, par, i, :], y[par][:, i * P:(i + 1) * P], C.ident[:, :])
                last.then_inc(y_turned, 1)

            pe.wait_ge(wo_ready, KD)
            order(pe, first, second)


def at_least(t, back):
    if isinstance(t, int):
        return max(t + back, 0)
    return t + back


def ffn_phase(nc, wg, wu, wd, h, g_scale, u_scale, d_scale_d, xT_d, x_d, x_out_d, xT_out_d, C):
    name = "ffn"
    with ExitStack() as ctx:
        sb = lambda n, s, d: ctx.enter_context(nc.sbuf_tensor(f"{name}_{n}", s, d))
        ps = lambda n, s, d: ctx.enter_context(nc.psum_tensor(f"{name}_{n}", s, d))
        sem = lambda n: ctx.enter_context(nc.semaphore(f"{name}_{n}"))
        xc = sb("xc", [P, KD, CH], F32)
        h = h.rearrange("p (i n) -> p i n", i=FT)
        d_scale = sb("d_scale", [P, D], F32)
        silu = [sb(f"silu{i}", [P, CH], F32) for i in range(2)]
        x = sb("x", [P, QPC, D], F32)
        down = sb("down", [P, D], F32)
        y = sb("y", [P, QPC, D], F32)
        y_T = sb("y_T", [P, KD, P], F32)
        stats = sb("stats", [P, QPC, 6], F32)
        mv = sb("mv", [P, QPC, 2], F32)
        idle = sb("idle", [P, 1], F32)
        std = sb("std", [P, QPC], F32)
        rstd = sb("rstd", [P, QPC], F32)
        p_g = ps("p_g", [P, 2, CH], F32)
        p_u = ps("p_u", [P, 2, CH], F32)
        p_d = ps("p_d", [P, 2, D], F32)
        p_yT = ps("p_yT", [P, 2, KD, P], F32)
        ready, scale_in = sem("ready"), sem("scale_in")
        xT_in, x_in = sem("xT_in"), sem("x_in")
        g_done, u_done, silu_done, h_done = sem("g_done"), sem("u_done"), sem("silu_done"), sem("h_done")
        d_done, d_scaled, added, stat1, stat2, std_done, rstd_done, y_done = (
            sem("d_done"), sem("d_scaled"), sem("added"), sem("stat1"), sem("stat2"), sem("std_done"),
            sem("rstd_done"), sem("y_done"))
        y_turned, y_kept, out, outT = sem("y_turned"), sem("y_kept"), sem("out"), sem("outT")
        block = ctx.enter_context(nc.Block())
        xT_v, xT_ov = (a.rearrange("(k p) n -> p k n", p=P) for a in (xT_d, xT_out_d))
        x_v, x_ov = (a.rearrange("(t p) n -> p t n", p=P) for a in (x_d, x_out_d))
        TURN_AT = 2

        @block.sync
        def _(sp):
            def store_T(c, base):
                for t in range(QPC):
                    sp.wait_ge(y_kept, base + t + 1)
                    sp.dma_start(xT_ov[:, :, ds(c * CH + t * P, P)], y_T[:, :, :]).then_inc(outT, 16)

            sp.dma_start(d_scale[:, :], d_scale_d.partition_broadcast(P)).then_inc(scale_in, 16)
            with sp.Fori(0, NCH, 1) as c:
                sp.wait_ge(u_done, c * FT)
                sp.dma_start(xc[:, :, :], xT_v[:, :, ds(c * CH, CH)]).then_inc(xT_in, 16)
                sp.wait_ge(added, c * QPC)
                sp.dma_start(x[:, :, :], x_v[:, ds(c * QPC, QPC), :]).then_inc(x_in, 16)
                store_T((c + (NCH - 1)) % NCH, c * QPC)
                sp.wait_ge(y_done, (c + 1) * QPC)
                sp.dma_start(x_ov[:, ds(c * QPC, QPC), :], y[:, :, :]).then_inc(out, 16)
            store_T(NCH - 1, NCH * QPC)
            sp.wait_ge(out, 16 * NCH)
            sp.wait_ge(outT, 16 * QPC * (NCH + 1))

        @block.gpsimd
        def _(pool):
            pool.memset(y[:, :, :], 0.0).then_inc(ready, 1)

        @block.tensor
        def _(pe):
            def turn(base):
                pe.wait_ge(y_done, base)
                for t in range(QPC):
                    pe.wait_ge(y_kept, base if t < 2 else base + t - 1)
                    for i in range(KD):
                        last = pe.transpose(p_yT[:, t % 2, i, :], y[:, t, i * P:(i + 1) * P], C.ident[:, :])
                    last.then_inc(y_turned, 1)

            pe.wait_ge(ready, 1)
            with pe.Fori(0, NCH, 1) as c:
                pe.wait_ge(xT_in, 16 * c + 16)
                for i in range(FT):
                    n = c * FT + i
                    pe.wait_ge(silu_done, c * FT + max(i - 1, 0))
                    for k in range(KD):
                        last = pe.matmul(p_g[:, i % 2, :], wg[:, k, i * P:(i + 1) * P], xc[:, k, :], start=k == 0,
                                         stop=k == KD - 1)
                    last.then_inc(g_done, 1)
                    pe.wait_ge(h_done, c * FT + max(i - 1, 0))
                    for k in range(KD):
                        last = pe.matmul(p_u[:, i % 2, :], wu[:, k, i * P:(i + 1) * P], xc[:, k, :], start=k == 0,
                                         stop=k == KD - 1)
                    last.then_inc(u_done, 1)
                    if i == TURN_AT:
                        turn(c * QPC)
                for t in range(QPC):
                    pe.wait_ge(d_scaled, c * QPC + max(t - 1, 0))
                    for i in range(FT):
                        if t == 0:
                            pe.wait_ge(h_done, c * FT + i + 1)
                        last = pe.matmul(p_d[:, t % 2, :], h[:, i, t * P:(t + 1) * P], wd[:, i, :], start=i == 0,
                                         stop=i == FT - 1)
                    last.then_inc(d_done, 1)
            turn(NCH * QPC)

        @block.scalar
        def _(act):
            def keep_turned(base):
                for t in range(QPC):
                    act.wait_ge(y_turned, base + t + 1)
                    act.wait_ge(outT, 16 * (base + t))
                    act.activation(y_T[:, :, :], p_yT[:, t % 2, :, :], ACT.Copy).then_inc(y_kept, 1)

            with act.Fori(0, NCH, 1) as c:
                for i in range(FT):
                    n = c * FT + i
                    act.wait_ge(g_done, n + 1)
                    act.wait_ge(h_done, c * FT + max(i - 1, 0))
                    act.activation(silu[i % 2][:, :], p_g[:, i % 2, :], ACT.Silu, scale=g_scale[:, i:i + 1]
                                   ).then_inc(silu_done, 1)
                    if i == TURN_AT:
                        keep_turned(c * QPC)
                act.wait_ge(stat2, (c + 1) * QPC)
                act.wait_ge(rstd_done, c)
                act.activation(std[:, :], mv[:, :, 1], ACT.Sqrt, bias=C.eps[:, 0:1]).then_inc(std_done, 1)
            keep_turned(NCH * QPC)

        @block.vector
        def _(dve):
            dve.wait_ge(scale_in, 16)
            with dve.Fori(0, NCH, 1) as c:
                for i in range(FT):
                    n = c * FT + i
                    dve.wait_ge(u_done, n + 1)
                    dve.wait_ge(silu_done, n + 1)
                    if i == 0:
                        dve.wait_ge(d_done, c * QPC)
                    dve.scalar_tensor_tensor(out=h[:, i, :], in0=p_u[:, i % 2, :], scalar=u_scale[:, i:i + 1],
                                             in1=silu[i % 2][:, :], op0=ALU.mult, op1=ALU.mult).then_inc(h_done, 1)
                dve.wait_ge(x_in, 16 * c + 16)
                for t in range(QPC):
                    n = c * QPC + t
                    dve.wait_ge(d_done, n + 1)
                    dve.wait_ge(added, n)
                    dve.tensor_tensor(down[:, :], p_d[:, t % 2, :], d_scale[:, :], ALU.mult).then_inc(d_scaled, 1)
                    dve.wait_ge(d_scaled, n + 1)
                    if t == 0:
                        dve.wait_ge(out, 16 * c)
                        dve.wait_ge(y_turned, c * QPC + QPC)
                    dve.tensor_tensor(y[:, t, :], down[:, :], x[:, t, :], ALU.add).then_inc(added, 1)
                    dve.wait_ge(added, n + 1)
                    dve.bn_stats(stats[:, t, :], y[:, t, :]).then_inc(stat1, 1)
                    if t == 0:
                        dve.wait_ge(std_done, c)
                    dve.wait_ge(stat1, n + 1)
                    dve.memset(idle[:, :], 0.0)
                    dve.bn_aggr(mv[:, t, :], stats[:, t, :]).then_inc(stat2, 1)
                dve.wait_ge(std_done, c + 1)
                dve.reciprocal(rstd[:, :], std[:, :]).then_inc(rstd_done, 1)
                dve.wait_ge(rstd_done, c + 1)
                for t in range(QPC):
                    dve.tensor_scalar(y[:, t, :], y[:, t, :], mv[:, t, 0:1], rstd[:, t:t + 1], ALU.subtract,
                                      ALU.mult).then_inc(y_done, 1)


def linear_phase(nc, w_d, scale_d, bias_d, xT_d, x_d, out_d, C):
    name = "lin"
    with ExitStack() as ctx:
        sb = lambda n, s, d: ctx.enter_context(nc.sbuf_tensor(f"{name}_{n}", s, d))
        ps = lambda n, s, d: ctx.enter_context(nc.psum_tensor(f"{name}_{n}", s, d))
        sem = lambda n: ctx.enter_context(nc.semaphore(f"{name}_{n}"))
        w = sb("w", [P, KD, D], F32)
        scale_b, bias_b = sb("scale", [P, D], F32), sb("bias", [P, D], F32)
        rows_in = sem("rows_in")
        xT = [sb(f"xT{i}", [P, KD, P], F32) for i in range(2)]
        x = [sb(f"x{i}", [P, D], F32) for i in range(2)]
        scaled = sb("scaled", [P, D], F32)
        biased = sb("biased", [P, D], F32)
        res = sb("res", [P, D], F32)
        y = [sb(f"y{i}", [P, D], F32) for i in range(2)]
        stats = sb("stats", [P, 6], F32)
        mv = sb("mv", [P, 2], F32)
        idle = sb("idle", [P, 1], F32)
        std = sb("std", [P, 1], F32)
        rstd = sb("rstd", [P, 1], F32)
        p_o = ps("p_o", [P, 2, D], F32)
        w_in, x_in = sem("w_in"), [sem("x_in0"), sem("x_in1")]
        o_done, o_scaled, o_biased, added, stat1, stat2, std_done, rstd_done, y_done = (
            sem("o_done"), sem("o_scaled"), sem("o_biased"), sem("added"), sem("stat1"), sem("stat2"),
            sem("std_done"), sem("rstd_done"), sem("y_done"))
        out = [sem("out0"), sem("out1")]
        block = ctx.enter_context(nc.Block())
        xT_v = xT_d.rearrange("(k p) n -> p k n", p=P)

        @block.gpsimd
        def _(pool):
            pool.dma_start(w[:, :, :], w_d.rearrange("(k p) n -> p k n", p=P)).then_inc(w_in, 16)
            with pool.Fori(0, NT // 2, 1) as j:
                for par in range(2):
                    t = 2 * j + par
                    pool.wait_ge(y_done, t)
                    pool.wait_ge(y_done, t + 1)
                    pool.dma_start(out_d[ds(t * P, P), :], y[par][:, :]).then_inc(out[par], 16)
            for par in range(2):
                pool.wait_ge(out[par], 16 * NT // 2)

        @block.sync
        def _(sp):
            sp.dma_start(scale_b[:, :], scale_d.partition_broadcast(P)).then_inc(rows_in, 16)
            sp.dma_start(bias_b[:, :], bias_d.partition_broadcast(P)).then_inc(rows_in, 16)
            with sp.Fori(0, NT // 2, 1) as j:
                for par in range(2):
                    t = 2 * j + par
                    sp.wait_ge(added, 2 * j)
                    sp.dma_start(xT[par][:, :, :], xT_v[:, :, ds(t * P, P)]).then_inc(x_in[par], 16)
                    sp.dma_start(x[par][:, :], x_d[ds(t * P, P), :]).then_inc(x_in[par], 16)

        @block.tensor
        def _(pe):
            pe.wait_ge(w_in, 16)
            with pe.Fori(0, NT // 2, 1) as j:
                for par in range(2):
                    pe.wait_ge(x_in[par], 32 * j + 32)
                    pe.wait_ge(o_scaled, 2 * j)
                    for i in range(KD):
                        last = pe.matmul(p_o[:, par, :], xT[par][:, i, :], w[:, i, :], start=i == 0, stop=i == KD - 1)
                    last.then_inc(o_done, 1)

        @block.scalar
        def _(act):
            with act.Fori(0, NT, 1) as t:
                act.wait_ge(stat2, t + 1)
                act.wait_ge(rstd_done, t)
                act.activation(std[:, :], mv[:, 1:2], ACT.Sqrt, bias=C.eps[:, 0:1]).then_inc(std_done, 1)

        @block.vector
        def _(dve):
            dve.wait_ge(rows_in, 32)
            with dve.Fori(0, NT // 2, 1) as j:
                for par in range(2):
                    t = 2 * j + par
                    dve.wait_ge(o_done, t + 1)
                    dve.wait_ge(o_biased, t)
                    dve.tensor_tensor(scaled[:, :], p_o[:, par, :], scale_b[:, :], ALU.mult).then_inc(o_scaled, 1)
                    dve.wait_ge(o_scaled, t + 1)
                    dve.wait_ge(added, t)
                    dve.tensor_tensor(biased[:, :], scaled[:, :], bias_b[:, :], ALU.add).then_inc(o_biased, 1)
                    dve.wait_ge(o_biased, t + 1)
                    dve.wait_ge(x_in[par], 32 * j + 32)
                    dve.wait_ge(y_done, t)
                    dve.tensor_tensor(res[:, :], biased[:, :], x[par][:, :], ALU.add).then_inc(added, 1)
                    dve.wait_ge(added, t + 1)
                    dve.bn_stats(stats[:, :], res[:, :]).then_inc(stat1, 1)
                    dve.wait_ge(stat1, t + 1)
                    dve.memset(idle[:, :], 0.0)
                    dve.bn_aggr(mv[:, :], stats[:, :]).then_inc(stat2, 1)
                    dve.wait_ge(std_done, t + 1)
                    dve.reciprocal(rstd[:, :], std[:, :]).then_inc(rstd_done, 1)
                    dve.wait_ge(rstd_done, t + 1)
                    dve.wait_ge(out[par], 16 * j)
                    dve.tensor_scalar(y[par][:, :], res[:, :], mv[:, 0:1], rstd[:, 0:1], ALU.subtract,
                                      ALU.mult).then_inc(y_done, 1)


class Constants:
    pass


def setup_phase(nc, C, lambdas, neg_lambda, norm_ws, norm_w, rows):
    with ExitStack() as ctx:
        sb = lambda n, s, d: ctx.enter_context(nc.sbuf_tensor(f"set_{n}", s, d))
        sem = lambda n: ctx.enter_context(nc.semaphore(f"set_{n}"))
        vec = sb("vec", [P, 2, 2, 2, HD], F32)
        prod = sb("prod", [P, 2, 2, HD], F32)
        dots = sb("dots", [P, 2, 2], F32)
        lam = sb("lam", [P, 2, 2], F32)
        v_in, w_in, r_in = sem("v_in"), sem("w_in"), sem("r_in")
        blank, c1, c2, c3, c4 = sem("blank"), sem("c1"), sem("c2"), sem("c3"), sem("c4")
        block = ctx.enter_context(nc.Block())

        @block.sync
        def _(sp):
            for l in range(2):
                for e in range(2):
                    for f in range(2):
                        sp.dma_start(vec[:, l, e, f, :], lambdas[l][2 * e + f].partition_broadcast(P)
                                     ).then_inc(v_in, 16)
                for i in range(P // VD):
                    sp.dma_start(norm_w[i * VD:(i + 1) * VD, l:l + 1], norm_ws[l].unsqueeze(1)).then_inc(w_in, 16)
            for dst, src in rows:
                sp.dma_start(dst, src).then_inc(r_in, 16)
            sp.wait_ge(r_in, 16 * len(rows))
            sp.wait_ge(w_in, 16 * 2 * (P // VD))

        @block.gpsimd
        def _(pool):
            for t in (C.ident, C.ident_b, C.mask_qk, C.mask_kq):
                pool.memset(t[:, :], 0.0).then_inc(blank, 1)
            pool.memset(C.eps[:, :], EPS).then_inc(blank, 1)
            pool.wait_ge(blank, 5)
            for t in (C.ident, C.ident_b):
                pool.affine_select(out=t[:, :], in_=t[:, :], compare_op=ALU.not_equal, fill=1.0, base=0,
                                   pattern=[[-1, P]], channel_multiplier=1)
            pool.affine_select(out=C.mask_qk[:, :], in_=C.mask_qk[:, :], compare_op=ALU.is_ge, fill=MASKED, base=0,
                               pattern=[[-1, P]], channel_multiplier=1)
            pool.affine_select(out=C.mask_kq[:, :], in_=C.mask_kq[:, :], compare_op=ALU.is_ge, fill=MASKED, base=0,
                               pattern=[[1, P]], channel_multiplier=-1)

        @block.vector
        def _(dve):
            dve.wait_ge(v_in, 16 * 8)
            dve.tensor_tensor(prod[:, :, :, :], vec[:, :, :, 0, :], vec[:, :, :, 1, :], ALU.mult).then_inc(c1, 1)
            dve.wait_ge(c1, 1)
            dve.tensor_reduce(dots[:, :, :], prod[:, :, :, :], AX.X, ALU.add).then_inc(c2, 1)
            dve.wait_ge(c3, 1)
            for l in range(2):
                dve.scalar_tensor_tensor(out=neg_lambda[l][:, :], in0=lam[:, l, 1:2], scalar=-LAMBDA_INIT,
                                         in1=lam[:, l, 0:1], op0=ALU.add, op1=ALU.subtract)

        @block.scalar
        def _(act):
            act.wait_ge(c2, 1)
            act.activation(lam[:, :, :], dots[:, :, :], ACT.Exp).then_inc(c3, 1)


def program(nc, A, out):
    dram = lambda n, s, d: nc.dram_tensor(n, s, d, kind="Internal").ap()
    q_stack = [dram(f"q_stack{l}", (B * D // HD, SROWS, T), BF16) for l in range(2)]
    k_stack = [dram(f"k_stack{l}", (B * L.k_dims // HD, SROWS, T), BF16) for l, L in enumerate((L0, L1))]
    x1, x2, x3 = (dram(f"x{i}", (TOK, D), F32) for i in (1, 2, 3))
    x1T, x2T, x3T = (dram(f"x{i}T", (D, TOK), F32) for i in (1, 2, 3))
    x0 = A["L0_attn_x"].rearrange("b t d -> (b t) d")
    out = out.rearrange("b t d -> (b t) d")
    with ExitStack() as ctx:
        sb = lambda n, s, d: ctx.enter_context(nc.sbuf_tensor(n, s, d))
        C = Constants()
        C.ident = sb("ident", [P, P], F32)
        C.ident_b = sb("ident_b", [P, P], BF16)
        C.mask_qk = sb("mask_qk", [P, P], BF16)
        C.mask_kq = sb("mask_kq", [P, P], BF16)
        C.eps = sb("eps", [P, 1], F32)
        neg_lambda = [sb(f"neg_lambda{l}", [P, 1], F32) for l in range(2)]
        norm_w = sb("norm_w", [P, 2], F32)
        g_scale = sb("g_scale", [P, FT], F32)
        u_scale = sb("u_scale", [P, FT], F32)
        setup_phase(
            nc, C, [[A[f"L{l}_attn_lambda_{x}"] for x in ("q1", "k1", "q2", "k2")] for l in range(2)], neg_lambda,
            [A["L0_attn_subln_w"], A["L1_attn_ln_w"]], norm_w,
            [(g_scale[:, :], A["L0_ffn_gate_scale_T"]),
             (u_scale[:, :], A["L0_ffn_up_scale_T"])])
        v_sb = sb("v_all", [P, NT * D], F32)
        qkv_phase(nc, L0, A["x_T"], [A[f"L0_attn_{w}_T"] for w in ("wq", "wk", "wv")], q_stack[0], k_stack[0], v_sb)
        attn = sb("attn", [P, NT * D], F32)
        with ExitStack() as ffn_ctx:
            ffn_w = ffn_ctx.enter_context(nc.sbuf_tensor("ffn_w", [P, FFN_W], F32))
            w_at = [0, KD * FFN, 2 * KD * FFN]
            wg, wu = (ffn_w[:, a:a + KD * FFN].rearrange("p (k n) -> p k n", k=KD) for a in w_at[:2])
            wd = ffn_w[:, w_at[2]:FFN_W].rearrange("p (k n) -> p k n", k=FT)
            ffn_src = [(a, A[f"L0_ffn_{w}_w_T"].rearrange("(k p) n -> p k n", p=P))
                       for a, w in zip(w_at, ("gate", "up", "down"))]
            attention_phase(nc, L0, q_stack[0], k_stack[0], v_sb, attn, neg_lambda[0][:, 0:1], C, ffn_w, ffn_src)
            mix_phase(nc, "mix0", attn, A["L0_attn_wo_T"], norm_w[:, 0:1], x0, x1, x1T, C)
            ffn_phase(nc, wg, wu, wd, attn[:, :], g_scale, u_scale, A["L0_ffn_down_scale"], x1T, x1, x2, x2T, C)
        qkv_phase(nc, L1, x2T, [A[f"L1_attn_{w}_T"] for w in ("Wq", "Wk", "Wv")], q_stack[1], k_stack[1], v_sb)
        attention_phase(nc, L1, q_stack[1], k_stack[1], v_sb, attn, neg_lambda[1][:, 0:1], C)
        mix_phase(nc, "mix1", attn, A["L1_attn_Wo_T"], norm_w[:, 1:2], x2, x3, x3T, C)
        linear_phase(nc, A["L1_ffn_weight_T"], A["L1_ffn_scale_weight"], A["L1_ffn_bias"], x3T, x3, out, C)


TRANSPOSED = ["L0_attn_wq", "L0_attn_wk", "L0_attn_wv", "L0_attn_wo", "L0_ffn_gate_w", "L0_ffn_up_w",
              "L0_ffn_down_w", "L1_attn_Wq", "L1_attn_Wk", "L1_attn_Wv", "L1_attn_Wo", "L1_ffn_weight"]
PLAIN = ["L0_attn_x", "L0_attn_lambda_q1", "L0_attn_lambda_k1", "L0_attn_lambda_q2", "L0_attn_lambda_k2",
         "L0_attn_subln_w", "L0_ffn_down_scale", "L1_attn_lambda_q1",
         "L1_attn_lambda_k1", "L1_attn_lambda_q2", "L1_attn_lambda_k2", "L1_attn_ln_w", "L1_ffn_scale_weight",
         "L1_ffn_bias"]


def kernel(**inputs):
    import numpy as np
    import concourse.bacc as bacc
    from concourse.bass_utils import run_bass_kernel_spmd

    arrays = {name: np.ascontiguousarray(inputs[name]) for name in PLAIN}
    for name in TRANSPOSED:
        arrays[name + "_T"] = np.ascontiguousarray(np.asarray(inputs[name]).T)
    for name in ("L0_ffn_gate_scale", "L0_ffn_up_scale"):
        arrays[name + "_T"] = np.ascontiguousarray(np.asarray(inputs[name]).reshape(FT, P).T)
    x = np.asarray(inputs["L0_attn_x"])
    arrays["x_T"] = np.ascontiguousarray(x.reshape(-1, x.shape[-1]).T)
    nc = bacc.Bacc("TRN2", target_bir_lowering=False, num_devices=1)
    A = {name: nc.dram_tensor(f"in_{name}", a.shape, mybir.dt.from_np(a.dtype), kind="ExternalInput").ap()
         for name, a in arrays.items()}
    out = nc.dram_tensor("out", (B, T, D), F32, kind="ExternalOutput").ap()
    program(nc, A, out)
    r = run_bass_kernel_spmd(nc, [{f"in_{name}": a for name, a in arrays.items()}], core_ids=[0])
    return r.results[0]["out"]
```

```python
import math
from contextlib import ExitStack

import concourse.bass as bass
from concourse import mybir

F32 = mybir.dt.float32
BF16 = mybir.dt.bfloat16
I32 = mybir.dt.int32
F32R = mybir.dt.float32r
ALU = mybir.AluOpType
ACT = mybir.ActivationFunctionType
AX = mybir.AxisListType
ds = bass.ds

P = 128
B, T, D = 2, 1024, 512
TOK = B * T
KD = D // P
CH = 512
NCH = TOK // CH
NT = TOK // P
HD = 16
VD = 2 * HD
NH = D // VD
KV_HEADS = 4
PARTS = 3
FFN = 2048
FT = FFN // P
Q_PART = [0, 0, 0, 1, 1, 2]
K_PART = [0, 1, 2, 0, 1, 0]
SROWS = len(Q_PART) * HD
FROWS = SROWS + 2
KT = T // P
QC = T // CH
QPC = CH // P
HEADS = B * NH
SBUF_ALIGN = 32
GT = 2
GROUPS = FT // GT
GROUP_BUFFERS = 2
H_SIZE = GROUP_BUFFERS * GT * CH
WRITTEN_OUT = 6
GW = KD * GT * P
EPS = 1e-5
LAMBDA_INIT = 0.8 - 0.6 * math.exp(-0.3 * 12)
MASKED = -1e30
ZERO_POINT = 128.0
PRING = 4
TURN_LAG = 1
RING = 3
AHEAD = PRING
UNIT_FIXED = 75


class Layer:

    def __init__(self, name, k_dims, v_dims, causal, max_begins, max_ends, shift_turned):
        self.max_begins, self.max_ends, self.shift_turned = max_begins, max_ends, shift_turned
        self.name, self.k_dims, self.v_dims, self.causal = name, k_dims, v_dims, causal
        self.k_subs = k_dims // HD // NH if k_dims == D else 1
        self.steps = [(qc, kt, max(0, kt - QPC * qc) * P if causal else 0)
                      for qc in range(QC) for kt in range(QPC * (qc + 1) if causal else KT)]
        self.units = []
        for sub in range(2):
            for qt in range(KT):
                keys = (qt + 1) * P if causal else T
                for kc in range(-(-keys // CH)):
                    self.units.append((sub, qt, kc, min(CH, keys - kc * CH)))
        assert len(self.steps) % PRING == 0 and len(self.units) % 2 == 0
        self.qc_last = [max(s for s, x in enumerate(self.steps) if x[0] == qc) for qc in range(QC)]
        self.ring_first = len(self.units) + 1
        self.ring_head = len(self.units) + 1 + QC
        self.orders = {has_next: self.order(has_next) for has_next in (False, True)}

    def order(self, has_next):
        S = len(self.steps)
        items = []
        for s in range(1, S + 1):
            if s < S or has_next:
                items.append(("score", s, 2 * (CH - self.steps[s % S][2])))
            if s == TURN_LAG:
                items.append(("turn", QC - 1, 0))
            for qc in range(QC - 1):
                if s == self.qc_last[qc] + 1 + TURN_LAG:
                    items.append(("turn", qc, 0))
            items.append(("sum", s - 1, 4 * (CH - self.steps[s - 1][2])))
        if not has_next:
            return [x[:2] for x in items]
        work = sum(x[2] for x in items)
        cost = [keys + UNIT_FIXED for _, _, _, keys in self.units]
        out, done, u, spent, turned = [], 0, 0, 0, False
        for what, i, weight in items:
            if (what, i) == ("score", S) and not turned:
                out.append(("turn_shift", 0))
                turned = True
            out.append((what, i))
            done += weight
            while u < len(cost) and done >= work * (self.max_begins + (self.max_ends - self.max_begins) * spent / sum(cost)):
                out.append(("max", u))
                spent += cost[u]
                u += 1
            if u == len(cost) and not turned and done >= work * self.shift_turned:
                out.append(("turn_shift", 0))
                turned = True
        assert u == len(cost) and turned
        return out

    def v_column(self, n):
        return (n % NH) * VD if self.v_dims == D else ((n % NH) // (NH // KV_HEADS)) * VD

    def k_stack(self, n):
        return n if self.k_subs == 2 else n // 2


import os
_a=[float(z) for z in os.environ.get("PA","0.05 0.72 0.76 0.05 0.65 0.7").split()]
L0 = Layer("l0", D, D, False, *_a[:3])
L1 = Layer("l1", D // 4, D // 4, True, *_a[3:])


class Area:

    def __init__(self, ctx, nc, name, size):
        self.nc, self.name = nc, name
        self.offset = -(-nc.sbuf_base // SBUF_ALIGN) * SBUF_ALIGN
        self.whole = ctx.enter_context(nc.sbuf_tensor(name, [P, size], F32))

    def taken_by(self, user, shape, dtype, at=0):
        return self.nc.alloc_sbuf_tensor_at(f"{self.name}_{user}", shape, dtype, offset=self.offset + 4 * at)


class Split:

    def __init__(self, hi, lo):
        self.hi, self.lo = hi, lo

    def __getitem__(self, at):
        return Split(self.hi[at], self.lo[at])


def product(pe, out, terms, start=True, stop=True):
    passes = [x for lhs, rhs in terms for x in ((lhs.hi, rhs.hi), (lhs.hi, rhs.lo), (lhs.lo, rhs.hi))]
    for i, (lhs, rhs) in enumerate(passes):
        last = pe.matmul(out, lhs, rhs, start=start and i == 0, stop=stop and i == len(passes) - 1)
    return last


def wait_from_first(engine, semaphore, count):
    if not isinstance(count, int) or count > 0:
        engine.wait_ge(semaphore, count)


def credit(engine, *semaphores):
    for semaphore in semaphores:
        engine.sem_inc(semaphore, AHEAD)


def qkv_phase(nc, L, xT, q_stack_d, k_stack_d, v_sb, w_area, w_first, w_d=None, x_stage=None, xT_d=None):
    widths = [D, L.k_dims, L.v_dims]
    q_tiles, k_tiles = D // P, L.k_dims // P
    MT = q_tiles + k_tiles
    first_load = xT_d is not None
    QK_BANKS = math.gcd(2 * MT, 4)
    with ExitStack() as ctx:
        sb = lambda n, s, d: ctx.enter_context(nc.sbuf_tensor(f"{L.name}_{n}", s, d))
        ps = lambda n, s, d: ctx.enter_context(nc.psum_tensor(f"{L.name}_{n}", s, d))
        sem = lambda n: ctx.enter_context(nc.semaphore(f"{L.name}_{n}"))
        w_at = [w_first + KD * sum(widths[:i]) for i in range(3)]
        staged = [w_area.whole[:, at:at + KD * x].rearrange("p (k n) -> p k n", k=KD) for at, x in zip(w_at, widths)]
        w = [Split(sb(f"w{n}_hi", [P, KD, x], F32R), w_area.taken_by(f"{L.name}_w{n}_lo", [P, KD, x], F32R, at))
             for n, at, x in zip("qkv", w_at, widths)]
        part = [[sb(f"part{r}{i}", [P, CH], BF16) for i in range(PARTS)] for r in range(2)]
        rest = [sb(f"rest{r}", [P, CH], F32) for r in range(2)]
        p_qk = ps("p_qk", [P, QK_BANKS, CH], F32)
        p_v = ps("p_v", [P, 2, CH], F32)
        w_in = x_in = 3 * [None]
        if first_load:
            w_in, x_in = [sem(f"w_in{i}") for i in range(3)], [sem(f"x_in{c}") for c in range(NCH)]
            pool_hi, pool_lo = sem("pool_hi"), sem("pool_lo")
        split_hi, split_lo = sem("split_hi"), sem("split_lo")
        qk_done, v_done, v_kept = sem("qk_done"), sem("v_done"), sem("v_kept")
        part1, rest1, part2, part3 = sem("part1"), sem("rest1"), sem("part2"), sem("part3")
        stored = [sem("stored0"), sem("stored1")]
        block = ctx.enter_context(nc.Block())
        jobs = [(staged[0][:, k, :], w[0][:, k, :], w_in[0]) for k in range(KD)]
        if first_load:
            jobs += [(x_stage[:, k, 0:CH], xT[:, k, 0:CH], x_in[0]) for k in range(KD)]
        qk_jobs = len(jobs)
        jobs += [(staged[1][:, k, :], w[1][:, k, :], w_in[1]) for k in range(KD)]
        jobs += [(staged[2][:, k, :], w[2][:, k, :], w_in[2]) for k in range(KD)]

        @block.sync
        def _(sp):
            def load_w(i):
                sp.dma_start(staged[i], w_d[i].rearrange("(k p) n -> p k n", p=P)).then_inc(w_in[i], 16)

            def load_x(c):
                cols = slice(c * CH, (c + 1) * CH)
                sp.dma_start(x_stage[:, :, cols], xT_d.rearrange("(k p) n -> p k n", p=P)[:, :, cols]
                             ).then_inc(x_in[c], 16)

            credit(sp, *stored)
            if first_load:
                load_w(0)
                load_x(0)
                load_w(1)
                load_w(2)
                for c in range(1, NCH):
                    load_x(c)
            with sp.Fori(0, NCH // 2, 1) as j:
                for par in range(2):
                    for m in range(MT):
                        r = (par * MT + m) % 2
                        is_q = m < q_tiles
                        dst = q_stack_d if is_q else k_stack_d
                        bat, tin = j, par * CH
                        sp.wait_ge(part3, AHEAD + (j * 2 + par) * MT + m + 1)
                        for g in range(len(Q_PART)):
                            i = (Q_PART if is_q else K_PART)[g]
                            subs = P // HD
                            mm = m if is_q else m - q_tiles
                            per_batch = (D if is_q else L.k_dims) // HD
                            out = dst[ds(bat * per_batch + mm * subs, subs), g * HD:(g + 1) * HD, tin:tin + CH]
                            sp.dma_start(out, part[r][i][:, :]).then_inc(stored[r], 16)
            for r in range(2):
                sp.wait_ge(stored[r], AHEAD + 16 * len(Q_PART) * NCH * MT // 2)

        @block.gpsimd
        def _(pool):
            if first_load:
                for c in range(1, NCH):
                    pool.wait_ge(x_in[c], 16)
                    for k in range(KD):
                        at = (slice(None), k, slice(c * CH, (c + 1) * CH))
                        pool.tensor_copy(xT.hi[at], x_stage[at]).then_inc(pool_hi, 1)
                        pool.wait_ge(pool_hi, (c - 1) * KD + k + 1)
                        pool.tensor_tensor(xT.lo[at], x_stage[at], xT.hi[at], ALU.subtract).then_inc(pool_lo, 1)

        @block.tensor
        def _(pe):
            pe.wait_ge(split_lo, qk_jobs)
            for c in range(NCH):
                if first_load and c:
                    pe.wait_ge(pool_lo, KD * c)
                for m in range(MT):
                    u = c * MT + m
                    if u >= QK_BANKS:
                        pe.wait_ge(rest1, AHEAD + u + 1 - QK_BANKS)
                    if u == q_tiles:
                        pe.wait_ge(split_lo, qk_jobs + KD)
                    lhs, mm = (w[0], m) if m < q_tiles else (w[1], m - q_tiles)
                    product(pe, p_qk[:, u % QK_BANKS, :],
                            [(lhs[:, k, mm * P:(mm + 1) * P], xT[:, k, c * CH:(c + 1) * CH]) for k in range(KD)]
                            ).then_inc(qk_done, 1)
                if c == 0:
                    pe.wait_ge(split_lo, qk_jobs + 2 * KD)
                for t in range(c * QPC, (c + 1) * QPC):
                    if t >= 2:
                        pe.wait_ge(v_kept, AHEAD + t - 1)
                    product(pe, p_v[:, t % 2, 0:L.v_dims],
                            [(xT[:, k, t * P:(t + 1) * P], w[2][:, k, :]) for k in range(KD)]).then_inc(v_done, 1)

        @block.scalar
        def _(act):
            credit(act, v_kept)
            for i, (src, to, came) in enumerate(jobs):
                if first_load:
                    act.wait_ge(came, 16)
                act.activation(to.hi, src, ACT.Copy).then_inc(split_hi, 1)
            with act.Fori(0, NCH // 2, 1) as j:
                for u in range(2 * MT):
                    n = j * (2 * MT) + u
                    r = u % 2
                    act.wait_ge(qk_done, n + 1)
                    act.wait_ge(stored[r], AHEAD + 16 * len(Q_PART) * (j * MT + u // 2))
                    act.activation(part[r][0][:, :], p_qk[:, u % QK_BANKS, :], ACT.Copy).then_inc(part1, 1)
                    act.wait_ge(rest1, AHEAD + n + 1)
                    act.activation(part[r][1][:, :], rest[r][:, :], ACT.Copy).then_inc(part2, 1)
                    if u % MT == MT - 1:
                        for t in range(QPC):
                            k = (u // MT) * QPC + t
                            act.wait_ge(v_done, j * (2 * QPC) + k + 1)
                            act.activation(v_sb[:, ds((j * (2 * QPC) + k) * L.v_dims, L.v_dims)],
                                           p_v[:, k % 2, 0:L.v_dims], ACT.Copy).then_inc(v_kept, 1)

        @block.vector
        def _(dve):
            credit(dve, rest1, part3)
            for i, (src, to, _) in enumerate(jobs):
                dve.wait_ge(split_hi, i + 1)
                dve.tensor_tensor(to.lo, src, to.hi, ALU.subtract).then_inc(split_lo, 1)
            with dve.Fori(0, NCH // 2, 1) as j:
                for u in range(2 * MT):
                    n = j * (2 * MT) + u
                    r = u % 2
                    dve.wait_ge(part1, n + 1)
                    dve.wait_ge(part3, AHEAD + n - 1)
                    dve.tensor_tensor(rest[r][:, :], p_qk[:, u % QK_BANKS, :], part[r][0][:, :],
                                      ALU.subtract).then_inc(rest1, 1)
                    dve.wait_ge(part2, n + 1)
                    dve.tensor_tensor(part[r][2][:, :], rest[r][:, :], part[r][1][:, :],
                                      ALU.subtract).then_inc(part3, 1)


def attention_phase(nc, L, q_stack_d, k_stack_d, v_sb, attn, neg_lambda, C, loads=()):
    S, U = len(L.steps), len(L.units)
    KS = L.k_subs
    with ExitStack() as ctx:
        sb = lambda n, s, d: ctx.enter_context(nc.sbuf_tensor(f"{L.name}_{n}", s, d))
        ps = lambda n, s, d: ctx.enter_context(nc.psum_tensor(f"{L.name}_{n}", s, d))
        sem = lambda n: ctx.enter_context(nc.semaphore(f"{L.name}_{n}"))
        q = [sb(f"q{i}", [P, 2, T], BF16) for i in range(2)]
        k = [sb(f"k{i}", [P, KS, T], BF16) for i in range(2)]
        v = [sb(f"v{i}", [P, KT, VD], F32) for i in range(2)]
        prob = [sb(f"prob{i}", [P, 2, CH], F32) for i in range(PRING)]
        ones = sb("ones", [P, VD], F32)
        maxima = sb("maxima", [P, 2 * KT, 2], F32)
        shift = sb("shift", [P, 2 * KT], F32)
        shift_parts = sb("shift_parts", [P, 2, 2 * KT], BF16)
        shift_rows = sb("shift_rows", [4 * KT, P], BF16)
        sums = sb("sums", [P, CH], F32)
        recip = sb("recip", [P, QPC, 2], F32)
        half = sb("half", [P, 2, QPC, VD], F32)
        p_score = ps("p_score", [P, 2, 2, CH], F32)
        p_ring = ps("p_ring", [P, RING, CH], F32)
        p_out = ps("p_out", [P, CH], F32)
        q_in = [sem("q_in0"), sem("q_in1")]
        shift_in = [sem("shift_in0"), sem("shift_in1")]
        ready = sem("ready")
        scored, exped, summed, out_copied = sem("scored"), sem("exped"), sem("summed"), sem("out_copied")
        filled, freed = sem("filled"), sem("freed")
        shift_made, shift_rest, shift_copied = sem("shift_made"), sem("shift_rest"), sem("shift_copied")
        out_recip, out_scaled, out_kept = sem("out_recip"), sem("out_scaled"), sem("out_kept")
        v_in, loaded = sem("v_in"), sem("loaded")
        block = ctx.enter_context(nc.Block())

        def ring_items(n, has_next=True):
            at = 0
            for what, i in L.orders[has_next]:
                if what in ("max", "turn", "turn_shift"):
                    yield what, i, at
                    at += 1
                else:
                    yield what, i, None
            assert at == (L.ring_head if has_next else QC)

        def ring_count(n, at):
            return at if n is None else L.ring_first + n * L.ring_head + at

        @block.sync
        def _(sp):
            def load(n, par, first=False):
                if not first:
                    sp.wait_ge(scored, (n - 1) * S)
                sp.dma_start(q[par][0:SROWS, :, :],
                             q_stack_d[ds(2 * n, 2)].rearrange("s r t -> r s t")).then_inc(q_in[par], 16)
                sp.dma_start(k[par][0:SROWS, :, :],
                             k_stack_d[ds(L.k_stack(n) * KS, KS)].rearrange("s r t -> r s t")
                             ).then_inc(q_in[par], 16)

            def shift_row(n, par):
                sp.wait_ge(shift_copied, n + 1)
                for i in range(2):
                    sp.dma_start(q[par][SROWS + i:SROWS + i + 1, :, :],
                                 shift_rows[2 * KT * i:2 * KT * (i + 1), :]).then_inc(shift_in[par], 16)

            load(0, 0, first=True)
            shift_row(0, 0)
            load(1, 1, first=True)
            shift_row(1, 1)
            with sp.Fori(0, HEADS // 2 - 1, 1) as j:
                for par in range(2):
                    load(2 * j + 2 + par, par)
                    shift_row(2 * j + 2 + par, par)
            for par in range(2):
                sp.wait_ge(shift_in[par], 32 * HEADS // 2)

        @block.gpsimd
        def _(pool):
            def take_v(n, par):
                tiles = v_sb[:, 0:NT * L.v_dims].rearrange("p (t c) -> p t c", c=L.v_dims)
                pool.tensor_copy(v[par][:, :, :], tiles[:, ds((n // NH) * KT, KT), ds(L.v_column(n), VD)]
                                 ).then_inc(v_in, 1)

            for dst, src in loads:
                pool.dma_start(dst, src).then_inc(loaded, 16)
            for par in range(2):
                take_v(par, par)
            with pool.Fori(0, HEADS // 2 - 1, 1) as j:
                for par in range(2):
                    pool.wait_ge(summed, AHEAD + (2 * j + par + 1) * S)
                    take_v(2 * j + 2 + par, par)
            pool.wait_ge(loaded, 16 * len(loads))

        @block.tensor
        def _(pe):
            credit(pe, summed)

            def take_bank(count, at):
                pe.wait_ge(freed, AHEAD + count - at + max(at - RING + 1, 0))

            def max_unit(n, par, u, count, at):
                sub, qt, kc, keys = L.units[u]
                bank = p_ring[:, at % RING, :]
                if u == 0:
                    pe.wait_ge(q_in[par], 32 * (n // 2) + 32)
                take_bank(count, at)
                diagonal = L.causal and kc == qt // QPC
                last = pe.matmul(bank[:, 0:keys], q[par][0:SROWS, sub, qt * P:(qt + 1) * P],
                                 k[par][0:SROWS, sub * (KS - 1), kc * CH:kc * CH + keys], start=True, stop=not diagonal)
                if diagonal:
                    last = pe.matmul(bank[:, keys - P:keys], C.ident_b[:, :], C.mask_qk[:, :], start=False, stop=True)
                last.then_inc(filled, 1)

            def turn_shift(n, count, at):
                pe.wait_ge(shift_rest, n + 1)
                take_bank(count, at)
                pe.transpose(p_ring[0:4 * KT, at % RING, 0:P // 2].bitcast(BF16),
                             shift_parts[:, :, :].rearrange("p a b -> p (a b)"), C.ident_b[:, :]).then_inc(filled, 1)

            def score(n, par, s):
                qc, kt, off = L.steps[s]
                if s == 0:
                    pe.wait_ge(shift_in[par], 32 * (n // 2) + 32)
                pe.wait_ge(exped, AHEAD + n * S + s - 1)
                for sub in range(2):
                    diagonal = L.causal and kt >= QPC * qc
                    last = pe.matmul(p_score[:, s % 2, sub, off:CH], k[par][0:FROWS, sub * (KS - 1), kt * P:(kt + 1) * P],
                                     q[par][0:FROWS, sub, qc * CH + off:(qc + 1) * CH], start=True, stop=not diagonal)
                    if diagonal:
                        last = pe.matmul(p_score[:, s % 2, sub, off:off + P], C.ident_b[:, :], C.mask_kq[:, :],
                                         start=False, stop=True)
                last.then_inc(scored, 1)

            def sum_up(n, par, s):
                qc, kt, off = L.steps[s]
                if s == 0:
                    pe.wait_ge(v_in, n + 1)
                first, final = kt == 0, s == L.qc_last[qc]
                if first:
                    pe.wait_ge(out_copied, AHEAD + QC * n + qc)
                pe.wait_ge(exped, AHEAD + n * S + s + 1)
                for sub in range(2):
                    for i, lhs in enumerate((v[par][:, kt, :], ones[:, :])):
                        r0 = (2 * sub + i) * VD
                        last = pe.matmul(p_out[r0:r0 + VD, off:CH], lhs, prob[s % PRING][:, sub, off:CH],
                                         start=first, stop=final)
                last.then_inc(summed, 1)

            def turn(copied, count, at):
                pe.wait_ge(out_copied, AHEAD + copied)
                take_bank(count, at)
                for i in range(QPC):
                    last = pe.transpose(p_ring[:, at % RING, i * P:(i + 1) * P], sums[:, i * P:(i + 1) * P],
                                        C.ident[:, :])
                last.then_inc(filled, 1)

            def head(n, par, has_next=True):
                for what, i, at in ring_items(n, has_next):
                    if what == "score":
                        score(*((n, par, i) if i < S else (n + 1, 1 - par, 0)))
                    elif what == "sum":
                        sum_up(n, par, i)
                    elif what == "turn":
                        turn(QC * n + (0 if i == QC - 1 else i + 1), ring_count(n, at), at)
                    elif what == "max":
                        max_unit(n + 1, 1 - par, i, ring_count(n, at), at)
                    else:
                        turn_shift(n + 1, ring_count(n, at), at)

            pe.wait_ge(ready, 5)
            for u in range(U):
                max_unit(0, 0, u, u, u)
            turn_shift(0, U, U)
            score(0, 0, 0)
            with pe.Fori(0, HEADS // 2 - 1, 1) as j:
                for par in range(2):
                    head(2 * j + par, par)
            head(HEADS - 2, 0)
            head(HEADS - 1, 1, has_next=False)
            turn(QC * HEADS, ring_count(HEADS - 1, QC), QC)

        @block.scalar
        def _(act):
            credit(act, exped, out_copied)

            def copy_out(n, qc):
                act.wait_ge(summed, AHEAD + n * S + L.qc_last[qc] + 1)
                act.wait_ge(out_kept, AHEAD + QC * n + qc + 1)
                act.activation(sums[:, :], p_out[:, :], ACT.Copy).then_inc(out_copied, 1)

            def exp(n, i):
                qc, kt, off = L.steps[i]
                act.wait_ge(scored, n * S + i + 1)
                act.wait_ge(summed, AHEAD + n * S + i - PRING + 1)
                act.activation(prob[i % PRING][:, :, off:CH], p_score[:, i % 2, :, off:CH], ACT.Exp,
                               scale=HD ** -0.5).then_inc(exped, 1)

            def head(n, par, has_next=True):
                for what, i in L.orders[has_next]:
                    if what == "score":
                        exp(*((n, i) if i < S else (n + 1, 0)))
                    elif what == "sum" and i in L.qc_last:
                        copy_out(n, L.qc_last.index(i))

            exp(0, 0)
            with act.Fori(0, HEADS // 2 - 1, 1) as j:
                for par in range(2):
                    head(2 * j + par, par)
            head(HEADS - 2, 0)
            head(HEADS - 1, 1, has_next=False)

        @block.vector
        def _(dve):
            credit(dve, freed, out_kept)

            def reduce(u, count, at):
                sub, qt, kc, keys = L.units[u]
                dve.wait_ge(filled, count + 1)
                dve.tensor_reduce(maxima[:, sub * KT + qt, kc:kc + 1], p_ring[:, at % RING, 0:keys], AX.X, ALU.max,
                                  negate=True).then_inc(freed, 1)

            def make_shift(n, count):
                dve.wait_ge(freed, AHEAD + count + 1)
                dve.tensor_reduce(shift[:, :], maxima[:, :, :], AX.X, ALU.min).then_inc(shift_made, 1)
                dve.wait_ge(shift_made, 2 * n + 1)
                dve.tensor_copy(shift_parts[:, 0, :], shift[:, :]).then_inc(shift_made, 1)
                dve.wait_ge(shift_made, 2 * n + 2)
                dve.tensor_tensor(shift_parts[:, 1, :], shift[:, :], shift_parts[:, 0, :],
                                  ALU.subtract).then_inc(shift_rest, 1)

            def copy_shift(n, count, at, sent=None):
                dve.wait_ge(filled, count + 1)
                if sent:
                    dve.wait_ge(*sent)
                dve.tensor_copy(shift_rows[:, :], p_ring[0:4 * KT, at % RING, 0:P // 2].bitcast(BF16)
                                ).then_inc(shift_copied, 1)
                dve.wait_ge(shift_copied, n + 1)
                dve.sem_inc(freed, 1)

            def keep(kept, n, qc, count, at):
                dve.wait_ge(filled, count + 1)
                cols = p_ring[:, at % RING, :].rearrange("p (b s w) -> p b s w", b=QPC, s=2)
                dve.wait_ge(out_kept, AHEAD + kept)
                dve.reciprocal(recip[:, :, :], cols[:, :, :, VD]).then_inc(out_recip, 1)
                dve.wait_ge(out_recip, kept + 1)
                dve.tensor_tensor(half[:, 0, :, :], cols[:, :, 0, 0:VD], recip[:, :, 0:1].to_broadcast([P, QPC, VD]),
                                  ALU.mult).then_inc(out_scaled, 1)
                dve.tensor_tensor(half[:, 1, :, :], cols[:, :, 1, 0:VD], recip[:, :, 1:2].to_broadcast([P, QPC, VD]),
                                  ALU.mult).then_inc(freed, 1)
                dve.wait_ge(out_scaled, kept + 1)
                dve.wait_ge(freed, AHEAD + count + 1)
                tiles = attn[:, :].rearrange("p (t c) -> p t c", c=D)
                to = tiles[:, ds((n // NH) * KT + qc * QPC, QPC), ds((n % NH) * VD, VD)]
                dve.scalar_tensor_tensor(
                    out=to, in0=half[:, 1, :, :], scalar=neg_lambda, in1=half[:, 0, :, :],
                    op0=ALU.mult, op1=ALU.add).then_inc(out_kept, 1)

            def head(n, par, has_next=True):
                for what, i, at in ring_items(n, has_next):
                    if what == "max":
                        reduce(i, ring_count(n, at), at)
                        if i == U - 1:
                            make_shift(n + 1, ring_count(n, at))
                    elif what == "turn_shift":
                        copy_shift(n + 1, ring_count(n, at), at, (shift_in[par], 32 * (n // 2) + 32))
                    elif what == "turn" and i == QC - 1:
                        keep(QC * n, (n + (HEADS - 1)) % HEADS, i, ring_count(n, at), at)
                    elif what == "turn":
                        keep(QC * n + i + 1, n, i, ring_count(n, at), at)

            dve.memset(ones[:, :], 1.0).then_inc(ready, 1)
            for i in range(2):
                dve.memset(k[i][SROWS:FROWS, :, :], 1.0).then_inc(ready, 1)
            dve.memset(sums[:, :], 1.0).then_inc(ready, 1)
            dve.memset(maxima[:, :, :], 3e38).then_inc(ready, 1)
            dve.wait_ge(ready, 5)
            for u in range(U):
                reduce(u, u, u)
            make_shift(0, U - 1)
            copy_shift(0, U, U)
            with dve.Fori(0, HEADS // 2 - 1, 1) as j:
                for par in range(2):
                    head(2 * j + par, par)
            head(HEADS - 2, 0)
            head(HEADS - 1, 1, has_next=False)
            keep(QC * HEADS, HEADS - 1, QC - 1, ring_count(HEADS - 1, QC), QC)


def tile_pipeline(engine, *stages, written_out=WRITTEN_OUT):
    def step(i, par, live=lambda t: True):
        for lag, f in stages:
            if live(i - lag):
                f(i - lag, (par - lag) % 2)

    for i in range(written_out):
        step(i, i % 2, lambda t: t >= 0)
    if written_out < NT:
        with engine.Fori(0, (NT - written_out) // 2, 1) as j:
            for par in range(2):
                step(2 * j + (written_out + par), par)
    for i in range(NT, NT + max(lag for lag, _ in stages)):
        step(i, i % 2, lambda t: t < NT)


def mix_phase(nc, name, attn, wo_area, norm_w, x, xT, C, loads):
    with ExitStack() as ctx:
        sb = lambda n, s, d: ctx.enter_context(nc.sbuf_tensor(f"{name}_{n}", s, d))
        ps = lambda n, s, d: ctx.enter_context(nc.psum_tensor(f"{name}_{n}", s, d))
        sem = lambda n: ctx.enter_context(nc.semaphore(f"{name}_{n}"))
        wo_stage = wo_area.whole[:, :].rearrange("p (k n) -> p k n", k=KD)
        wo = Split(sb("wo_hi", [P, KD, D], F32R), wo_area.taken_by(f"{name}_wo_lo", [P, KD, D], F32R))
        square = sb("square", [P, D], F32)
        mean_sq = sb("mean_sq", [P, NH], F32)
        rms = sb("rms", [P, NH], F32)
        inv_rms = sb("inv_rms", [P, NH], F32)
        normed = [sb(f"normed{i}", [P, D], F32) for i in range(2)]
        normed_T = [Split(sb(f"normed_T{i}_hi", [P, KD, P], F32R), sb(f"normed_T{i}_lo", [P, KD, P], F32R))
                    for i in range(2)]
        stats = sb("stats", [P, 6], F32)
        mv = sb("mv", [P, 2], F32)
        idle = sb("idle", [P, 1], F32)
        std, rstd, offset = sb("std", [P, 1], F32), sb("rstd", [P, 1], F32), sb("offset", [P, 1], F32)
        p_nT = ps("p_nT", [P, 2, KD, P], F32)
        p_o = ps("p_o", [P, 2, D], F32)
        p_yT = ps("p_yT", [P, 2, KD, P], F32)
        wo_scaled, wo_hi, wo_lo, loaded = sem("wo_scaled"), sem("wo_hi"), sem("wo_lo"), sem("loaded")
        squared, summed, rooted, inverted, scaled = (sem("squared"), sem("summed"), sem("rooted"), sem("inverted"),
                                                     sem("scaled"))
        turned, turned_hi, turned_lo, projected = sem("turned"), sem("turned_hi"), sem("turned_lo"), sem("projected")
        added, stat1, stat2, std_done, rstd_done, offset_done, y_done = (
            sem("added"), sem("stat1"), sem("stat2"), sem("std_done"), sem("rstd_done"), sem("offset_done"),
            sem("y_done"))
        y_turned, y_hi, y_lo = sem("y_turned"), sem("y_hi"), sem("y_lo")
        block = ctx.enter_context(nc.Block())

        @block.gpsimd
        def _(pool):
            for dst, src in loads:
                pool.dma_start(dst, src).then_inc(loaded, 16)
            pool.wait_ge(loaded, 16 * len(loads))

        @block.vector
        def _(dve):
            def invert(t, par):
                dve.wait_ge(rooted, t + 1)
                wait_from_first(dve, scaled, t)
                dve.reciprocal(inv_rms[:, :], rms[:, :]).then_inc(inverted, 1)
                dve.wait_ge(inverted, t + 1)
                wait_from_first(dve, turned, t - 1)
                dve.tensor_tensor(normed[par][:, :].rearrange("p (h w) -> p h w", w=VD),
                                  attn[:, ds(t * D, D)].rearrange("p (h w) -> p h w", w=VD),
                                  inv_rms[:, :].unsqueeze(2).to_broadcast([P, NH, VD]), ALU.mult).then_inc(scaled, 1)

            def scalars(t, par):
                dve.wait_ge(std_done, t + 1)
                wait_from_first(dve, y_done, t)
                dve.reciprocal(rstd[:, :], std[:, :]).then_inc(rstd_done, 1)
                dve.wait_ge(rstd_done, t + 1)
                dve.scalar_tensor_tensor(out=offset[:, :], in0=mv[:, 0:1], scalar=-1.0, in1=rstd[:, :],
                                         op0=ALU.mult, op1=ALU.mult).then_inc(offset_done, 1)

            def rest_of_turned(t, par):
                dve.wait_ge(turned_hi, t + 1)
                wait_from_first(dve, projected, t - 1)
                dve.tensor_tensor(normed_T[par].lo[:, :, :], p_nT[:, par, :, :], normed_T[par].hi[:, :, :],
                                  ALU.subtract).then_inc(turned_lo, 1)

            def rest_of_y(t, par):
                dve.wait_ge(y_hi, t + 1)
                dve.tensor_tensor(xT.lo[:, :, ds(t * P, P)], p_yT[:, par, :, :], xT.hi[:, :, ds(t * P, P)],
                                  ALU.subtract).then_inc(y_lo, 1)

            def mean_squares(t, par):
                dve.wait_ge(squared, t + 1)
                wait_from_first(dve, rooted, t)
                dve.tensor_reduce(mean_sq[:, :], square[:, :].rearrange("p (h w) -> p h w", w=VD), AX.X,
                                  ALU.add).then_inc(summed, 1)

            def add(t, par):
                dve.wait_ge(projected, t + 1)
                dve.tensor_tensor(x[:, ds(t, 1), :].squeeze(1), p_o[:, par, :], x[:, ds(t, 1), :].squeeze(1), ALU.add
                                  ).then_inc(added, 1)
                dve.wait_ge(added, t + 1)
                dve.memset(idle[:, :], 0.0)
                dve.bn_stats(stats[:, :], x[:, ds(t, 1), :].squeeze(1)).then_inc(stat1, 1)
                dve.wait_ge(stat1, t + 1)
                wait_from_first(dve, offset_done, t)
                dve.memset(idle[:, :], 0.0)
                dve.bn_aggr(mv[:, :], stats[:, :]).then_inc(stat2, 1)

            for k in range(KD):
                dve.tensor_scalar(wo_stage[:, k, :], wo_stage[:, k, :], norm_w, 1.0 - LAMBDA_INIT, ALU.mult,
                                  ALU.mult).then_inc(wo_scaled, 1)
            for k in range(KD):
                dve.wait_ge(wo_hi, k + 1)
                dve.tensor_tensor(wo.lo[:, k, :], wo_stage[:, k, :], wo.hi[:, k, :], ALU.subtract).then_inc(wo_lo, 1)
            tile_pipeline(dve, (1, invert), (4, scalars), (2, rest_of_turned), (5, rest_of_y), (0, mean_squares),
                          (3, add))

        @block.scalar
        def _(act):
            def root(t, par):
                act.wait_ge(summed, t + 1)
                wait_from_first(act, inverted, t)
                act.activation(rms[:, :], mean_sq[:, :], ACT.Sqrt, bias=C.eps[:, 0:1], scale=1.0 / VD
                               ).then_inc(rooted, 1)

            def deviation(t, par):
                act.wait_ge(stat2, t + 1)
                wait_from_first(act, rstd_done, t)
                act.activation(std[:, :], mv[:, 1:2], ACT.Sqrt, bias=C.eps[:, 0:1]).then_inc(std_done, 1)

            def turned_value(t, par):
                act.wait_ge(turned, t + 1)
                wait_from_first(act, projected, t - 1)
                act.activation(normed_T[par].hi[:, :, :], p_nT[:, par, :, :], ACT.Copy).then_inc(turned_hi, 1)

            def squares(t, par):
                wait_from_first(act, summed, t)
                act.activation(square[:, :], attn[:, ds(t * D, D)], ACT.Square).then_inc(squared, 1)

            def normalise(t, par):
                act.wait_ge(offset_done, t + 1)
                act.activation(x[:, ds(t, 1), :].squeeze(1), x[:, ds(t, 1), :].squeeze(1), ACT.Identity, bias=offset[:, 0:1],
                               scale=rstd[:, 0:1]).then_inc(y_done, 1)

            def y_value(t, par):
                act.wait_ge(y_turned, t + 1)
                act.activation(xT.hi[:, :, ds(t * P, P)], p_yT[:, par, :, :], ACT.Copy).then_inc(y_hi, 1)

            for k in range(KD):
                act.wait_ge(wo_scaled, k + 1)
                act.activation(wo.hi[:, k, :], wo_stage[:, k, :], ACT.Copy).then_inc(wo_hi, 1)
            tile_pipeline(act, (1, root), (4, deviation), (2, turned_value), (0, squares), (4, normalise),
                          (5, y_value))

        @block.tensor
        def _(pe):
            def turn(t, par):
                pe.wait_ge(scaled, t + 1)
                wait_from_first(pe, turned_lo, t - 1)
                for i in range(KD):
                    last = pe.transpose(p_nT[:, par, i, :], normed[par][:, i * P:(i + 1) * P], C.ident[:, :])
                last.then_inc(turned, 1)

            def project(t, par):
                pe.wait_ge(turned_lo, t + 1)
                wait_from_first(pe, added, t - 1)
                product(pe, p_o[:, par, :], [(normed_T[par][:, i, :], wo[:, i, :]) for i in range(KD)]
                        ).then_inc(projected, 1)

            def turn_y(t, par):
                pe.wait_ge(y_done, t + 1)
                wait_from_first(pe, y_lo, t - 1)
                for i in range(KD):
                    last = pe.transpose(p_yT[:, par, i, :], x[:, t, i * P:(i + 1) * P], C.ident[:, :])
                last.then_inc(y_turned, 1)

            pe.wait_ge(wo_lo, KD)
            tile_pipeline(pe, (3, project), (1, turn), (4, turn_y), written_out=NT)


def ffn_group_loads(stage, weights, g):
    gate, up, down = weights
    cut = lambda i, **sizes: stage[:, i * GW:(i + 1) * GW].rearrange("p (k n) -> p k n", **sizes)
    return [(cut(0, k=KD), gate[:, :, ds(g * (GT * P), GT * P)]), (cut(1, k=KD), up[:, :, ds(g * (GT * P), GT * P)]),
            (cut(2, k=GT), down[:, ds(g * GT, GT), :])]


def ffn_phase(nc, weights, areas, d_scale, room, scales, x, xT, C, loads):
    name = "ffn"
    with ExitStack() as ctx:
        sb = lambda n, s, d: ctx.enter_context(nc.sbuf_tensor(f"{name}_{n}", s, d))
        ps = lambda n, s, d: ctx.enter_context(nc.psum_tensor(f"{name}_{n}", s, d))
        sem = lambda n: ctx.enter_context(nc.semaphore(f"{name}_{n}"))
        w = [Split(sb(f"w{i}_hi", [P, 3 * GW], F32R), area.taken_by("lo", [P, 3 * GW], F32R))
             for i, area in enumerate(areas)]
        stage = [area.whole[:, :].bitcast(I32) for area in areas]
        real = [area.whole[:, :] for area in areas]
        cut = lambda i, part, **sizes: Split(*(a[:, part * GW:(part + 1) * GW].rearrange("p (k n) -> p k n", **sizes)
                                               for a in (w[i].hi, w[i].lo)))
        wg, wu, wd = ([cut(i, part, k=k) for i in range(2)] for part, k in ((0, KD), (1, KD), (2, GT)))
        h_shape = [P, GROUP_BUFFERS, GT, CH]
        h = Split(room.taken_by("h_hi", h_shape, F32R), room.taken_by("h_lo", h_shape, F32R, H_SIZE))
        h_full = [sb(f"h{i}", [P, CH], F32) for i in range(2)]
        silu = [sb(f"silu{i}", [P, CH], F32) for i in range(2)]
        stats = sb("stats", [P, QPC, 6], F32)
        mv = sb("mv", [P, QPC, 2], F32)
        std, rstd, offset = sb("std", [P, QPC], F32), sb("rstd", [P, QPC], F32), sb("offset", [P, QPC], F32)
        group_scales = [sb(f"group_scales{i}", [P, 2, GT], F32) for i in range(2)]
        p_g = ps("p_g", [P, 2, CH], F32)
        p_u = ps("p_u", [P, 2, CH], F32)
        p_d = ps("p_d", [P, 2, D], F32)
        p_yT = ps("p_yT", [P, 2, KD, P], F32)
        loaded, w_in, w_real, w_scaled = sem("loaded"), sem("w_in"), sem("w_real"), sem("w_scaled")
        w_hi, w_lo, scales_ready = sem("w_hi"), sem("w_lo"), sem("scales_ready")
        g_done, u_done, silu_done = sem("g_done"), sem("u_done"), sem("silu_done")
        h_done, h_hi, h_lo = sem("h_done"), sem("h_hi"), sem("h_lo")
        d_done, added, stat1, stat2 = sem("d_done"), sem("added"), sem("stat1"), sem("stat2")
        std_done, rstd_done, offset_done, y_done = sem("std_done"), sem("rstd_done"), sem("offset_done"), sem("y_done")
        y_turned, y_hi, y_lo = sem("y_turned"), sem("y_hi"), sem("y_lo")
        block = ctx.enter_context(nc.Block())
        PREPARED = [[], [0], [1, 2], []]

        def over_groups(engine, group):
            group(0, 0)
            with engine.Fori(0, (GROUPS - 2) // 2, 1) as j:
                for i in range(2):
                    group(2 * j + 1 + i, 1 - i)
            group(GROUPS - 1, 1)

        @block.sync
        def _(sp):
            def load(g, par):
                wait_from_first(sp, d_done, (g - 1) * (NCH * QPC))
                for dst, src in ffn_group_loads(stage[par], weights, g):
                    sp.dma_start(dst, src).then_inc(w_in, 16)

            for dst, src in loads:
                sp.dma_start(dst, src).then_inc(loaded, 16)
            load(1, 1)
            with sp.Fori(0, GROUPS // 2 - 1, 1) as j:
                for par in range(2):
                    load(2 * j + 2 + par, par)
            sp.wait_ge(loaded, 16 * len(loads))
            sp.wait_ge(w_in, 16 * 3 * (GROUPS - 1))

        @block.gpsimd
        def _(pool):
            def convert(g, par):
                for i in range(3):
                    piece = slice(i * GW, (i + 1) * GW)
                    pool.tensor_scalar(real[par][:, piece], stage[par][:, piece], 1.0, -ZERO_POINT, ALU.mult, ALU.add
                                       ).then_inc(w_real, 1)

            for g in range(GROUPS):
                if g:
                    pool.wait_ge(w_in, 16 * 3 * g)
                convert(g, g % 2)

        @block.tensor
        def _(pe):
            def gate_up(n, c, par):
                for i in range(GT):
                    m = n * GT + i
                    at = slice(c * CH, (c + 1) * CH)
                    wait_from_first(pe, silu_done, m - 1)
                    product(pe, p_g[:, i % 2, :], [(wg[par][:, k, i * P:(i + 1) * P], xT[:, k, at]) for k in range(KD)]
                            ).then_inc(g_done, 1)
                    wait_from_first(pe, h_done, m - 1)
                    product(pe, p_u[:, i % 2, :], [(wu[par][:, k, i * P:(i + 1) * P], xT[:, k, at]) for k in range(KD)]
                            ).then_inc(u_done, 1)

            def down(n, c, par):
                pe.wait_ge(h_lo, GT * n + GT)
                for t in range(QPC):
                    wait_from_first(pe, added, n * QPC + t - 1)
                    product(pe, p_d[:, t % 2, :],
                            [(h[:, c % 2, i, t * P:(t + 1) * P], wd[par][:, i, :]) for i in range(GT)]
                            ).then_inc(d_done, 1)

            def turn(c):
                for t in range(QPC):
                    u = c * QPC + t
                    pe.wait_ge(y_done, u + 1)
                    wait_from_first(pe, y_lo, u - 1)
                    for i in range(KD):
                        last = pe.transpose(p_yT[:, t % 2, i, :], x[:, u, i * P:(i + 1) * P], C.ident[:, :])
                    last.then_inc(y_turned, 1)

            def group(g, par):
                pe.wait_ge(w_lo, 3 * g + 3)
                for c in range(NCH):
                    n = g * NCH + c
                    gate_up(n, c, par)
                    if not (isinstance(g, int) and n == 0):
                        down(n - 1, (c - 1) % NCH, par if c else 1 - par)
                    if isinstance(g, int) and g and c >= 2:
                        turn(c - 2)

            over_groups(pe, group)
            down(GROUPS * NCH - 1, NCH - 1, 1)
            turn(NCH - 2)
            turn(NCH - 1)

        @block.scalar
        def _(act):
            def gate_up(g, c, par):
                n = g * NCH + c
                for i in range(GT):
                    m = n * GT + i
                    act.wait_ge(g_done, m + 1)
                    if c == 0 and i == 0:
                        act.wait_ge(scales_ready, g + 1)
                    wait_from_first(act, h_done, m - 1)
                    act.activation(silu[i % 2][:, :], p_g[:, i % 2, :], ACT.Silu, scale=group_scales[par][:, 0, i:i + 1]
                                   ).then_inc(silu_done, 1)
                    act.wait_ge(h_done, m + 1)
                    wait_from_first(act, d_done, (n - 1) * QPC)
                    act.activation(h.hi[:, c % 2, i, :], h_full[i % 2][:, :], ACT.Copy).then_inc(h_hi, 1)

            def prepare(g, par, i):
                act.wait_ge(w_real, 3 * g + i + 1)
                if i == 2:
                    act.wait_ge(w_scaled, GT * g + GT)
                piece = slice(i * GW, (i + 1) * GW)
                act.activation(w[par].hi[:, piece], real[par][:, piece], ACT.Copy).then_inc(w_hi, 1)

            def deviation(c):
                act.wait_ge(stat2, (c + 1) * QPC)
                wait_from_first(act, rstd_done, c)
                act.activation(std[:, :], mv[:, :, 1], ACT.Sqrt, bias=C.eps[:, 0:1]).then_inc(std_done, 1)
                act.wait_ge(offset_done, c + 1)
                for t in range(QPC):
                    tile = x[:, c * QPC + t, :]
                    act.activation(tile, tile, ACT.Identity, bias=offset[:, t:t + 1], scale=rstd[:, t:t + 1]
                                   ).then_inc(y_done, 1)

            def y_value(c):
                for t in range(QPC):
                    u = c * QPC + t
                    act.wait_ge(y_turned, u + 1)
                    act.activation(xT.hi[:, :, u * P:(u + 1) * P], p_yT[:, t % 2, :, :], ACT.Copy).then_inc(y_hi, 1)

            def group(g, par):
                for c in range(NCH):
                    gate_up(g, c, par)
                    if isinstance(g, int) and g:
                        if c >= 1:
                            deviation(c - 1)
                        if c >= 2:
                            y_value(c - 2)
                    else:
                        for i in PREPARED[c]:
                            wait_from_first(act, d_done, g * NCH * QPC)
                            prepare(g + 1, 1 - par, i)

            for i in range(3):
                prepare(0, 0, i)
            over_groups(act, group)
            deviation(NCH - 1)
            y_value(NCH - 2)
            y_value(NCH - 1)

        @block.vector
        def _(dve):
            def gate_up(g, c, par):
                n = g * NCH + c
                for i in range(GT):
                    m = n * GT + i
                    dve.wait_ge(u_done, m + 1)
                    dve.wait_ge(silu_done, m + 1)
                    wait_from_first(dve, h_lo, m - 1)
                    if c == 0 and i == 0:
                        dve.wait_ge(scales_ready, g + 1)
                    dve.scalar_tensor_tensor(out=h_full[i % 2][:, :], in0=p_u[:, i % 2, :],
                                             scalar=group_scales[par][:, 1, i:i + 1], in1=silu[i % 2][:, :], op0=ALU.mult,
                                             op1=ALU.mult).then_inc(h_done, 1)
                    dve.wait_ge(h_hi, m + 1)
                    dve.tensor_tensor(h.lo[:, c % 2, i, :], h_full[i % 2][:, :], h.hi[:, c % 2, i, :], ALU.subtract
                                      ).then_inc(h_lo, 1)

            def add(n, c, final=False):
                for t in range(QPC):
                    tile = x[:, c * QPC + t, :]
                    dve.wait_ge(d_done, n * QPC + t + 1)
                    wait_from_first(dve, added, n * QPC + t - 1)
                    dve.tensor_tensor(tile, p_d[:, t % 2, :], tile, ALU.add).then_inc(added, 1)
                    if final:
                        u = c * QPC + t
                        dve.wait_ge(added, n * QPC + t + 1)
                        if c:
                            dve.wait_ge(offset_done, c)
                        dve.bn_stats(stats[:, t, :], tile).then_inc(stat1, 1)
                        dve.wait_ge(stat1, u + 1)
                        dve.bn_aggr(mv[:, t, :], stats[:, t, :]).then_inc(stat2, 1)
                if final:
                    dve.wait_ge(std_done, c + 1)
                    wait_from_first(dve, y_done, c * QPC)
                    dve.reciprocal(rstd[:, :], std[:, :]).then_inc(rstd_done, 1)
                    dve.wait_ge(rstd_done, c + 1)
                    dve.scalar_tensor_tensor(out=offset[:, :], in0=mv[:, :, 0], scalar=-1.0, in1=rstd[:, :],
                                             op0=ALU.mult, op1=ALU.mult).then_inc(offset_done, 1)

            def rest_of_y(c):
                for t in range(QPC):
                    u = c * QPC + t
                    at = slice(u * P, (u + 1) * P)
                    dve.wait_ge(y_hi, u + 1)
                    dve.tensor_tensor(xT.lo[:, :, at], p_yT[:, t % 2, :, :], xT.hi[:, :, at], ALU.subtract
                                      ).then_inc(y_lo, 1)

            def prepare(g, par, i):
                if i == 0:
                    wait_from_first(dve, silu_done, (g - 1) * (NCH * GT))
                    wait_from_first(dve, h_done, (g - 1) * (NCH * GT))
                    dve.tensor_copy(group_scales[par][:, :, :], scales[:, :, ds(g * GT, GT)]).then_inc(scales_ready, 1)
                if i == 2:
                    dve.wait_ge(w_real, 3 * g + 3)
                    for k in range(GT):
                        cols = slice(2 * GW + k * D, 2 * GW + (k + 1) * D)
                        dve.tensor_tensor(real[par][:, cols], real[par][:, cols], d_scale[:, :], ALU.mult).then_inc(w_scaled, 1)
                piece = slice(i * GW, (i + 1) * GW)
                dve.wait_ge(w_hi, 3 * g + i + 1)
                dve.tensor_tensor(w[par].lo[:, piece], real[par][:, piece], w[par].hi[:, piece], ALU.subtract
                                  ).then_inc(w_lo, 1)

            def group(g, par):
                last = isinstance(g, int) and g > 0
                for c in range(NCH):
                    n = g * NCH + c
                    gate_up(g, c, par)
                    if not (isinstance(g, int) and n == 0):
                        add(n - 1, (c - 1) % NCH, last and c > 0)
                    if last and c >= 2:
                        rest_of_y(c - 2)
                    if not last:
                        for i in PREPARED[c]:
                            prepare(g + 1, 1 - par, i)

            for i in range(3):
                prepare(0, 0, i)
            over_groups(dve, group)
            add(GROUPS * NCH - 1, NCH - 1, True)
            rest_of_y(NCH - 2)
            rest_of_y(NCH - 1)



def linear_phase(nc, w_area, scale, bias, x, xT, out_d, C):
    name = "lin"
    BANKS = 4
    with ExitStack() as ctx:
        sb = lambda n, s, d: ctx.enter_context(nc.sbuf_tensor(f"{name}_{n}", s, d))
        ps = lambda n, s, d: ctx.enter_context(nc.psum_tensor(f"{name}_{n}", s, d))
        sem = lambda n: ctx.enter_context(nc.semaphore(f"{name}_{n}"))
        w_stage = w_area.whole[:, :].rearrange("p (k n) -> p k n", k=KD)
        w = Split(sb("w_hi", [P, KD, D], F32R), w_area.taken_by("lin_w_lo", [P, KD, D], F32R))
        stats = sb("stats", [P, 6], F32)
        mv = sb("mv", [P, 2], F32)
        idle = sb("idle", [P, 1], F32)
        std, rstd, offset = sb("std", [P, 1], F32), sb("rstd", [P, 1], F32), sb("offset", [P, 1], F32)
        p_o = ps("p_o", [P, 2, D], F32)
        w_scaled, w_hi, w_lo = sem("w_scaled"), sem("w_hi"), sem("w_lo")
        o_done, biased, added, stat1, stat2, std_done, rstd_done, offset_done, y_done = (
            sem("o_done"), sem("biased"), sem("added"), sem("stat1"), sem("stat2"), sem("std_done"),
            sem("rstd_done"), sem("offset_done"), sem("y_done"))
        stored = sem("stored")
        block = ctx.enter_context(nc.Block())
        tile = lambda t: x[:, ds(t, 1), :].squeeze(1)

        @block.sync
        def _(sp):
            for t in range(NT):
                sp.wait_ge(y_done, t + 1)
                sp.dma_start(out_d[t * P:(t + 1) * P, :], x[:, t, :]).then_inc(stored, 16)
            sp.wait_ge(stored, 16 * NT)

        @block.gpsimd
        def _(pool):
            with pool.Fori(0, NT, 1) as t:
                pool.tensor_tensor(tile(t), tile(t), bias, ALU.add).then_inc(biased, 1)

        @block.tensor
        def _(pe):
            def project(t, par):
                wait_from_first(pe, added, t - 1)
                product(pe, p_o[:, par, :], [(xT[:, i, t * P:(t + 1) * P], w[:, i, :]) for i in range(KD)]
                        ).then_inc(o_done, 1)

            pe.wait_ge(w_lo, KD)
            tile_pipeline(pe, (0, project), written_out=NT)

        @block.scalar
        def _(act):
            def deviation(t, par):
                act.wait_ge(stat2, t + 1)
                wait_from_first(act, rstd_done, t)
                act.activation(std[:, :], mv[:, 1:2], ACT.Sqrt, bias=C.eps[:, 0:1]).then_inc(std_done, 1)

            def normalise(t, par):
                act.wait_ge(offset_done, t + 1)
                act.activation(tile(t), tile(t), ACT.Identity, bias=offset[:, 0:1], scale=rstd[:, 0:1]
                               ).then_inc(y_done, 1)

            for k in range(KD):
                act.wait_ge(w_scaled, k + 1)
                act.activation(w.hi[:, k, :], w_stage[:, k, :], ACT.Copy).then_inc(w_hi, 1)
            tile_pipeline(act, (1, deviation), (1, normalise))

        @block.vector
        def _(dve):
            def add(t, par):
                dve.wait_ge(o_done, t + 1)
                dve.wait_ge(biased, t + 1)
                dve.tensor_tensor(tile(t), p_o[:, par, :], tile(t), ALU.add).then_inc(added, 1)
                dve.wait_ge(added, t + 1)
                dve.memset(idle[:, :], 0.0)
                dve.bn_stats(stats[:, :], tile(t)).then_inc(stat1, 1)
                dve.wait_ge(stat1, t + 1)
                wait_from_first(dve, offset_done, t)
                dve.memset(idle[:, :], 0.0)
                dve.bn_aggr(mv[:, :], stats[:, :]).then_inc(stat2, 1)

            def scalars(t, par):
                dve.wait_ge(std_done, t + 1)
                wait_from_first(dve, y_done, t)
                dve.reciprocal(rstd[:, :], std[:, :]).then_inc(rstd_done, 1)
                dve.wait_ge(rstd_done, t + 1)
                dve.scalar_tensor_tensor(out=offset[:, :], in0=mv[:, 0:1], scalar=-1.0, in1=rstd[:, :],
                                         op0=ALU.mult, op1=ALU.mult).then_inc(offset_done, 1)

            for k in range(KD):
                dve.tensor_tensor(w_stage[:, k, :], w_stage[:, k, :], scale, ALU.mult).then_inc(w_scaled, 1)
            for k in range(KD):
                dve.wait_ge(w_hi, k + 1)
                dve.tensor_tensor(w.lo[:, k, :], w_stage[:, k, :], w.hi[:, k, :], ALU.subtract).then_inc(w_lo, 1)
            tile_pipeline(dve, (1, scalars), (0, add))


class Constants:
    pass


def setup_phase(nc, C, lambdas, neg_lambda, norm_ws, norm_w, rows):
    with ExitStack() as ctx:
        sb = lambda n, s, d: ctx.enter_context(nc.sbuf_tensor(f"set_{n}", s, d))
        sem = lambda n: ctx.enter_context(nc.semaphore(f"set_{n}"))
        vec = sb("vec", [P, 2, 2, 2, HD], F32)
        prod = sb("prod", [P, 2, 2, HD], F32)
        dots = sb("dots", [P, 2, 2], F32)
        lam = sb("lam", [P, 2, 2], F32)
        v_in, rest_in = sem("v_in"), sem("rest_in")
        blank, products, exps = sem("blank"), sem("products"), sem("exps")
        block = ctx.enter_context(nc.Block())

        @block.sync
        def _(sp):
            for l in range(2):
                for e in range(2):
                    for f in range(2):
                        sp.dma_start(vec[:, l, e, f, :], lambdas[l][2 * e + f].partition_broadcast(P)
                                     ).then_inc(v_in, 16)
                for i in range(P // VD):
                    sp.dma_start(norm_w[i * VD:(i + 1) * VD, l:l + 1], norm_ws[l].unsqueeze(1)).then_inc(rest_in, 16)
            for dst, src in rows:
                sp.dma_start(dst, src).then_inc(rest_in, 16)
            sp.wait_ge(rest_in, 16 * (len(rows) + 2 * (P // VD)))

        @block.gpsimd
        def _(pool):
            for t in (C.ident, C.ident_b, C.mask_qk, C.mask_kq):
                pool.memset(t[:, :], 0.0).then_inc(blank, 1)
            pool.memset(C.eps[:, :], EPS).then_inc(blank, 1)
            pool.wait_ge(blank, 5)
            for t in (C.ident, C.ident_b):
                pool.affine_select(out=t[:, :], in_=t[:, :], compare_op=ALU.not_equal, fill=1.0, base=0,
                                   pattern=[[-1, P]], channel_multiplier=1)
            pool.affine_select(out=C.mask_qk[:, :], in_=C.mask_qk[:, :], compare_op=ALU.is_ge, fill=MASKED, base=0,
                               pattern=[[-1, P]], channel_multiplier=1)
            pool.affine_select(out=C.mask_kq[:, :], in_=C.mask_kq[:, :], compare_op=ALU.is_ge, fill=MASKED, base=0,
                               pattern=[[1, P]], channel_multiplier=-1)

        @block.vector
        def _(dve):
            dve.wait_ge(v_in, 16 * 8)
            dve.tensor_tensor(prod[:, :, :, :], vec[:, :, :, 0, :], vec[:, :, :, 1, :], ALU.mult).then_inc(products, 1)
            dve.wait_ge(products, 1)
            dve.tensor_reduce(dots[:, :, :], prod[:, :, :, :], AX.X, ALU.add).then_inc(products, 1)
            dve.wait_ge(exps, 1)
            for l in range(2):
                dve.scalar_tensor_tensor(out=neg_lambda[l][:, :], in0=lam[:, l, 1:2], scalar=-LAMBDA_INIT,
                                         in1=lam[:, l, 0:1], op0=ALU.add, op1=ALU.subtract)

        @block.scalar
        def _(act):
            act.wait_ge(products, 2)
            act.activation(lam[:, :, :], dots[:, :, :], ACT.Exp).then_inc(exps, 1)


def program(nc, A, out):
    dram = lambda n, s, d: nc.dram_tensor(n, s, d, kind="Internal").ap()
    q_stack = [dram(f"q_stack{l}", (B * D // HD, SROWS, T), BF16) for l in range(2)]
    k_stack = [dram(f"k_stack{l}", (B * L.k_dims // HD, SROWS, T), BF16) for l, L in enumerate((L0, L1))]
    x0 = A["L0_attn_x"].rearrange("b t d -> (b t) d")
    out = out.rearrange("b t d -> (b t) d")
    with ExitStack() as ctx:
        sb = lambda n, s, d: ctx.enter_context(nc.sbuf_tensor(n, s, d))
        C = Constants()
        C.ident = sb("ident", [P, P], F32)
        C.ident_b = sb("ident_b", [P, P], BF16)
        C.mask_qk = sb("mask_qk", [P, P], BF16)
        C.mask_kq = sb("mask_kq", [P, P], BF16)
        C.eps = sb("eps", [P, 1], F32)
        neg_lambda = [sb(f"neg_lambda{l}", [P, 1], F32) for l in range(2)]
        norm_w = sb("norm_w", [P, 2], F32)
        scales = sb("scales", [P, 2, FT], F32)
        setup_phase(
            nc, C, [[A[f"L{l}_attn_lambda_{x}"] for x in ("q1", "k1", "q2", "k2")] for l in range(2)], neg_lambda,
            [A["L0_attn_subln_w"], A["L1_attn_ln_w"]], norm_w,
            [(scales[:, 0, :], A["L0_ffn_gate_scale_T"]),
             (scales[:, 1, :], A["L0_ffn_up_scale_T"])])
        x = sb("x", [P, NT * D], F32)
        x_tiles = x[:, :].rearrange("p (t c) -> p t c", c=D)
        xT = Split(sb("xT_hi", [P, KD, TOK], F32R), sb("xT_lo", [P, KD, TOK], F32R))
        attn_area = Area(ctx, nc, "attn", NT * D)
        attn = attn_area.whole
        wo_area = Area(ctx, nc, "wo", KD * D)
        wo_stage = wo_area.whole[:, :].rearrange("p (k n) -> p k n", k=KD)
        by_k = lambda a: a.rearrange("(k p) n -> p k n", p=P)
        with ExitStack() as layer:
            v_sb = layer.enter_context(nc.sbuf_tensor("v_all0", [P, NT * L0.v_dims], F32))
            qkv_phase(nc, L0, xT, q_stack[0], k_stack[0], v_sb, attn_area, 0,
                      [A[f"L0_attn_{w}_T"] for w in ("wq", "wk", "wv")],
                      x[:, :].rearrange("p (k n) -> p k n", k=KD), A["x_T"])
            attention_phase(nc, L0, q_stack[0], k_stack[0], v_sb, attn, neg_lambda[0][:, 0:1], C,
                            [(x_tiles, x0.rearrange("(t p) d -> p t d", p=P)), (wo_stage, by_k(A["L0_attn_wo_T"]))])
        with ExitStack() as layer:
            ffn_areas = [Area(layer, nc, f"ffn_w{i}", 3 * GW) for i in range(2)]
            d_scale = layer.enter_context(nc.sbuf_tensor("d_scale", [P, D], F32))
            w_gud = [by_k(A[f"L0_ffn_{w}_w_T"]) for w in ("gate", "up", "down")]
            loads = [(d_scale[:, :], A["L0_ffn_down_scale"].partition_broadcast(P))]
            mix_phase(nc, "mix0", attn, wo_area, norm_w[:, 0:1], x_tiles, xT, C,
                      loads + ffn_group_loads(ffn_areas[0].whole[:, :].bitcast(I32), w_gud, 0))
            qkv1_loads, w_at = [], 2 * H_SIZE
            for w in ("Wq", "Wk", "Wv"):
                src = by_k(A[f"L1_attn_{w}_T"])
                width = KD * src.shape[2]
                qkv1_loads.append((attn[:, w_at:w_at + width].rearrange("p (k n) -> p k n", k=KD), src))
                w_at += width
            ffn_phase(nc, w_gud, ffn_areas, d_scale, attn_area, scales, x_tiles, xT, C, qkv1_loads)
        with ExitStack() as layer:
            v_sb = layer.enter_context(nc.sbuf_tensor("v_all1", [P, NT * L1.v_dims], F32))
            qkv_phase(nc, L1, xT, q_stack[1], k_stack[1], v_sb, attn_area, 2 * H_SIZE)
            attention_phase(nc, L1, q_stack[1], k_stack[1], v_sb, attn, neg_lambda[1][:, 0:1], C,
                            [(wo_stage, by_k(A["L1_attn_Wo_T"]))])
            lin_area = Area(layer, nc, "lin_w", KD * D)
            lin_rows = layer.enter_context(nc.sbuf_tensor("lin_rows", [P, 2, D], F32))
            mix_phase(nc, "mix1", attn, wo_area, norm_w[:, 1:2], x_tiles, xT, C,
                      [(lin_area.whole[:, :].rearrange("p (k n) -> p k n", k=KD), by_k(A["L1_ffn_weight_T"])),
                       (lin_rows[:, 0, :], A["L1_ffn_scale_weight"].partition_broadcast(P)),
                       (lin_rows[:, 1, :], A["L1_ffn_bias"].partition_broadcast(P))])
            linear_phase(nc, lin_area, lin_rows[:, 0, :], lin_rows[:, 1, :], x_tiles, xT, out, C)


TRANSPOSED = ["L0_attn_wq", "L0_attn_wk", "L0_attn_wv", "L0_attn_wo", "L0_ffn_gate_w", "L0_ffn_up_w",
              "L0_ffn_down_w", "L1_attn_Wq", "L1_attn_Wk", "L1_attn_Wv", "L1_attn_Wo", "L1_ffn_weight"]
PLAIN = ["L0_attn_x", "L0_attn_lambda_q1", "L0_attn_lambda_k1", "L0_attn_lambda_q2", "L0_attn_lambda_k2",
         "L0_attn_subln_w", "L0_ffn_down_scale", "L1_attn_lambda_q1",
         "L1_attn_lambda_k1", "L1_attn_lambda_q2", "L1_attn_lambda_k2", "L1_attn_ln_w", "L1_ffn_scale_weight",
         "L1_ffn_bias"]


def kernel(**inputs):
    import numpy as np
    import concourse.bacc as bacc
    from concourse.bass_utils import run_bass_kernel_spmd

    arrays = {name: np.ascontiguousarray(inputs[name]) for name in PLAIN}
    for name in TRANSPOSED:
        arrays[name + "_T"] = np.ascontiguousarray(np.asarray(inputs[name]).T)
    for name in ("L0_ffn_gate_scale", "L0_ffn_up_scale"):
        arrays[name + "_T"] = np.ascontiguousarray(np.asarray(inputs[name]).reshape(FT, P).T)
    x = np.asarray(inputs["L0_attn_x"])
    arrays["x_T"] = np.ascontiguousarray(x.reshape(-1, x.shape[-1]).T)
    nc = bacc.Bacc("TRN2", target_bir_lowering=False, num_devices=1)
    A = {name: nc.dram_tensor(f"in_{name}", a.shape, mybir.dt.from_np(a.dtype), kind="ExternalInput").ap()
         for name, a in arrays.items()}
    out = nc.dram_tensor("out", (B, T, D), F32, kind="ExternalOutput").ap()
    program(nc, A, out)
    r = run_bass_kernel_spmd(nc, [{f"in_{name}": a for name, a in arrays.items()}], core_ids=[0])
    return r.results[0]["out"]
```

```python
import math
from contextlib import ExitStack

import concourse.bass as bass
from concourse import mybir

F32 = mybir.dt.float32
BF16 = mybir.dt.bfloat16
I32 = mybir.dt.int32
F32R = mybir.dt.float32r
ALU = mybir.AluOpType
ACT = mybir.ActivationFunctionType
AX = mybir.AxisListType
ds = bass.ds

P = 128
B, T, D = 2, 1024, 512
TOK = B * T
KD = D // P
CH = 512
NCH = TOK // CH
NT = TOK // P
HD = 16
VD = 2 * HD
NH = D // VD
KV_HEADS = 4
PARTS = 3
FFN = 2048
FT = FFN // P
Q_PART = [0, 0, 0, 1, 1, 2]
SROWS = len(Q_PART) * HD
STACK_LOADS = len(Q_PART) + PARTS
FROWS = SROWS + 2
KT = T // P
QC = T // CH
QPC = CH // P
HEADS = B * NH
SBUF_ALIGN = 32
GT = 2
GROUPS = FT // GT
GROUP_BUFFERS = 2
H_SIZE = GROUP_BUFFERS * GT * CH
WRITTEN_OUT = 6
GW = KD * GT * P
EPS = 1e-5
LAMBDA_INIT = 0.8 - 0.6 * math.exp(-0.3 * 12)
MASKED = -1e30
ZERO_POINT = 128.0
PRING = 4
FILL = 2
TURN_LAG = 1
RING = 3
AHEAD = PRING
UNIT_FIXED = 75


class Layer:

    def __init__(self, name, k_dims, v_dims, causal, max_begins, max_ends, shift_turned):
        self.max_begins, self.max_ends, self.shift_turned = max_begins, max_ends, shift_turned
        self.name, self.k_dims, self.v_dims, self.causal = name, k_dims, v_dims, causal
        self.pair_stacks = 4 if k_dims == D else 1
        self.steps = [(qc, kt, max(0, kt - QPC * qc) * P if causal else 0)
                      for qc in range(QC) for kt in range(QPC * (qc + 1) if causal else KT)]
        self.units = []
        for sub in range(2):
            for qt in range(KT):
                keys = (qt + 1) * P if causal else T
                for kc in range(-(-keys // CH)):
                    self.units.append((sub, qt, kc, min(CH, keys - kc * CH)))
        assert len(self.steps) % PRING == 0 and len(self.units) % 2 == 0
        self.qc_last = [max(s for s, x in enumerate(self.steps) if x[0] == qc) for qc in range(QC)]
        self.ring_first = len(self.units) + 1
        self.ring_head = len(self.units) + 1 + QC
        self.orders = {has_next: self.order(has_next) for has_next in (False, True)}

    def order(self, has_next):
        S = len(self.steps)
        items = []
        for s in range(1, S + 1):
            if s < S or has_next:
                items.append(("score", s, 2 * (CH - self.steps[s % S][2])))
            if s == TURN_LAG:
                items += [("fill", FILL, 0), ("turn", QC - 1, 0)]
            for qc in range(QC - 1):
                if s == self.qc_last[qc] + 1 + TURN_LAG:
                    items += [("fill", FILL, 0), ("turn", qc, 0)]
            items.append(("sum", s - 1, 4 * (CH - self.steps[s - 1][2])))
        if not has_next:
            return [x[:2] for x in items if x[0] != "fill"]
        work = sum(x[2] for x in items)
        cost = [keys + UNIT_FIXED for _, _, _, keys in self.units]
        out, done, u, spent, turned = [], 0, 0, 0, False
        for what, i, weight in items:
            if (what, i) == ("score", S) and not turned:
                out.append(("turn_shift", 0))
                turned = True
            if what == "fill":
                for _ in range(min(i, len(cost) - u)):
                    out.append(("max", u))
                    spent += cost[u]
                    u += 1
                continue
            out.append((what, i))
            done += weight
            window = self.max_ends - self.max_begins
            while u < len(cost) and done >= work * (self.max_begins + window * spent / sum(cost)):
                out.append(("max", u))
                spent += cost[u]
                u += 1
            if u == len(cost) and not turned and done >= work * self.shift_turned:
                out.append(("turn_shift", 0))
                turned = True
        assert u == len(cost) and turned
        return out

    def v_column(self, n):
        return (n % NH) * VD if self.v_dims == D else ((n % NH) // (NH // KV_HEADS)) * VD

    def k_stack(self, h, sub):
        return 2 * (h % 2) + sub if self.pair_stacks == 4 else 0


L0 = Layer("l0", D, D, False, 0.03, 0.73, 0.77)
L1 = Layer("l1", D // 4, D // 4, True, 0.0, 0.6, 0.7)


class Area:

    def __init__(self, ctx, nc, name, size):
        self.nc, self.name = nc, name
        self.offset = -(-nc.sbuf_base // SBUF_ALIGN) * SBUF_ALIGN
        self.whole = ctx.enter_context(nc.sbuf_tensor(name, [P, size], F32))

    def taken_by(self, user, shape, dtype, at=0):
        return self.nc.alloc_sbuf_tensor_at(f"{self.name}_{user}", shape, dtype, offset=self.offset + 4 * at)


class Split:

    def __init__(self, hi, lo):
        self.hi, self.lo = hi, lo

    def __getitem__(self, at):
        return Split(self.hi[at], self.lo[at])


def product(pe, out, terms, start=True, stop=True):
    passes = [x for lhs, rhs in terms for x in ((lhs.hi, rhs.hi), (lhs.hi, rhs.lo), (lhs.lo, rhs.hi))]
    for i, (lhs, rhs) in enumerate(passes):
        last = pe.matmul(out, lhs, rhs, start=start and i == 0, stop=stop and i == len(passes) - 1)
    return last


def wait_from_first(engine, semaphore, count):
    if not isinstance(count, int) or count > 0:
        engine.wait_ge(semaphore, count)


def credit(engine, *semaphores):
    for semaphore in semaphores:
        engine.sem_inc(semaphore, AHEAD)


def qkv_phase(nc, L, xT, q_parts_d, k_parts_d, v_sb, w_area, w_first, w_d=None, x_stage=None, xT_d=None):
    widths = [D, L.k_dims, L.v_dims]
    q_tiles, k_tiles = D // P, L.k_dims // P
    MT = q_tiles + k_tiles
    first_load = xT_d is not None
    QK_BANKS = math.gcd(2 * MT, 4)
    with ExitStack() as ctx:
        sb = lambda n, s, d: ctx.enter_context(nc.sbuf_tensor(f"{L.name}_{n}", s, d))
        ps = lambda n, s, d: ctx.enter_context(nc.psum_tensor(f"{L.name}_{n}", s, d))
        sem = lambda n: ctx.enter_context(nc.semaphore(f"{L.name}_{n}"))
        w_at = [w_first + KD * sum(widths[:i]) for i in range(3)]
        staged = [w_area.whole[:, at:at + KD * x].rearrange("p (k n) -> p k n", k=KD) for at, x in zip(w_at, widths)]
        w = [Split(sb(f"w{n}_hi", [P, KD, x], F32R), w_area.taken_by(f"{L.name}_w{n}_lo", [P, KD, x], F32R, at))
             for n, at, x in zip("qkv", w_at, widths)]
        part = [[sb(f"part{r}{i}", [P, CH], BF16) for i in range(PARTS)] for r in range(2)]
        rest = [sb(f"rest{r}", [P, CH], F32) for r in range(2)]
        p_qk = ps("p_qk", [P, QK_BANKS, CH], F32)
        p_v = ps("p_v", [P, QPC, CH], F32)
        w_in = x_in = 3 * [None]
        if first_load:
            w_in, x_in = [None, sem("w_in1"), sem("w_in2")], [None] + [sem(f"x_in{c}") for c in range(1, NCH)]
            pool_hi, pool_lo = sem("pool_hi"), sem("pool_lo")
        split_hi, split_lo = sem("split_hi"), sem("split_lo")
        qk_done, v_done, v_kept = sem("qk_done"), sem("v_done"), sem("v_kept")
        part1, rest1, part2, part3 = sem("part1"), sem("rest1"), sem("part2"), sem("part3")
        stored = [sem("stored0"), sem("stored1")]
        block = ctx.enter_context(nc.Block())
        jobs = [(staged[0][:, k, :], w[0][:, k, :], None) for k in range(KD)]
        if first_load:
            jobs += [(x_stage[:, k, 0:CH], xT[:, k, 0:CH], None) for k in range(KD)]
        qk_jobs = len(jobs)
        jobs += [(staged[1][:, k, :], w[1][:, k, :], w_in[1]) for k in range(KD)]
        jobs += [(staged[2][:, k, :], w[2][:, k, :], w_in[2]) for k in range(KD)]

        @block.sync
        def _(sp):
            def load_w(i):
                sp.dma_start(staged[i], w_d[i].rearrange("(k p) n -> p k n", p=P)).then_inc(w_in[i], 16)

            def load_x(c):
                cols = slice(c * CH, (c + 1) * CH)
                sp.dma_start(x_stage[:, :, cols], xT_d.rearrange("(k p) n -> p k n", p=P)[:, :, cols]
                             ).then_inc(x_in[c], 16)

            credit(sp, *stored)
            if first_load:
                load_w(1)
                load_w(2)
                for c in range(1, NCH):
                    load_x(c)
            with sp.Fori(0, NCH // 2, 1) as j:
                for par in range(2):
                    for m in range(MT):
                        r = (par * MT + m) % 2
                        is_q = m < q_tiles
                        dst = q_parts_d if is_q else k_parts_d
                        bat, tin = j, par * CH
                        sp.wait_ge(part3, AHEAD + (j * 2 + par) * MT + m + 1)
                        subs = P // HD
                        mm = m if is_q else m - q_tiles
                        per_batch = (D if is_q else L.k_dims) // HD
                        for i in range(PARTS):
                            out = dst[ds(bat * per_batch + mm * subs, subs), i * HD:(i + 1) * HD, tin:tin + CH]
                            sp.dma_start(out, part[r][i][:, :]).then_inc(stored[r], 16)
            for r in range(2):
                sp.wait_ge(stored[r], AHEAD + 16 * PARTS * NCH * MT // 2)

        @block.gpsimd
        def _(pool):
            if first_load:
                for c in range(1, NCH):
                    pool.wait_ge(x_in[c], 16)
                    for k in range(KD):
                        at = (slice(None), k, slice(c * CH, (c + 1) * CH))
                        pool.tensor_copy(xT.hi[at], x_stage[at]).then_inc(pool_hi, 1)
                        pool.wait_ge(pool_hi, (c - 1) * KD + k + 1)
                        pool.tensor_tensor(xT.lo[at], x_stage[at], xT.hi[at], ALU.subtract).then_inc(pool_lo, 1)

        @block.tensor
        def _(pe):
            pe.wait_ge(split_lo, qk_jobs)
            for c in range(NCH):
                if first_load and c:
                    pe.wait_ge(pool_lo, KD * c)
                for m in range(MT):
                    u = c * MT + m
                    if u >= QK_BANKS:
                        pe.wait_ge(rest1, AHEAD + u + 1 - QK_BANKS)
                    if u == q_tiles:
                        pe.wait_ge(split_lo, qk_jobs + KD)
                    lhs, mm = (w[0], m) if m < q_tiles else (w[1], m - q_tiles)
                    product(pe, p_qk[:, u % QK_BANKS, :],
                            [(lhs[:, k, mm * P:(mm + 1) * P], xT[:, k, c * CH:(c + 1) * CH]) for k in range(KD)]
                            ).then_inc(qk_done, 1)
                if c == 0:
                    pe.wait_ge(split_lo, qk_jobs + 2 * KD)
                for t in range(c * QPC, (c + 1) * QPC):
                    if t >= QPC:
                        pe.wait_ge(v_kept, AHEAD + t + 1 - QPC)
                    product(pe, p_v[:, t % QPC, 0:L.v_dims],
                            [(xT[:, k, t * P:(t + 1) * P], w[2][:, k, :]) for k in range(KD)]).then_inc(v_done, 1)

        @block.scalar
        def _(act):
            credit(act, v_kept)
            for i, (src, to, came) in enumerate(jobs):
                if came:
                    act.wait_ge(came, 16)
                act.activation(to.hi, src, ACT.Copy).then_inc(split_hi, 1)
            with act.Fori(0, NCH // 2, 1) as j:
                for u in range(2 * MT):
                    n = j * (2 * MT) + u
                    r = u % 2
                    act.wait_ge(qk_done, n + 1)
                    act.wait_ge(stored[r], AHEAD + 16 * PARTS * (j * MT + u // 2))
                    act.activation(part[r][0][:, :], p_qk[:, u % QK_BANKS, :], ACT.Copy).then_inc(part1, 1)
                    act.wait_ge(rest1, AHEAD + n + 1)
                    act.activation(part[r][1][:, :], rest[r][:, :], ACT.Copy).then_inc(part2, 1)
                    if u % MT == MT - 1:
                        for t in range(QPC):
                            k = (u // MT) * QPC + t
                            act.wait_ge(v_done, j * (2 * QPC) + k + 1)
                            act.activation(v_sb[:, ds((j * (2 * QPC) + k) * L.v_dims, L.v_dims)],
                                           p_v[:, k % QPC, 0:L.v_dims], ACT.Copy).then_inc(v_kept, 1)

        @block.vector
        def _(dve):
            credit(dve, rest1, part3)
            for i, (src, to, _) in enumerate(jobs):
                dve.wait_ge(split_hi, i + 1)
                dve.tensor_tensor(to.lo, src, to.hi, ALU.subtract).then_inc(split_lo, 1)
            with dve.Fori(0, NCH // 2, 1) as j:
                for u in range(2 * MT):
                    n = j * (2 * MT) + u
                    r = u % 2
                    dve.wait_ge(part1, n + 1)
                    dve.wait_ge(part3, AHEAD + n - 1)
                    dve.tensor_tensor(rest[r][:, :], p_qk[:, u % QK_BANKS, :], part[r][0][:, :],
                                      ALU.subtract).then_inc(rest1, 1)
                    dve.wait_ge(part2, n + 1)
                    dve.tensor_tensor(part[r][2][:, :], rest[r][:, :], part[r][1][:, :],
                                      ALU.subtract).then_inc(part3, 1)


def attention_phase(nc, L, q_parts_d, k_parts_d, v_sb, attn, neg_lambda, C, rooms, loads=()):
    S, U = len(L.steps), len(L.units)
    KS = L.pair_stacks
    with ExitStack() as ctx:
        sb = lambda n, s, d: ctx.enter_context(nc.sbuf_tensor(f"{L.name}_{n}", s, d))
        ps = lambda n, s, d: ctx.enter_context(nc.psum_tensor(f"{L.name}_{n}", s, d))
        sem = lambda n: ctx.enter_context(nc.semaphore(f"{L.name}_{n}"))
        q = [rooms[0].taken_by(f"{L.name}_q{i}", [P, 4, T], BF16, i * 2 * T) for i in range(2)]
        k = [rooms[1].taken_by(f"{L.name}_k{i}", [P, KS, T], BF16, i * 2 * T) for i in range(2)]
        v = [sb(f"v{i}", [P, KT, VD], F32) for i in range(2)]
        prob = [sb(f"prob{i}", [P, 2, CH], F32) for i in range(PRING)]
        ones = sb("ones", [P, VD], F32)
        maxima = sb("maxima", [P, 2 * KT, 2], F32)
        shift = sb("shift", [P, 2 * KT], F32)
        shift_parts = sb("shift_parts", [P, 2, 2 * KT], BF16)
        shift_rows = sb("shift_rows", [4 * KT, P], BF16)
        sums = sb("sums", [P, CH], F32)
        recip = sb("recip", [P, QPC, 2], F32)
        half = sb("half", [P, 2, QPC, VD], F32)
        p_score = ps("p_score", [P, 2, 2, CH], F32)
        p_ring = ps("p_ring", [P, RING, CH], F32)
        p_out = ps("p_out", [P, CH], F32)
        q_in = [sem("q_in0"), sem("q_in1")]
        shift_in = [sem("shift_in0"), sem("shift_in1")]
        ready = sem("ready")
        scored, exped, summed, out_copied = sem("scored"), sem("exped"), sem("summed"), sem("out_copied")
        filled, freed = sem("filled"), sem("freed")
        shift_made, shift_rest, shift_copied = sem("shift_made"), sem("shift_rest"), sem("shift_copied")
        out_recip, out_scaled, out_kept = sem("out_recip"), sem("out_scaled"), sem("out_kept")
        v_in, loaded = sem("v_in"), sem("loaded")
        block = ctx.enter_context(nc.Block())

        def ring_items(n, has_next=True):
            at = 0
            for what, i in L.orders[has_next]:
                if what in ("max", "turn", "turn_shift"):
                    yield what, i, at
                    at += 1
                else:
                    yield what, i, None
            assert at == (L.ring_head if has_next else QC)

        def ring_count(n, at):
            return at if n is None else L.ring_first + n * L.ring_head + at

        @block.sync
        def _(sp):
            def load(p, pp, first=False):
                if not first:
                    sp.wait_ge(scored, (p - 1) * (2 * S))
                for at, kept in enumerate(Q_PART):
                    sp.dma_start(q[pp][at * HD:(at + 1) * HD, :, :],
                                 q_parts_d[ds(4 * p, 4), kept * HD:(kept + 1) * HD, :].rearrange("s r t -> r s t")
                                 ).then_inc(q_in[pp], 16)
                at = 0
                for parts in range(PARTS, 0, -1):
                    rows = parts * HD
                    sp.dma_start(k[pp][at:at + rows, :, :],
                                 k_parts_d[ds(p * KS, KS), 0:rows, :].rearrange("s r t -> r s t")
                                 ).then_inc(q_in[pp], 16)
                    at += rows

            def shift_row(n, h):
                sp.wait_ge(shift_copied, n + 1)
                for i in range(2):
                    sp.dma_start(q[h // 2][SROWS + i:SROWS + i + 1, 2 * (h % 2):2 * (h % 2) + 2, :],
                                 shift_rows[2 * KT * i:2 * KT * (i + 1), :]).then_inc(shift_in[h % 2], 16)

            load(0, 0, first=True)
            shift_row(0, 0)
            load(1, 1, first=True)
            with sp.Fori(0, HEADS // 4 - 1, 1) as j:
                for pp in range(2):
                    shift_row(4 * j + 2 * pp + 1, 2 * pp + 1)
                    shift_row(4 * j + 2 * pp + 2, (2 * pp + 2) % 4)
                    load(2 * j + 2 + pp, pp)
            for n in range(HEADS - 3, HEADS):
                shift_row(n, n % 4)
            for par in range(2):
                sp.wait_ge(shift_in[par], 32 * HEADS // 2)

        @block.gpsimd
        def _(pool):
            def take_v(n, par):
                tiles = v_sb[:, 0:NT * L.v_dims].rearrange("p (t c) -> p t c", c=L.v_dims)
                pool.tensor_copy(v[par][:, :, :], tiles[:, ds((n // NH) * KT, KT), ds(L.v_column(n), VD)]
                                 ).then_inc(v_in, 1)

            for par in range(2):
                take_v(par, par)
            pool.wait_ge(summed, AHEAD + S)
            for dst, src in loads:
                pool.dma_start(dst, src).then_inc(loaded, 16)
            with pool.Fori(0, HEADS // 2 - 1, 1) as j:
                for par in range(2):
                    pool.wait_ge(summed, AHEAD + (2 * j + par + 1) * S)
                    take_v(2 * j + 2 + par, par)
            pool.wait_ge(loaded, 16 * len(loads))

        @block.tensor
        def _(pe):
            credit(pe, summed)

            def take_bank(count, at):
                pe.wait_ge(freed, AHEAD + count - at + max(at - RING + 1, 0))

            def max_unit(n, h, u, count, at):
                sub, qt, kc, keys = L.units[u]
                bank = p_ring[:, at % RING, :]
                if u == 0:
                    pe.wait_ge(q_in[h // 2], 16 * STACK_LOADS * (n // 4 + 1))
                take_bank(count, at)
                diagonal = L.causal and kc == qt // QPC
                last = pe.matmul(bank[:, 0:keys], q[h // 2][0:SROWS, 2 * (h % 2) + sub, qt * P:(qt + 1) * P],
                                 k[h // 2][0:SROWS, L.k_stack(h, sub), kc * CH:kc * CH + keys], start=True,
                                 stop=not diagonal)
                if diagonal:
                    last = pe.matmul(bank[:, keys - P:keys], C.ident_b[:, :], C.mask_qk[:, :], start=False, stop=True)
                last.then_inc(filled, 1)

            def turn_shift(n, count, at):
                pe.wait_ge(shift_rest, n + 1)
                take_bank(count, at)
                pe.transpose(p_ring[0:4 * KT, at % RING, 0:P // 2].bitcast(BF16),
                             shift_parts[:, :, :].rearrange("p a b -> p (a b)"), C.ident_b[:, :]).then_inc(filled, 1)

            def score(n, h, s):
                qc, kt, off = L.steps[s]
                if s == 0:
                    pe.wait_ge(shift_in[h % 2], 32 * (n // 2) + 32)
                pe.wait_ge(exped, AHEAD + n * S + s - 1)
                for sub in range(2):
                    diagonal = L.causal and kt >= QPC * qc
                    last = pe.matmul(p_score[:, s % 2, sub, off:CH],
                                     k[h // 2][0:FROWS, L.k_stack(h, sub), kt * P:(kt + 1) * P],
                                     q[h // 2][0:FROWS, 2 * (h % 2) + sub, qc * CH + off:(qc + 1) * CH],
                                     start=True, stop=not diagonal)
                    if diagonal:
                        last = pe.matmul(p_score[:, s % 2, sub, off:off + P], C.ident_b[:, :], C.mask_kq[:, :],
                                         start=False, stop=True)
                last.then_inc(scored, 1)

            def sum_up(n, h, s):
                qc, kt, off = L.steps[s]
                if s == 0:
                    pe.wait_ge(v_in, n + 1)
                first, final = kt == 0, s == L.qc_last[qc]
                if first:
                    pe.wait_ge(out_copied, AHEAD + QC * n + qc)
                pe.wait_ge(exped, AHEAD + n * S + s + 1)
                for sub in range(2):
                    for i, lhs in enumerate((v[h % 2][:, kt, :], ones[:, :])):
                        r0 = (2 * sub + i) * VD
                        last = pe.matmul(p_out[r0:r0 + VD, off:CH], lhs, prob[s % PRING][:, sub, off:CH],
                                         start=first, stop=final)
                last.then_inc(summed, 1)

            def turn(copied, count, at):
                pe.wait_ge(out_copied, AHEAD + copied)
                take_bank(count, at)
                for i in range(QPC):
                    last = pe.transpose(p_ring[:, at % RING, i * P:(i + 1) * P], sums[:, i * P:(i + 1) * P],
                                        C.ident[:, :])
                last.then_inc(filled, 1)

            def head(n, h, has_next=True):
                for what, i, at in ring_items(n, has_next):
                    if what == "score":
                        score(*((n, h, i) if i < S else (n + 1, (h + 1) % 4, 0)))
                    elif what == "sum":
                        sum_up(n, h, i)
                    elif what == "turn":
                        turn(QC * n + (0 if i == QC - 1 else i + 1), ring_count(n, at), at)
                    elif what == "max":
                        max_unit(n + 1, (h + 1) % 4, i, ring_count(n, at), at)
                    else:
                        turn_shift(n + 1, ring_count(n, at), at)

            pe.wait_ge(ready, 5)
            for u in range(U):
                max_unit(0, 0, u, u, u)
            turn_shift(0, U, U)
            score(0, 0, 0)
            with pe.Fori(0, HEADS // 4 - 1, 1) as j:
                for h in range(4):
                    head(4 * j + h, h)
            for h in range(4):
                head(HEADS - 4 + h, h, has_next=h < 3)
            turn(QC * HEADS, ring_count(HEADS - 1, QC), QC)

        @block.scalar
        def _(act):
            credit(act, exped, out_copied)

            def copy_out(n, qc):
                act.wait_ge(summed, AHEAD + n * S + L.qc_last[qc] + 1)
                act.wait_ge(out_kept, AHEAD + QC * n + qc + 1)
                act.activation(sums[:, :], p_out[:, :], ACT.Copy).then_inc(out_copied, 1)

            def exp(n, i):
                qc, kt, off = L.steps[i]
                act.wait_ge(scored, n * S + i + 1)
                act.wait_ge(summed, AHEAD + n * S + i - PRING + 1)
                act.activation(prob[i % PRING][:, :, off:CH], p_score[:, i % 2, :, off:CH], ACT.Exp,
                               scale=HD ** -0.5).then_inc(exped, 1)

            def head(n, h, has_next=True):
                for what, i in L.orders[has_next]:
                    late = L.causal and i % S in [0] + [last + 1 for last in L.qc_last]
                    step = (n, i) if i < S else (n + 1, 0)
                    if what == "score" and not late:
                        exp(*step)
                    elif what == "score":
                        held = step
                    elif what == "sum" and i in L.qc_last:
                        copy_out(n, L.qc_last.index(i))
                        if L.causal and (has_next or i < S - 1):
                            exp(*held)

            exp(0, 0)
            with act.Fori(0, HEADS // 4 - 1, 1) as j:
                for h in range(4):
                    head(4 * j + h, h)
            for h in range(4):
                head(HEADS - 4 + h, h, has_next=h < 3)

        @block.vector
        def _(dve):
            credit(dve, freed, out_kept)

            def reduce(u, count, at):
                sub, qt, kc, keys = L.units[u]
                dve.wait_ge(filled, count + 1)
                dve.tensor_reduce(maxima[:, sub * KT + qt, kc:kc + 1], p_ring[:, at % RING, 0:keys], AX.X, ALU.max,
                                  negate=True).then_inc(freed, 1)

            def make_shift(n, count):
                dve.wait_ge(freed, AHEAD + count + 1)
                dve.tensor_reduce(shift[:, :], maxima[:, :, :], AX.X, ALU.min).then_inc(shift_made, 1)
                dve.wait_ge(shift_made, 2 * n + 1)
                dve.tensor_copy(shift_parts[:, 0, :], shift[:, :]).then_inc(shift_made, 1)
                dve.wait_ge(shift_made, 2 * n + 2)
                dve.tensor_tensor(shift_parts[:, 1, :], shift[:, :], shift_parts[:, 0, :],
                                  ALU.subtract).then_inc(shift_rest, 1)

            def copy_shift(n, count, at, sent=None):
                dve.wait_ge(filled, count + 1)
                if sent:
                    dve.wait_ge(*sent)
                dve.tensor_copy(shift_rows[:, :], p_ring[0:4 * KT, at % RING, 0:P // 2].bitcast(BF16)
                                ).then_inc(shift_copied, 1)
                dve.wait_ge(shift_copied, n + 1)
                dve.sem_inc(freed, 1)

            def keep(kept, n, qc, count, at):
                dve.wait_ge(filled, count + 1)
                cols = p_ring[:, at % RING, :].rearrange("p (b s w) -> p b s w", b=QPC, s=2)
                dve.wait_ge(out_kept, AHEAD + kept)
                dve.reciprocal(recip[:, :, :], cols[:, :, :, VD]).then_inc(out_recip, 1)
                dve.wait_ge(out_recip, kept + 1)
                dve.tensor_tensor(half[:, 0, :, :], cols[:, :, 0, 0:VD], recip[:, :, 0:1].to_broadcast([P, QPC, VD]),
                                  ALU.mult).then_inc(out_scaled, 1)
                dve.tensor_tensor(half[:, 1, :, :], cols[:, :, 1, 0:VD], recip[:, :, 1:2].to_broadcast([P, QPC, VD]),
                                  ALU.mult).then_inc(freed, 1)
                dve.wait_ge(out_scaled, kept + 1)
                dve.wait_ge(freed, AHEAD + count + 1)
                tiles = attn[:, :].rearrange("p (t c) -> p t c", c=D)
                to = tiles[:, ds((n // NH) * KT + qc * QPC, QPC), ds((n % NH) * VD, VD)]
                dve.scalar_tensor_tensor(
                    out=to, in0=half[:, 1, :, :], scalar=neg_lambda, in1=half[:, 0, :, :],
                    op0=ALU.mult, op1=ALU.add).then_inc(out_kept, 1)

            def head(n, h, has_next=True):
                for what, i, at in ring_items(n, has_next):
                    if what == "max":
                        reduce(i, ring_count(n, at), at)
                        if i == U - 1:
                            make_shift(n + 1, ring_count(n, at))
                    elif what == "turn_shift":
                        copy_shift(n + 1, ring_count(n, at), at, (shift_in[h % 2], 32 * (n // 2) + 32))
                    elif what == "turn" and i == QC - 1:
                        keep(QC * n, (n + (HEADS - 1)) % HEADS, i, ring_count(n, at), at)
                    elif what == "turn":
                        keep(QC * n + i + 1, n, i, ring_count(n, at), at)

            dve.memset(ones[:, :], 1.0).then_inc(ready, 1)
            for i in range(2):
                dve.memset(k[i][SROWS:FROWS, :, :], 1.0).then_inc(ready, 1)
            dve.memset(sums[:, :], 1.0).then_inc(ready, 1)
            dve.memset(maxima[:, :, :], 3e38).then_inc(ready, 1)
            dve.wait_ge(ready, 5)
            for u in range(U):
                reduce(u, u, u)
            make_shift(0, U - 1)
            copy_shift(0, U, U)
            with dve.Fori(0, HEADS // 4 - 1, 1) as j:
                for h in range(4):
                    head(4 * j + h, h)
            for h in range(4):
                head(HEADS - 4 + h, h, has_next=h < 3)
            keep(QC * HEADS, HEADS - 1, QC - 1, ring_count(HEADS - 1, QC), QC)


def tile_pipeline(engine, *stages, written_out=WRITTEN_OUT):
    def step(i, par, live=lambda t: True):
        for lag, f in stages:
            if live(i - lag):
                f(i - lag, (par - lag) % 2)

    for i in range(written_out):
        step(i, i % 2, lambda t: t >= 0)
    if written_out < NT:
        with engine.Fori(0, (NT - written_out) // 2, 1) as j:
            for par in range(2):
                step(2 * j + (written_out + par), par)
    for i in range(NT, NT + max(lag for lag, _ in stages)):
        step(i, i % 2, lambda t: t < NT)


def mix_phase(nc, name, attn, wo_area, norm_w, x, xT, C, loads, convert=None):
    with ExitStack() as ctx:
        sb = lambda n, s, d: ctx.enter_context(nc.sbuf_tensor(f"{name}_{n}", s, d))
        ps = lambda n, s, d: ctx.enter_context(nc.psum_tensor(f"{name}_{n}", s, d))
        sem = lambda n: ctx.enter_context(nc.semaphore(f"{name}_{n}"))
        wo_stage = wo_area.whole[:, :].rearrange("p (k n) -> p k n", k=KD)
        wo = Split(sb("wo_hi", [P, KD, D], F32R), wo_area.taken_by(f"{name}_wo_lo", [P, KD, D], F32R))
        square = sb("square", [P, D], F32)
        mean_sq = sb("mean_sq", [P, NH], F32)
        rms = sb("rms", [P, NH], F32)
        inv_rms = sb("inv_rms", [P, NH], F32)
        normed = [sb(f"normed{i}", [P, D], F32) for i in range(2)]
        normed_T = [Split(sb(f"normed_T{i}_hi", [P, KD, P], F32R), sb(f"normed_T{i}_lo", [P, KD, P], F32R))
                    for i in range(2)]
        stats = sb("stats", [P, 6], F32)
        mv = sb("mv", [P, 2], F32)
        idle = sb("idle", [P, 1], F32)
        std, rstd, offset = sb("std", [P, 1], F32), sb("rstd", [P, 1], F32), sb("offset", [P, 1], F32)
        p_nT = ps("p_nT", [P, 2, KD, P], F32)
        p_o = ps("p_o", [P, 2, D], F32)
        p_yT = ps("p_yT", [P, 2, KD, P], F32)
        wo_scaled, wo_hi, wo_lo, loaded = sem("wo_scaled"), sem("wo_hi"), sem("wo_lo"), sem("loaded")
        squared, summed, rooted, inverted, scaled = (sem("squared"), sem("summed"), sem("rooted"), sem("inverted"),
                                                     sem("scaled"))
        turned, turned_hi, turned_lo, projected = sem("turned"), sem("turned_hi"), sem("turned_lo"), sem("projected")
        added, stat1, stat2, std_done, rstd_done, offset_done, y_done = (
            sem("added"), sem("stat1"), sem("stat2"), sem("std_done"), sem("rstd_done"), sem("offset_done"),
            sem("y_done"))
        y_turned, y_hi, y_lo = sem("y_turned"), sem("y_hi"), sem("y_lo")
        block = ctx.enter_context(nc.Block())
        tile = lambda t: x[:, ds(t, 1), :].squeeze(1)

        @block.gpsimd
        def _(pool):
            for dst, src in loads:
                pool.dma_start(dst, src).then_inc(loaded, 16)
            pool.wait_ge(loaded, 16 * len(loads))
            if convert is not None:
                convert_weights(pool, convert)

        @block.vector
        def _(dve):
            def invert(t, par):
                dve.wait_ge(rooted, t + 1)
                wait_from_first(dve, scaled, t)
                dve.reciprocal(inv_rms[:, :], rms[:, :]).then_inc(inverted, 1)
                dve.wait_ge(inverted, t + 1)
                wait_from_first(dve, turned, t - 1)
                dve.tensor_tensor(normed[par][:, :].rearrange("p (h w) -> p h w", w=VD),
                                  attn[:, ds(t * D, D)].rearrange("p (h w) -> p h w", w=VD),
                                  inv_rms[:, :].unsqueeze(2).to_broadcast([P, NH, VD]), ALU.mult).then_inc(scaled, 1)

            def scalars(t, par):
                dve.wait_ge(std_done, t + 1)
                wait_from_first(dve, y_done, t)
                dve.reciprocal(rstd[:, :], std[:, :]).then_inc(rstd_done, 1)
                dve.wait_ge(rstd_done, t + 1)
                dve.scalar_tensor_tensor(out=offset[:, :], in0=mv[:, 0:1], scalar=-1.0, in1=rstd[:, :],
                                         op0=ALU.mult, op1=ALU.mult).then_inc(offset_done, 1)

            def rest_of_turned(t, par):
                dve.wait_ge(turned_hi, t + 1)
                wait_from_first(dve, projected, t - 1)
                dve.tensor_tensor(normed_T[par].lo[:, :, :], p_nT[:, par, :, :], normed_T[par].hi[:, :, :],
                                  ALU.subtract).then_inc(turned_lo, 1)

            def rest_of_y(t, par):
                dve.wait_ge(y_hi, t + 1)
                dve.tensor_tensor(xT.lo[:, :, ds(t * P, P)], p_yT[:, par, :, :], xT.hi[:, :, ds(t * P, P)],
                                  ALU.subtract).then_inc(y_lo, 1)

            def mean_squares(t, par):
                dve.wait_ge(squared, t + 1)
                wait_from_first(dve, rooted, t)
                dve.tensor_reduce(mean_sq[:, :], square[:, :].rearrange("p (h w) -> p h w", w=VD), AX.X,
                                  ALU.add).then_inc(summed, 1)

            def add(t, par):
                dve.wait_ge(projected, t + 1)
                dve.tensor_tensor(tile(t), p_o[:, par, :], tile(t), ALU.add).then_inc(added, 1)
                dve.wait_ge(added, t + 1)
                dve.memset(idle[:, :], 0.0)
                dve.bn_stats(stats[:, :], tile(t)).then_inc(stat1, 1)
                dve.wait_ge(stat1, t + 1)
                wait_from_first(dve, offset_done, t)
                dve.memset(idle[:, :], 0.0)
                dve.bn_aggr(mv[:, :], stats[:, :]).then_inc(stat2, 1)

            for k in range(KD):
                dve.tensor_scalar(wo_stage[:, k, :], wo_stage[:, k, :], norm_w, 1.0 - LAMBDA_INIT, ALU.mult,
                                  ALU.mult).then_inc(wo_scaled, 1)
            for k in range(KD):
                dve.wait_ge(wo_hi, k + 1)
                dve.tensor_tensor(wo.lo[:, k, :], wo_stage[:, k, :], wo.hi[:, k, :], ALU.subtract).then_inc(wo_lo, 1)
            tile_pipeline(dve, (1, invert), (4, scalars), (2, rest_of_turned), (6, rest_of_y), (0, mean_squares),
                          (3, add))

        @block.scalar
        def _(act):
            def root(t, par):
                act.wait_ge(summed, t + 1)
                wait_from_first(act, inverted, t)
                act.activation(rms[:, :], mean_sq[:, :], ACT.Sqrt, bias=C.eps[:, 0:1], scale=1.0 / VD
                               ).then_inc(rooted, 1)

            def deviation(t, par):
                act.wait_ge(stat2, t + 1)
                wait_from_first(act, rstd_done, t)
                act.activation(std[:, :], mv[:, 1:2], ACT.Sqrt, bias=C.eps[:, 0:1]).then_inc(std_done, 1)

            def turned_value(t, par):
                act.wait_ge(turned, t + 1)
                wait_from_first(act, projected, t - 1)
                act.activation(normed_T[par].hi[:, :, :], p_nT[:, par, :, :], ACT.Copy).then_inc(turned_hi, 1)

            def squares(t, par):
                wait_from_first(act, summed, t)
                act.activation(square[:, :], attn[:, ds(t * D, D)], ACT.Square).then_inc(squared, 1)

            def normalise(t, par):
                act.wait_ge(offset_done, t + 1)
                act.activation(tile(t), tile(t), ACT.Identity, bias=offset[:, 0:1], scale=rstd[:, 0:1]
                               ).then_inc(y_done, 1)

            def y_value(t, par):
                act.wait_ge(y_turned, t + 1)
                act.activation(xT.hi[:, :, ds(t * P, P)], p_yT[:, par, :, :], ACT.Copy).then_inc(y_hi, 1)

            for k in range(KD):
                act.wait_ge(wo_scaled, k + 1)
                act.activation(wo.hi[:, k, :], wo_stage[:, k, :], ACT.Copy).then_inc(wo_hi, 1)
            tile_pipeline(act, (1, root), (4, deviation), (2, turned_value), (6, y_value), (0, squares),
                          (4, normalise))

        @block.tensor
        def _(pe):
            def turn(t, par):
                pe.wait_ge(scaled, t + 1)
                wait_from_first(pe, turned_lo, t - 1)
                for i in range(KD):
                    last = pe.transpose(p_nT[:, par, i, :], normed[par][:, i * P:(i + 1) * P], C.ident[:, :])
                last.then_inc(turned, 1)

            def project(t, par):
                pe.wait_ge(turned_lo, t + 1)
                wait_from_first(pe, added, t - 1)
                product(pe, p_o[:, par, :], [(normed_T[par][:, i, :], wo[:, i, :]) for i in range(KD)]
                        ).then_inc(projected, 1)

            def turn_y(t, par):
                pe.wait_ge(y_done, t + 1)
                wait_from_first(pe, y_lo, t - 1)
                for i in range(KD):
                    last = pe.transpose(p_yT[:, par, i, :], x[:, t, i * P:(i + 1) * P], C.ident[:, :])
                last.then_inc(y_turned, 1)

            pe.wait_ge(wo_lo, KD)
            tile_pipeline(pe, (3, project), (5, turn_y), (1, turn), written_out=NT)


def convert_weights(pool, area, done=None):
    for i in range(3):
        piece = area.whole[:, i * GW:(i + 1) * GW]
        converted = pool.tensor_scalar(piece, piece.bitcast(I32), 1.0, -ZERO_POINT, ALU.mult, ALU.add)
        if done is not None:
            converted.then_inc(done, 1)


def ffn_group_loads(stage, weights, g):
    gate, up, down = weights
    cut = lambda i, **sizes: stage[:, i * GW:(i + 1) * GW].rearrange("p (k n) -> p k n", **sizes)
    return [(cut(0, k=KD), gate[:, :, ds(g * (GT * P), GT * P)]), (cut(1, k=KD), up[:, :, ds(g * (GT * P), GT * P)]),
            (cut(2, k=GT), down[:, ds(g * GT, GT), :])]


def ffn_phase(nc, weights, areas, d_scale, room, scales, x, xT, C, loads):
    name = "ffn"
    with ExitStack() as ctx:
        sb = lambda n, s, d: ctx.enter_context(nc.sbuf_tensor(f"{name}_{n}", s, d))
        ps = lambda n, s, d: ctx.enter_context(nc.psum_tensor(f"{name}_{n}", s, d))
        sem = lambda n: ctx.enter_context(nc.semaphore(f"{name}_{n}"))
        w = [Split(sb(f"w{i}_hi", [P, 3 * GW], F32R), area.taken_by("lo", [P, 3 * GW], F32R))
             for i, area in enumerate(areas)]
        stage = [area.whole[:, :].bitcast(I32) for area in areas]
        real = [area.whole[:, :] for area in areas]
        cut = lambda i, part, **sizes: Split(*(a[:, part * GW:(part + 1) * GW].rearrange("p (k n) -> p k n", **sizes)
                                               for a in (w[i].hi, w[i].lo)))
        wg, wu, wd = ([cut(i, part, k=k) for i in range(2)] for part, k in ((0, KD), (1, KD), (2, GT)))
        h_shape = [P, GROUP_BUFFERS, GT, CH]
        h = Split(room.taken_by("h_hi", h_shape, F32R), room.taken_by("h_lo", h_shape, F32R, H_SIZE))
        h_full = [sb(f"h{i}", [P, CH], F32) for i in range(2)]
        silu = [sb(f"silu{i}", [P, CH], F32) for i in range(2)]
        stats = sb("stats", [P, QPC, 6], F32)
        mv = sb("mv", [P, QPC, 2], F32)
        std, rstd, offset = sb("std", [P, QPC], F32), sb("rstd", [P, QPC], F32), sb("offset", [P, QPC], F32)
        group_scales = [sb(f"group_scales{i}", [P, 2, GT], F32) for i in range(2)]
        p_g = ps("p_g", [P, 2, CH], F32)
        p_u = ps("p_u", [P, 2, CH], F32)
        p_d = ps("p_d", [P, QPC, D], F32)
        p_yT = p_d[:, 2:4, :].rearrange("p b (k n) -> p b k n", k=KD)
        loaded, w_in, w_real, w_scaled = sem("loaded"), sem("w_in"), sem("w_real"), sem("w_scaled")
        w_hi, w_lo, scales_ready = sem("w_hi"), sem("w_lo"), sem("scales_ready")
        g_done, u_done, silu_done = sem("g_done"), sem("u_done"), sem("silu_done")
        h_done, h_hi, h_lo = sem("h_done"), sem("h_hi"), sem("h_lo")
        d_done, added, stat1, stat2 = sem("d_done"), sem("added"), sem("stat1"), sem("stat2")
        std_done, rstd_done, offset_done, y_done = sem("std_done"), sem("rstd_done"), sem("offset_done"), sem("y_done")
        y_turned, y_hi, y_lo = sem("y_turned"), sem("y_hi"), sem("y_lo")
        block = ctx.enter_context(nc.Block())
        PREPARED = [[], [0], [1, 2], []]

        def over_groups(engine, group):
            group(0, 0)
            with engine.Fori(0, (GROUPS - 2) // 2, 1) as j:
                for i in range(2):
                    group(2 * j + 1 + i, 1 - i)
            group(GROUPS - 1, 1)

        @block.sync
        def _(sp):
            def load(g, par):
                wait_from_first(sp, d_done, (g - 1) * (NCH * QPC))
                for dst, src in ffn_group_loads(stage[par], weights, g):
                    sp.dma_start(dst, src).then_inc(w_in, 16)

            for dst, src in loads:
                sp.dma_start(dst, src).then_inc(loaded, 16)
            load(1, 1)
            with sp.Fori(0, GROUPS // 2 - 1, 1) as j:
                for par in range(2):
                    load(2 * j + 2 + par, par)
            sp.wait_ge(loaded, 16 * len(loads))
            sp.wait_ge(w_in, 16 * 3 * (GROUPS - 1))

        @block.gpsimd
        def _(pool):
            for g in range(1, GROUPS):
                pool.wait_ge(w_in, 16 * 3 * g)
                convert_weights(pool, areas[g % 2], w_real)

        @block.tensor
        def _(pe):
            def gate_up(n, c, par):
                for i in range(GT):
                    m = n * GT + i
                    at = slice(c * CH, (c + 1) * CH)
                    wait_from_first(pe, silu_done, m - 1)
                    product(pe, p_g[:, i % 2, :], [(wg[par][:, k, i * P:(i + 1) * P], xT[:, k, at]) for k in range(KD)]
                            ).then_inc(g_done, 1)
                    wait_from_first(pe, h_done, m - 1)
                    product(pe, p_u[:, i % 2, :], [(wu[par][:, k, i * P:(i + 1) * P], xT[:, k, at]) for k in range(KD)]
                            ).then_inc(u_done, 1)

            def down(n, c, par, banks):
                pe.wait_ge(h_lo, GT * n + GT)
                for t in range(QPC):
                    wait_from_first(pe, added, n * QPC + t + 1 - banks)
                    product(pe, p_d[:, t % banks, :],
                            [(h[:, c % 2, i, t * P:(t + 1) * P], wd[par][:, i, :]) for i in range(GT)]
                            ).then_inc(d_done, 1)

            def turn(c):
                for t in range(QPC):
                    u = c * QPC + t
                    pe.wait_ge(y_done, u + 1)
                    wait_from_first(pe, y_lo, u - 1)
                    for i in range(KD):
                        last = pe.transpose(p_yT[:, t % 2, i, :], x[:, u, i * P:(i + 1) * P], C.ident[:, :])
                    last.then_inc(y_turned, 1)

            def group(g, par):
                pe.wait_ge(w_lo, 3 * g + 3)
                for c in range(NCH):
                    n = g * NCH + c
                    gate_up(n, c, par)
                    if not (isinstance(g, int) and n == 0):
                        banks = 2 if isinstance(g, int) and g and c else QPC
                        down(n - 1, (c - 1) % NCH, par if c else 1 - par, banks)
                    if isinstance(g, int) and g and c >= 2:
                        turn(c - 2)

            over_groups(pe, group)
            down(GROUPS * NCH - 1, NCH - 1, 1, 2)
            turn(NCH - 2)
            turn(NCH - 1)

        @block.scalar
        def _(act):
            def gate_up(g, c, par):
                n = g * NCH + c
                for i in range(GT):
                    m = n * GT + i
                    act.wait_ge(g_done, m + 1)
                    if c == 0 and i == 0:
                        act.wait_ge(scales_ready, g + 1)
                    wait_from_first(act, h_done, m - 1)
                    act.activation(silu[i % 2][:, :], p_g[:, i % 2, :], ACT.Silu, scale=group_scales[par][:, 0, i:i + 1]
                                   ).then_inc(silu_done, 1)
                    act.wait_ge(h_done, m + 1)
                    wait_from_first(act, d_done, (n - 1) * QPC)
                    act.activation(h.hi[:, c % 2, i, :], h_full[i % 2][:, :], ACT.Copy).then_inc(h_hi, 1)

            def prepare(g, par, i):
                if not isinstance(g, int) or g:
                    act.wait_ge(w_real, 3 * g + i - 2)
                if i == 2:
                    act.wait_ge(w_scaled, GT * g + GT)
                piece = slice(i * GW, (i + 1) * GW)
                act.activation(w[par].hi[:, piece], real[par][:, piece], ACT.Copy).then_inc(w_hi, 1)

            def deviation(c):
                act.wait_ge(stat2, (c + 1) * QPC)
                wait_from_first(act, rstd_done, c)
                act.activation(std[:, :], mv[:, :, 1], ACT.Sqrt, bias=C.eps[:, 0:1]).then_inc(std_done, 1)
                act.wait_ge(offset_done, c + 1)
                for t in range(QPC):
                    tile = x[:, c * QPC + t, :]
                    act.activation(tile, tile, ACT.Identity, bias=offset[:, t:t + 1], scale=rstd[:, t:t + 1]
                                   ).then_inc(y_done, 1)

            def y_value(c):
                for t in range(QPC):
                    u = c * QPC + t
                    act.wait_ge(y_turned, u + 1)
                    act.activation(xT.hi[:, :, u * P:(u + 1) * P], p_yT[:, t % 2, :, :], ACT.Copy).then_inc(y_hi, 1)

            def group(g, par):
                for c in range(NCH):
                    gate_up(g, c, par)
                    if isinstance(g, int) and g:
                        if c >= 1:
                            deviation(c - 1)
                        if c >= 2:
                            y_value(c - 2)
                    else:
                        for i in PREPARED[c]:
                            wait_from_first(act, d_done, g * NCH * QPC)
                            prepare(g + 1, 1 - par, i)

            for i in range(3):
                prepare(0, 0, i)
            over_groups(act, group)
            deviation(NCH - 1)
            y_value(NCH - 2)
            y_value(NCH - 1)

        @block.vector
        def _(dve):
            def gate_up(g, c, par):
                n = g * NCH + c
                for i in range(GT):
                    m = n * GT + i
                    dve.wait_ge(u_done, m + 1)
                    dve.wait_ge(silu_done, m + 1)
                    wait_from_first(dve, h_lo, m - 1)
                    if c == 0 and i == 0:
                        dve.wait_ge(scales_ready, g + 1)
                    dve.scalar_tensor_tensor(out=h_full[i % 2][:, :], in0=p_u[:, i % 2, :],
                                             scalar=group_scales[par][:, 1, i:i + 1], in1=silu[i % 2][:, :],
                                             op0=ALU.mult,
                                             op1=ALU.mult).then_inc(h_done, 1)
                    dve.wait_ge(h_hi, m + 1)
                    dve.tensor_tensor(h.lo[:, c % 2, i, :], h_full[i % 2][:, :], h.hi[:, c % 2, i, :], ALU.subtract
                                      ).then_inc(h_lo, 1)

            def add(n, c, final=False):
                banks = 2 if final else QPC
                for t in range(QPC):
                    tile = x[:, c * QPC + t, :]
                    dve.wait_ge(d_done, n * QPC + t + 1)
                    wait_from_first(dve, added, n * QPC + t - 1)
                    dve.tensor_tensor(tile, p_d[:, t % banks, :], tile, ALU.add).then_inc(added, 1)
                    if final:
                        u = c * QPC + t
                        dve.wait_ge(added, n * QPC + t + 1)
                        if c:
                            dve.wait_ge(offset_done, c)
                        dve.bn_stats(stats[:, t, :], tile).then_inc(stat1, 1)
                        dve.wait_ge(stat1, u + 1)
                        dve.bn_aggr(mv[:, t, :], stats[:, t, :]).then_inc(stat2, 1)
                if final:
                    dve.wait_ge(std_done, c + 1)
                    wait_from_first(dve, y_done, c * QPC)
                    dve.reciprocal(rstd[:, :], std[:, :]).then_inc(rstd_done, 1)
                    dve.wait_ge(rstd_done, c + 1)
                    dve.scalar_tensor_tensor(out=offset[:, :], in0=mv[:, :, 0], scalar=-1.0, in1=rstd[:, :],
                                             op0=ALU.mult, op1=ALU.mult).then_inc(offset_done, 1)

            def rest_of_y(c):
                for t in range(QPC):
                    u = c * QPC + t
                    at = slice(u * P, (u + 1) * P)
                    dve.wait_ge(y_hi, u + 1)
                    dve.tensor_tensor(xT.lo[:, :, at], p_yT[:, t % 2, :, :], xT.hi[:, :, at], ALU.subtract
                                      ).then_inc(y_lo, 1)

            def prepare(g, par, i):
                if i == 0:
                    wait_from_first(dve, silu_done, (g - 1) * (NCH * GT))
                    wait_from_first(dve, h_done, (g - 1) * (NCH * GT))
                    dve.tensor_copy(group_scales[par][:, :, :], scales[:, :, ds(g * GT, GT)]).then_inc(scales_ready, 1)
                if i == 2:
                    wait_from_first(dve, w_real, 3 * g)
                    for k in range(GT):
                        cols = slice(2 * GW + k * D, 2 * GW + (k + 1) * D)
                        dve.tensor_tensor(real[par][:, cols], real[par][:, cols], d_scale[:, :], ALU.mult
                                          ).then_inc(w_scaled, 1)
                piece = slice(i * GW, (i + 1) * GW)
                dve.wait_ge(w_hi, 3 * g + i + 1)
                dve.tensor_tensor(w[par].lo[:, piece], real[par][:, piece], w[par].hi[:, piece], ALU.subtract
                                  ).then_inc(w_lo, 1)

            def group(g, par):
                last = isinstance(g, int) and g > 0
                for c in range(NCH):
                    n = g * NCH + c
                    gate_up(g, c, par)
                    if not (isinstance(g, int) and n == 0):
                        add(n - 1, (c - 1) % NCH, last and c > 0)
                    if last and c >= 2:
                        rest_of_y(c - 2)
                    if not last:
                        for i in PREPARED[c]:
                            prepare(g + 1, 1 - par, i)

            for i in range(3):
                prepare(0, 0, i)
            over_groups(dve, group)
            add(GROUPS * NCH - 1, NCH - 1, True)
            rest_of_y(NCH - 2)
            rest_of_y(NCH - 1)



def linear_phase(nc, w_area, scale, bias, x, xT, out_d, C):
    name = "lin"
    BANKS = 4
    with ExitStack() as ctx:
        sb = lambda n, s, d: ctx.enter_context(nc.sbuf_tensor(f"{name}_{n}", s, d))
        ps = lambda n, s, d: ctx.enter_context(nc.psum_tensor(f"{name}_{n}", s, d))
        sem = lambda n: ctx.enter_context(nc.semaphore(f"{name}_{n}"))
        w_stage = w_area.whole[:, :].rearrange("p (k n) -> p k n", k=KD)
        w = Split(sb("w_hi", [P, KD, D], F32R), w_area.taken_by("lin_w_lo", [P, KD, D], F32R))
        stats = sb("stats", [P, 6], F32)
        mv = sb("mv", [P, 2], F32)
        idle = sb("idle", [P, 1], F32)
        std, rstd, offset = sb("std", [P, 1], F32), sb("rstd", [P, 1], F32), sb("offset", [P, 1], F32)
        p_o = ps("p_o", [P, 2, D], F32)
        w_scaled, w_hi, w_lo = sem("w_scaled"), sem("w_hi"), sem("w_lo")
        o_done, biased, added, stat1, stat2, std_done, rstd_done, offset_done, y_done = (
            sem("o_done"), sem("biased"), sem("added"), sem("stat1"), sem("stat2"), sem("std_done"),
            sem("rstd_done"), sem("offset_done"), sem("y_done"))
        stored = sem("stored")
        block = ctx.enter_context(nc.Block())
        tile = lambda t: x[:, ds(t, 1), :].squeeze(1)

        @block.sync
        def _(sp):
            for t in range(NT):
                sp.wait_ge(y_done, t + 1)
                sp.dma_start(out_d[t * P:(t + 1) * P, :], x[:, t, :]).then_inc(stored, 16)
            sp.wait_ge(stored, 16 * NT)

        @block.gpsimd
        def _(pool):
            with pool.Fori(0, NT, 1) as t:
                pool.tensor_tensor(tile(t), tile(t), bias, ALU.add).then_inc(biased, 1)

        @block.tensor
        def _(pe):
            def project(t, par):
                wait_from_first(pe, added, t - 1)
                product(pe, p_o[:, par, :], [(xT[:, i, t * P:(t + 1) * P], w[:, i, :]) for i in range(KD)]
                        ).then_inc(o_done, 1)

            pe.wait_ge(w_lo, KD)
            tile_pipeline(pe, (0, project), written_out=NT)

        @block.scalar
        def _(act):
            def deviation(t, par):
                act.wait_ge(stat2, t + 1)
                wait_from_first(act, rstd_done, t)
                act.activation(std[:, :], mv[:, 1:2], ACT.Sqrt, bias=C.eps[:, 0:1]).then_inc(std_done, 1)

            def normalise(t, par):
                act.wait_ge(offset_done, t + 1)
                act.activation(tile(t), tile(t), ACT.Identity, bias=offset[:, 0:1], scale=rstd[:, 0:1]
                               ).then_inc(y_done, 1)

            for k in range(KD):
                act.wait_ge(w_scaled, k + 1)
                act.activation(w.hi[:, k, :], w_stage[:, k, :], ACT.Copy).then_inc(w_hi, 1)
            tile_pipeline(act, (1, deviation), (1, normalise))

        @block.vector
        def _(dve):
            def add(t, par):
                dve.wait_ge(o_done, t + 1)
                dve.wait_ge(biased, t + 1)
                dve.tensor_tensor(tile(t), p_o[:, par, :], tile(t), ALU.add).then_inc(added, 1)
                dve.wait_ge(added, t + 1)
                dve.memset(idle[:, :], 0.0)
                dve.bn_stats(stats[:, :], tile(t)).then_inc(stat1, 1)
                dve.wait_ge(stat1, t + 1)
                wait_from_first(dve, offset_done, t)
                dve.memset(idle[:, :], 0.0)
                dve.bn_aggr(mv[:, :], stats[:, :]).then_inc(stat2, 1)

            def scalars(t, par):
                dve.wait_ge(std_done, t + 1)
                wait_from_first(dve, y_done, t)
                dve.reciprocal(rstd[:, :], std[:, :]).then_inc(rstd_done, 1)
                dve.wait_ge(rstd_done, t + 1)
                dve.scalar_tensor_tensor(out=offset[:, :], in0=mv[:, 0:1], scalar=-1.0, in1=rstd[:, :],
                                         op0=ALU.mult, op1=ALU.mult).then_inc(offset_done, 1)

            for k in range(KD):
                dve.tensor_tensor(w_stage[:, k, :], w_stage[:, k, :], scale, ALU.mult).then_inc(w_scaled, 1)
            for k in range(KD):
                dve.wait_ge(w_hi, k + 1)
                dve.tensor_tensor(w.lo[:, k, :], w_stage[:, k, :], w.hi[:, k, :], ALU.subtract).then_inc(w_lo, 1)
            tile_pipeline(dve, (1, scalars), (0, add))


class Constants:
    pass


def setup_phase(nc, C, lambdas, neg_lambda, norm_ws, norm_w, loads):
    with ExitStack() as ctx:
        sb = lambda n, s, d: ctx.enter_context(nc.sbuf_tensor(f"set_{n}", s, d))
        sem = lambda n: ctx.enter_context(nc.semaphore(f"set_{n}"))
        vec = sb("vec", [P, 2, 2, 2, HD], F32)
        prod = sb("prod", [P, 2, 2, HD], F32)
        dots = sb("dots", [P, 2, 2], F32)
        lam = sb("lam", [P, 2, 2], F32)
        v_in, rest_in = sem("v_in"), sem("rest_in")
        blank, products, exps = sem("blank"), sem("products"), sem("exps")
        block = ctx.enter_context(nc.Block())

        @block.sync
        def _(sp):
            for dst, src in loads:
                sp.dma_start(dst, src).then_inc(rest_in, 16)
            for l in range(2):
                for e in range(2):
                    for f in range(2):
                        sp.dma_start(vec[:, l, e, f, :], lambdas[l][2 * e + f].partition_broadcast(P)
                                     ).then_inc(v_in, 16)
                for i in range(P // VD):
                    sp.dma_start(norm_w[i * VD:(i + 1) * VD, l:l + 1], norm_ws[l].unsqueeze(1)).then_inc(rest_in, 16)
            sp.wait_ge(rest_in, 16 * (len(loads) + 2 * (P // VD)))

        @block.gpsimd
        def _(pool):
            for t in (C.ident, C.ident_b, C.mask_qk, C.mask_kq):
                pool.memset(t[:, :], 0.0).then_inc(blank, 1)
            pool.memset(C.eps[:, :], EPS).then_inc(blank, 1)
            pool.wait_ge(blank, 5)
            for t in (C.ident, C.ident_b):
                pool.affine_select(out=t[:, :], in_=t[:, :], compare_op=ALU.not_equal, fill=1.0, base=0,
                                   pattern=[[-1, P]], channel_multiplier=1)
            pool.affine_select(out=C.mask_qk[:, :], in_=C.mask_qk[:, :], compare_op=ALU.is_ge, fill=MASKED, base=0,
                               pattern=[[-1, P]], channel_multiplier=1)
            pool.affine_select(out=C.mask_kq[:, :], in_=C.mask_kq[:, :], compare_op=ALU.is_ge, fill=MASKED, base=0,
                               pattern=[[1, P]], channel_multiplier=-1)

        @block.vector
        def _(dve):
            dve.wait_ge(v_in, 16 * 8)
            dve.tensor_tensor(prod[:, :, :, :], vec[:, :, :, 0, :], vec[:, :, :, 1, :], ALU.mult).then_inc(products, 1)
            dve.wait_ge(products, 1)
            dve.tensor_reduce(dots[:, :, :], prod[:, :, :, :], AX.X, ALU.add).then_inc(products, 1)
            dve.wait_ge(exps, 1)
            for l in range(2):
                dve.scalar_tensor_tensor(out=neg_lambda[l][:, :], in0=lam[:, l, 1:2], scalar=-LAMBDA_INIT,
                                         in1=lam[:, l, 0:1], op0=ALU.add, op1=ALU.subtract)

        @block.scalar
        def _(act):
            act.wait_ge(products, 2)
            act.activation(lam[:, :, :], dots[:, :, :], ACT.Exp).then_inc(exps, 1)


def program(nc, A, out):
    dram = lambda n, s, d: nc.dram_tensor(n, s, d, kind="Internal").ap()
    q_parts = [dram(f"q_parts{l}", (B * D // HD, PARTS * HD, T), BF16) for l in range(2)]
    k_parts = [dram(f"k_parts{l}", (B * L.k_dims // HD, PARTS * HD, T), BF16) for l, L in enumerate((L0, L1))]
    x0 = A["L0_attn_x"].rearrange("b t d -> (b t) d")
    out = out.rearrange("b t d -> (b t) d")
    with ExitStack() as ctx:
        sb = lambda n, s, d: ctx.enter_context(nc.sbuf_tensor(n, s, d))
        C = Constants()
        C.ident = sb("ident", [P, P], F32)
        C.ident_b = sb("ident_b", [P, P], BF16)
        C.mask_qk = sb("mask_qk", [P, P], BF16)
        C.mask_kq = sb("mask_kq", [P, P], BF16)
        C.eps = sb("eps", [P, 1], F32)
        neg_lambda = [sb(f"neg_lambda{l}", [P, 1], F32) for l in range(2)]
        norm_w = sb("norm_w", [P, 2], F32)
        scales = sb("scales", [P, 2, FT], F32)
        x = sb("x", [P, NT * D], F32)
        x_tiles = x[:, :].rearrange("p (t c) -> p t c", c=D)
        xT_rooms = [Area(ctx, nc, f"xT{i}", KD * TOK) for i in range(2)]
        xT = Split(*(room.taken_by("all", [P, KD, TOK], F32R) for room in xT_rooms))
        attn_area = Area(ctx, nc, "attn", NT * D)
        attn = attn_area.whole
        wo_area = Area(ctx, nc, "wo", KD * D)
        wo_stage = wo_area.whole[:, :].rearrange("p (k n) -> p k n", k=KD)
        by_k = lambda a: a.rearrange("(k p) n -> p k n", p=P)
        qkv0_w = [A[f"L0_attn_{w}_T"] for w in ("wq", "wk", "wv")]
        x_stage = x[:, :].rearrange("p (k n) -> p k n", k=KD)
        setup_phase(
            nc, C, [[A[f"L{l}_attn_lambda_{x}"] for x in ("q1", "k1", "q2", "k2")] for l in range(2)], neg_lambda,
            [A["L0_attn_subln_w"], A["L1_attn_ln_w"]], norm_w,
            [(attn[:, 0:KD * D].rearrange("p (k n) -> p k n", k=KD), by_k(qkv0_w[0])),
             (x_stage[:, :, 0:CH], by_k(A["x_T"])[:, :, 0:CH]),
             (scales[:, 0, :], A["L0_ffn_gate_scale_T"]), (scales[:, 1, :], A["L0_ffn_up_scale_T"])])
        with ExitStack() as layer:
            v_sb = layer.enter_context(nc.sbuf_tensor("v_all0", [P, NT * L0.v_dims], F32))
            qkv_phase(nc, L0, xT, q_parts[0], k_parts[0], v_sb, attn_area, 0,
                      qkv0_w, x_stage, A["x_T"])
            attention_phase(nc, L0, q_parts[0], k_parts[0], v_sb, attn, neg_lambda[0][:, 0:1], C, xT_rooms,
                            [(x_tiles, x0.rearrange("(t p) d -> p t d", p=P)), (wo_stage, by_k(A["L0_attn_wo_T"]))])
        with ExitStack() as layer:
            ffn_areas = [Area(layer, nc, f"ffn_w{i}", 3 * GW) for i in range(2)]
            d_scale = layer.enter_context(nc.sbuf_tensor("d_scale", [P, D], F32))
            w_gud = [by_k(A[f"L0_ffn_{w}_w_T"]) for w in ("gate", "up", "down")]
            loads = [(d_scale[:, :], A["L0_ffn_down_scale"].partition_broadcast(P))]
            mix_phase(nc, "mix0", attn, wo_area, norm_w[:, 0:1], x_tiles, xT, C,
                      loads + ffn_group_loads(ffn_areas[0].whole[:, :].bitcast(I32), w_gud, 0), ffn_areas[0])
            qkv1_loads, w_at = [], 2 * H_SIZE
            for w in ("Wq", "Wk", "Wv"):
                src = by_k(A[f"L1_attn_{w}_T"])
                width = KD * src.shape[2]
                qkv1_loads.append((attn[:, w_at:w_at + width].rearrange("p (k n) -> p k n", k=KD), src))
                w_at += width
            ffn_phase(nc, w_gud, ffn_areas, d_scale, attn_area, scales, x_tiles, xT, C, qkv1_loads)
        with ExitStack() as layer:
            v_sb = layer.enter_context(nc.sbuf_tensor("v_all1", [P, NT * L1.v_dims], F32))
            qkv_phase(nc, L1, xT, q_parts[1], k_parts[1], v_sb, attn_area, 2 * H_SIZE)
            attention_phase(nc, L1, q_parts[1], k_parts[1], v_sb, attn, neg_lambda[1][:, 0:1], C, xT_rooms,
                            [(wo_stage, by_k(A["L1_attn_Wo_T"]))])
            lin_area = Area(layer, nc, "lin_w", KD * D)
            lin_rows = layer.enter_context(nc.sbuf_tensor("lin_rows", [P, 2, D], F32))
            mix_phase(nc, "mix1", attn, wo_area, norm_w[:, 1:2], x_tiles, xT, C,
                      [(lin_area.whole[:, :].rearrange("p (k n) -> p k n", k=KD), by_k(A["L1_ffn_weight_T"])),
                       (lin_rows[:, 0, :], A["L1_ffn_scale_weight"].partition_broadcast(P)),
                       (lin_rows[:, 1, :], A["L1_ffn_bias"].partition_broadcast(P))])
            linear_phase(nc, lin_area, lin_rows[:, 0, :], lin_rows[:, 1, :], x_tiles, xT, out, C)


TRANSPOSED = ["L0_attn_wq", "L0_attn_wk", "L0_attn_wv", "L0_attn_wo", "L0_ffn_gate_w", "L0_ffn_up_w",
              "L0_ffn_down_w", "L1_attn_Wq", "L1_attn_Wk", "L1_attn_Wv", "L1_attn_Wo", "L1_ffn_weight"]
PLAIN = ["L0_attn_x", "L0_attn_lambda_q1", "L0_attn_lambda_k1", "L0_attn_lambda_q2", "L0_attn_lambda_k2",
         "L0_attn_subln_w", "L0_ffn_down_scale", "L1_attn_lambda_q1",
         "L1_attn_lambda_k1", "L1_attn_lambda_q2", "L1_attn_lambda_k2", "L1_attn_ln_w", "L1_ffn_scale_weight",
         "L1_ffn_bias"]


def kernel(**inputs):
    import numpy as np
    import concourse.bacc as bacc
    from concourse.bass_utils import run_bass_kernel_spmd

    arrays = {name: np.ascontiguousarray(inputs[name]) for name in PLAIN}
    for name in TRANSPOSED:
        arrays[name + "_T"] = np.ascontiguousarray(np.asarray(inputs[name]).T)
    for name in ("L0_ffn_gate_scale", "L0_ffn_up_scale"):
        arrays[name + "_T"] = np.ascontiguousarray(np.asarray(inputs[name]).reshape(FT, P).T)
    x = np.asarray(inputs["L0_attn_x"])
    arrays["x_T"] = np.ascontiguousarray(x.reshape(-1, x.shape[-1]).T)
    nc = bacc.Bacc("TRN2", target_bir_lowering=False, num_devices=1)
    A = {name: nc.dram_tensor(f"in_{name}", a.shape, mybir.dt.from_np(a.dtype), kind="ExternalInput").ap()
         for name, a in arrays.items()}
    out = nc.dram_tensor("out", (B, T, D), F32, kind="ExternalOutput").ap()
    program(nc, A, out)
    r = run_bass_kernel_spmd(nc, [{f"in_{name}": a for name, a in arrays.items()}], core_ids=[0])
    return r.results[0]["out"]
```
